# Optimizing a Trainium2 kernel written in Bass

```python
import numpy as np
import jax
import jax.numpy as jnp

def _softmax(x, axis=-1):
    return jax.nn.softmax(x, axis=axis)

def _gelu(x):
    return jax.nn.gelu(x, approximate=True)

def _silu(x):
    return jax.nn.silu(x)

def _sigmoid(x):
    return jax.nn.sigmoid(x)

def _layernorm(x, axis=-1, eps=1e-05):
    m = jnp.mean(x, axis=axis, keepdims=True)
    v = jnp.var(x, axis=axis, keepdims=True)
    return (x - m) / jnp.sqrt(v + eps)

def _scatter_add(tgt, idx, src, axis=0):
    return tgt.at[idx].add(src)

def _segment_sum(src, seg, n):
    return jax.ops.segment_sum(src, seg, n)
kernel_name = 'mk_seq_preln_d2_jaxref_r8_e9e58f'

def setup_inputs(seed: int=0):
    np.random.seed(seed)
    _w = jnp.asarray

    def _L0_attn_setup():
        import jax, jax.numpy as jnp
        import numpy as np
        B, T, D, S = (8, 512, 128, 128)
        EPS = 1e-05

        def _gla(x, Wq, bq, Wk, bk, Wv, bv, Wg, bg, Wo, bo, gamma, beta):
            q = x @ Wq + bq
            k = x @ Wk + bk
            v = x @ Wv + bv
            g = jax.nn.sigmoid(x @ Wg + bg)

            def step(state, qkvg):
                qt, kt, vt, gt = qkvg
                state = gt[:, :, None] * state + kt[:, :, None] * vt[:, None, :]
                out = jnp.einsum('bs,bst->bt', qt, state)
                return (state, out)
            init = jnp.zeros((x.shape[0], Wq.shape[1], Wq.shape[1]), x.dtype)
            seq = (q.transpose(1, 0, 2), k.transpose(1, 0, 2), v.transpose(1, 0, 2), g.transpose(1, 0, 2))
            _, outs = jax.lax.scan(step, init, seq)
            out = outs.transpose(1, 0, 2)
            y = x + out @ Wo + bo
            mu = jnp.mean(y, axis=-1, keepdims=True)
            var = jnp.mean(jnp.square(y - mu), axis=-1, keepdims=True)
            return (y - mu) * jax.lax.rsqrt(var + EPS) * gamma + beta
        key = jax.random.key(seed)
        ks = jax.random.split(key, 12)
        sD = 1.0 / np.sqrt(D)
        sS = 1.0 / np.sqrt(S)
        return {'x': jax.random.normal(ks[0], (B, T, D), jnp.float32), 'Wq': jax.random.normal(ks[1], (D, S), jnp.float32) * sD, 'bq': jnp.zeros((S,), jnp.float32), 'Wk': jax.random.normal(ks[2], (D, S), jnp.float32) * sD, 'bk': jnp.zeros((S,), jnp.float32), 'Wv': jax.random.normal(ks[3], (D, S), jnp.float32) * sD, 'bv': jnp.zeros((S,), jnp.float32), 'Wg': jax.random.normal(ks[4], (D, S), jnp.float32) * sD, 'bg': jnp.zeros((S,), jnp.float32), 'Wo': jax.random.normal(ks[5], (S, D), jnp.float32) * sS, 'bo': jnp.zeros((D,), jnp.float32), 'gamma': jnp.ones((D,), jnp.float32), 'beta': jnp.zeros((D,), jnp.float32)}
    _L0_attn_in = _L0_attn_setup()

    def _L0_ffn_setup():
        import jax, jax.numpy as jnp
        import numpy as np
        D = 128
        H = 512
        E = 64
        K = 3
        B, S = (2, 256)
        C = 64
        key = jax.random.key(seed)
        ks = jax.random.split(key, 6)
        s = 0.02
        return {'x': jax.random.normal(ks[0], (B, S, D), jnp.float32), 'gate_w': jax.random.normal(ks[1], (D, E), jnp.float32) * s, 'gate_b': jnp.zeros((E,), jnp.float32), 'w1': jax.random.normal(ks[2], (E, D, H), jnp.float32) * s, 'b1': jnp.zeros((E, H), jnp.float32), 'w2': jax.random.normal(ks[3], (E, H, D), jnp.float32) * s, 'b2': jnp.zeros((E, D), jnp.float32)}
    _L0_ffn_in = _L0_ffn_setup()

    def _L1_attn_setup():
        import jax, jax.numpy as jnp
        import numpy as np
        import math
        D_MODEL, D_C, D_R, NH = (128, 128, 32, 16)
        HD = D_MODEL // NH
        B, T = (2, 256)

        def _rope_tables(T, d_R):
            inv_freq = 1.0 / 10000.0 ** (jnp.arange(0, d_R, 2, dtype=jnp.float32) / d_R)
            t = jnp.arange(T, dtype=jnp.float32)
            freqs = jnp.outer(t, inv_freq)
            return (jnp.cos(freqs), jnp.sin(freqs))

        def _rotary_apply(x, cos, sin):
            d = x.shape[-1]
            x1, x2 = (x[..., :d // 2], x[..., d // 2:])
            return jnp.concatenate([x1 * cos - x2 * sin, x2 * cos + x1 * sin], axis=-1)
        key = jax.random.key(seed)
        ks = jax.random.split(key, 8)
        s = lambda fan_in: 1.0 / math.sqrt(fan_in)
        return {'x': jax.random.normal(ks[0], (B, T, D_MODEL), jnp.float32), 'W_kv_down': jax.random.normal(ks[1], (D_MODEL, D_C), jnp.float32) * s(D_MODEL), 'W_k_up': jax.random.normal(ks[2], (D_C, D_MODEL), jnp.float32) * s(D_C), 'W_v_up': jax.random.normal(ks[3], (D_C, D_MODEL), jnp.float32) * s(D_C), 'W_q': jax.random.normal(ks[4], (D_MODEL, D_MODEL), jnp.float32) * s(D_MODEL), 'W_q_rope': jax.random.normal(ks[5], (D_MODEL, D_R), jnp.float32) * s(D_MODEL), 'W_k_rope': jax.random.normal(ks[6], (D_C, D_R), jnp.float32) * s(D_C), 'W_o': jax.random.normal(ks[7], (D_MODEL, D_MODEL), jnp.float32) * s(D_MODEL)}
    _L1_attn_in = _L1_attn_setup()

    def _L1_ffn_setup():
        import jax, jax.numpy as jnp
        import numpy as np
        B, T, C = (4, 256, 128)
        E, F, K = (8, 256, 2)
        key = jax.random.key(seed)
        k0, k1, k2, k3 = jax.random.split(key, 4)
        s = lambda d: 1.0 / np.sqrt(d)
        x = jax.random.normal(k0, (B, T, C), dtype=jnp.float32)
        Wr = jax.random.normal(k1, (E, C), dtype=jnp.float32) * s(C)
        W1 = jax.random.normal(k2, (E, 2 * F, C), dtype=jnp.float32) * s(C)
        W2 = jax.random.normal(k3, (E, C, F), dtype=jnp.float32) * s(F)
        return {'x': x, 'Wr': Wr, 'W1': W1, 'W2': W2}
    _L1_ffn_in = _L1_ffn_setup()
    _d = {'L0_attn_x': _L0_attn_in['x'], 'L0_attn_Wq': _L0_attn_in['Wq'], 'L0_attn_bq': _L0_attn_in['bq'], 'L0_attn_Wk': _L0_attn_in['Wk'], 'L0_attn_bk': _L0_attn_in['bk'], 'L0_attn_Wv': _L0_attn_in['Wv'], 'L0_attn_bv': _L0_attn_in['bv'], 'L0_attn_Wg': _L0_attn_in['Wg'], 'L0_attn_bg': _L0_attn_in['bg'], 'L0_attn_Wo': _L0_attn_in['Wo'], 'L0_attn_bo': _L0_attn_in['bo'], 'L0_attn_gamma': _L0_attn_in['gamma'], 'L0_attn_beta': _L0_attn_in['beta'], 'L0_ffn_gate_w': _L0_ffn_in['gate_w'], 'L0_ffn_gate_b': _L0_ffn_in['gate_b'], 'L0_ffn_w1': _L0_ffn_in['w1'], 'L0_ffn_b1': _L0_ffn_in['b1'], 'L0_ffn_w2': _L0_ffn_in['w2'], 'L0_ffn_b2': _L0_ffn_in['b2'], 'L1_attn_W_kv_down': _L1_attn_in['W_kv_down'], 'L1_attn_W_k_up': _L1_attn_in['W_k_up'], 'L1_attn_W_v_up': _L1_attn_in['W_v_up'], 'L1_attn_W_q': _L1_attn_in['W_q'], 'L1_attn_W_q_rope': _L1_attn_in['W_q_rope'], 'L1_attn_W_k_rope': _L1_attn_in['W_k_rope'], 'L1_attn_W_o': _L1_attn_in['W_o'], 'L1_ffn_Wr': _L1_ffn_in['Wr'], 'L1_ffn_W1': _L1_ffn_in['W1'], 'L1_ffn_W2': _L1_ffn_in['W2']}
    _x0 = _d['L0_attn_x']
    _d['L0_attn_x'] = jax.random.normal(jax.random.fold_in(jax.random.key(seed), 1), (16, 256, 128), dtype=_x0.dtype)
    del _x0
    return _d

def reference(L0_attn_x, L0_attn_Wq, L0_attn_bq, L0_attn_Wk, L0_attn_bk, L0_attn_Wv, L0_attn_bv, L0_attn_Wg, L0_attn_bg, L0_attn_Wo, L0_attn_bo, L0_attn_gamma, L0_attn_beta, L0_ffn_gate_w, L0_ffn_gate_b, L0_ffn_w1, L0_ffn_b1, L0_ffn_w2, L0_ffn_b2, L1_attn_W_kv_down, L1_attn_W_k_up, L1_attn_W_v_up, L1_attn_W_q, L1_attn_W_q_rope, L1_attn_W_k_rope, L1_attn_W_o, L1_ffn_Wr, L1_ffn_W1, L1_ffn_W2):

    def _L0_attn_ref(x, Wq, bq, Wk, bk, Wv, bv, Wg, bg, Wo, bo, gamma, beta):
        import jax, jax.numpy as jnp
        import numpy as np
        B, T, D, S = (8, 512, 128, 128)
        EPS = 1e-05

        def _gla(x, Wq, bq, Wk, bk, Wv, bv, Wg, bg, Wo, bo, gamma, beta):
            q = x @ Wq + bq
            k = x @ Wk + bk
            v = x @ Wv + bv
            g = jax.nn.sigmoid(x @ Wg + bg)

            def step(state, qkvg):
                qt, kt, vt, gt = qkvg
                state = gt[:, :, None] * state + kt[:, :, None] * vt[:, None, :]
                out = jnp.einsum('bs,bst->bt', qt, state)
                return (state, out)
            init = jnp.zeros((x.shape[0], Wq.shape[1], Wq.shape[1]), x.dtype)
            seq = (q.transpose(1, 0, 2), k.transpose(1, 0, 2), v.transpose(1, 0, 2), g.transpose(1, 0, 2))
            _, outs = jax.lax.scan(step, init, seq)
            out = outs.transpose(1, 0, 2)
            y = x + out @ Wo + bo
            mu = jnp.mean(y, axis=-1, keepdims=True)
            var = jnp.mean(jnp.square(y - mu), axis=-1, keepdims=True)
            return (y - mu) * jax.lax.rsqrt(var + EPS) * gamma + beta
        return _gla(x, Wq, bq, Wk, bk, Wv, bv, Wg, bg, Wo, bo, gamma, beta)

    def _L0_ffn_ref(x, gate_w, gate_b, w1, b1, w2, b2):
        import jax, jax.numpy as jnp
        import numpy as np
        D = 128
        H = 512
        E = 64
        K = 3
        B, S = (2, 256)
        C = 64
        xf = x.reshape(-1, D)
        T = xf.shape[0]
        logits = xf @ gate_w + gate_b
        top_l, top_i = jax.lax.top_k(logits, K)
        gates = jax.nn.softmax(top_l, axis=-1)
        fe = top_i.reshape(-1)
        fg = gates.reshape(-1)
        tok = jnp.repeat(jnp.arange(T), K)
        oh = jax.nn.one_hot(fe, E, dtype=jnp.int32)
        pos = (jnp.cumsum(oh, axis=0) * oh).sum(-1) - 1
        valid = pos < C
        buf = jnp.zeros((E, C, D), x.dtype).at[fe, pos].set(xf[tok], mode='drop')
        h = jax.nn.gelu(jnp.einsum('ecd,edh->ech', buf, w1) + b1[:, None, :], approximate=False)
        y = jnp.einsum('ech,ehd->ecd', h, w2) + b2[:, None, :]
        rows = y[fe, jnp.minimum(pos, C - 1)] * (fg * valid.astype(x.dtype))[:, None]
        out = jnp.zeros_like(xf).at[tok].add(rows)
        return out.reshape(x.shape)

    def _L1_attn_ref(x, W_kv_down, W_k_up, W_v_up, W_q, W_q_rope, W_k_rope, W_o):
        import jax, jax.numpy as jnp
        import numpy as np
        import math
        D_MODEL, D_C, D_R, NH = (128, 128, 32, 16)
        HD = D_MODEL // NH
        B, T = (2, 256)

        def _rope_tables(T, d_R):
            inv_freq = 1.0 / 10000.0 ** (jnp.arange(0, d_R, 2, dtype=jnp.float32) / d_R)
            t = jnp.arange(T, dtype=jnp.float32)
            freqs = jnp.outer(t, inv_freq)
            return (jnp.cos(freqs), jnp.sin(freqs))

        def _rotary_apply(x, cos, sin):
            d = x.shape[-1]
            x1, x2 = (x[..., :d // 2], x[..., d // 2:])
            return jnp.concatenate([x1 * cos - x2 * sin, x2 * cos + x1 * sin], axis=-1)
        Bb, Tt, _ = x.shape
        cos, sin = _rope_tables(Tt, D_R)
        cos = cos[None]
        sin = sin[None]
        c_kv = x @ W_kv_down
        k_rope = _rotary_apply(c_kv @ W_k_rope, cos, sin)
        k = (c_kv @ W_k_up).reshape(Bb, Tt, NH, HD)
        v = (c_kv @ W_v_up).reshape(Bb, Tt, NH, HD)
        q = (x @ W_q).reshape(Bb, Tt, NH, HD)
        q_rope = _rotary_apply(x @ W_q_rope, cos, sin)
        scale = math.sqrt(HD + D_R)
        scores = jnp.einsum('bqhd,bkhd->bhqk', q, k)
        scores = scores + jnp.einsum('bqr,bkr->bqk', q_rope, k_rope)[:, None]
        scores = scores / scale
        causal = jnp.triu(jnp.ones((Tt, Tt), dtype=bool), k=1)
        scores = jnp.where(causal[None, None], -jnp.inf, scores)
        w = jax.nn.softmax(scores, axis=-1)
        attn = jnp.einsum('bhqk,bkhd->bqhd', w, v).reshape(Bb, Tt, D_MODEL)
        return attn @ W_o

    def _L1_ffn_ref(x, Wr, W1, W2):
        import jax, jax.numpy as jnp
        import numpy as np
        B, T, C = (4, 256, 128)
        E, F, K = (8, 256, 2)
        Bb, Tt, Cc = x.shape
        flat = x.reshape(-1, Cc)
        N = flat.shape[0]
        logits = flat @ Wr.T
        weights, ids = jax.lax.top_k(logits, K)
        weights = jax.nn.softmax(weights, axis=-1)
        rows = jnp.arange(N)[:, None]
        router_weights = jnp.zeros((N, E), dtype=flat.dtype).at[rows, ids].add(weights)
        h = jnp.einsum('nc,efc->nef', flat, W1)
        val, gate = (h[..., :F], h[..., F:])
        act = val * jax.nn.silu(gate)
        expert_outputs = jnp.einsum('nef,ecf->nec', act, W2)
        out = jnp.einsum('nec,ne->nc', expert_outputs, router_weights)
        return out.reshape(Bb, Tt, Cc)
    x = L0_attn_x
    x = x + _L0_attn_ref(_layernorm(x, axis=-1), L0_attn_Wq, L0_attn_bq, L0_attn_Wk, L0_attn_bk, L0_attn_Wv, L0_attn_bv, L0_attn_Wg, L0_attn_bg, L0_attn_Wo, L0_attn_bo, L0_attn_gamma, L0_attn_beta)
    x = x + _L0_ffn_ref(_layernorm(x, axis=-1), L0_ffn_gate_w, L0_ffn_gate_b, L0_ffn_w1, L0_ffn_b1, L0_ffn_w2, L0_ffn_b2)
    x = x + _L1_attn_ref(_layernorm(x, axis=-1), L1_attn_W_kv_down, L1_attn_W_k_up, L1_attn_W_v_up, L1_attn_W_q, L1_attn_W_q_rope, L1_attn_W_k_rope, L1_attn_W_o)
    x = x + _L1_ffn_ref(_layernorm(x, axis=-1), L1_ffn_Wr, L1_ffn_W1, L1_ffn_W2)
    return x

_drawn_inputs = setup_inputs


def setup_inputs(seed=0):
    import zlib

    import numpy as np

    out = dict(_drawn_inputs(seed))
    spreads = {'L0_attn_bq': (0.0, 0.1),
     'L0_attn_bk': (0.0, 0.1),
     'L0_attn_bv': (0.0, 0.1),
     'L0_attn_bg': (0.0, 0.1),
     'L0_attn_bo': (0.0, 0.329),
     'L0_attn_gamma': (1.0, 0.2),
     'L0_attn_beta': (0.0, 0.1),
     'L0_ffn_gate_b': (0.0, 0.1),
     'L0_ffn_b1': (0.0, 0.575),
     'L0_ffn_b2': (0.0, 0.1)}
    factors = {'L0_ffn_w1': 2.921}
    for name, (base, spread) in spreads.items():
        noise = np.random.default_rng([zlib.crc32(name.encode()), seed]).standard_normal(out[name].shape)
        drawn = base * np.exp(spread * noise) if base else spread * noise
        out[name] = jnp.asarray(drawn.astype(out[name].dtype))
    for name, factor in factors.items():
        out[name] = (out[name] * factor).astype(out[name].dtype)
    return out
```

```python
from contextlib import ExitStack

import numpy as np

import concourse.bass as bass
from concourse import mybir

ALU = mybir.AluOpType
ACT = mybir.ActivationFunctionType
AX = mybir.AxisListType
F32 = mybir.dt.float32
BF16 = mybir.dt.bfloat16
U32 = mybir.dt.uint32
U8 = mybir.dt.uint8

P = 128
B, T = 16, 256
NTOK = B * T
NT = NTOK // P
GT = 4
GN = GT * P
NG = NT // GT
GB = GN // T
LEVELS = [1, 2, 4, 8, 16, 32, 64]
NL = len(LEVELS)
EPS = 1e-5
NLP = NL + 1
NCONST = 17

E0, K0, CAP, H0 = 64, 3, 64, 512
HC = H0 // P
NSLOT0 = E0 * CAP
RING = 16
NPAIR = E0 // 2
NH, HD, DR = 16, 8, 32
SCORE_SCALE = float(1.0 / np.sqrt(HD + DR))
ND = NH // 2
RD = 4
KR = 3 * DR
KN = 3 * HD
KM = KR + KN
KS = KM + 2
MASKED = -1e30
E1, K1, F1 = 8, 2, 256
REG = NTOK
ND1 = NTOK * K1 // P + E1
ND1 = (ND1 + 7) // 8 * 8
LAP1 = 8
NQ1 = 4
AHEAD = 2
F32R = mybir.dt.float32r
NROUND = E0 // RING
PAIRS = RING // 2
NQ = 4


class Chain:

    def __init__(self, eng, sem, group, n, base=0, first=0):
        self.eng, self.sem, self.base, self.n, self.k = eng, sem, group * n + base, n, first

    def __call__(self, ins):
        self.k += 1
        ins.then_inc(self.sem, 1)
        self.eng.wait_ge(self.sem, self.base + self.k)

    def end(self, last=None):
        last = self.n if last is None else last
        assert self.k == last, (self.k, last)


def after(g, n):
    return not isinstance(g, int) or g >= n


def within(g, n):
    return not isinstance(g, int) or g < n


class Group:

    def __init__(self, j, p, k):
        self.par, self.half = (p - k) % 2, j + (p - k) // 2
        self.g = self.half * 2 + self.par


def steps(eng, stages):
    lags = 1 + max(k for _, k in stages)

    def step(j, p, there):
        for stage, k in stages:
            if there(k):
                stage(Group(j, p, k))

    full = lags // 2
    for s in range(2 * full):
        step(s // 2, s % 2, lambda k: 0 <= s - k)
    with eng.Fori(full, NG // 2) as j:
        for p in range(2):
            step(j, p, lambda k: True)
    for s in range(NG, NG + lags - 1):
        step(s // 2, s % 2, lambda k: s - k < NG)


def build(nc, x, Wq, bq, Wk, bk, Wv, bv, Wg, bg, Wo, bo, gamma, beta, gate_w, gate_b, w1, b1t, w2, b2,
          Wkvd, Wku, Wvu, Wq1, Wqr, Wkr, Wo1, Wr, W1t, W2t, out, const, masks, rope):
    with ExitStack() as ctx:
        def sb(name, shape, dt=F32):
            return ctx.enter_context(nc.sbuf_tensor("sb_" + name, shape, dt))

        def sem(name):
            return ctx.enter_context(nc.semaphore(name))

        slots_in = nc.dram_tensor("slots_in", [NSLOT0, P], F32).ap()
        slots_out = nc.dram_tensor("slots_out", [NSLOT0, P], F32).ap()
        parts = nc.dram_tensor("parts", [2, 2, KN, NH, GN], F32).ap()
        rows1_in = nc.dram_tensor("rows1_in", [E1 * REG, P], F32).ap()
        rows1_out = nc.dram_tensor("rows1_out", [ND1 * P, P], F32).ap()

        pairbank = [ctx.enter_context(nc.psum_tensor(f"banks{i}", [P, 1024], F32)) for i in range(2)]
        bank = [pairbank[i // 2][:, i % 2 * 512:(i % 2 + 1) * 512] for i in range(4)]
        bank += [ctx.enter_context(nc.psum_tensor(f"bank{i}", [P, 512], F32)) for i in range(4, 8)]

        X = sb("X", [P, NT, P])
        cst = sb("cst", [P, 2 * P + E0 + ND1 + NT])
        iota_t = cst[:, 2 * P + E0:2 * P + E0 + ND1]
        iota128 = cst[:, 2 * P + E0 + ND1:]
        ident = cst[:, 0:128]
        iota_e = cst[:, 256:320]
        mask_sb = sb("mask_sb", [P, NL, GT, P // 2], U8)
        tri = sb("tri", [P, P], BF16)
        ones = sb("ones", [P, P], BF16)
        wq_sb, wk_sb, wv_sb, wg_sb, wo_sb = (sb(n, [P, P]) for n in ("wq", "wk", "wv", "wg", "wo"))
        gw_sb = sb("gw", [P, E0])
        bq_c, bk_c, bg_c = (sb(n, [P, 1]) for n in ("bq", "bk", "bg"))
        bv_b, bo_b, gamma_b, beta_b = (sb(n, [P, P]) for n in ("bv_b", "bo_b", "gamma_b", "beta_b"))
        gb_b = sb("gb_b", [P, E0])
        mhalf = sb("mhalf", [P, GT])
        zrow = sb("zrow", [P, 1024])
        top0 = sb("top0", [P, NT, K0])
        gslot = sb("gslot", [P, NT, K0], U32)
        valid = sb("valid", [P, NT, K0])
        count = sb("count", [P, E0])
        countb = sb("countb", [P, 2, E0], BF16)

        Y = sb("Y", [P, GT, P])
        st = sb("st", [P, 5, GT, 6])
        mv = sb("mv", [P, 5, GT, 2])
        ve = sb("ve", [P, 5, GT])
        rs = sb("rs", [P, 5, GT])

        early = ExitStack()

        def eb(name, shape, dt=F32):
            return early.enter_context(nc.sbuf_tensor("sb_" + name, shape, dt))

        xn = eb("xn", [P, 2, GT, P])
        xb = eb("xb", [P, 2, GT, P])
        xnT = eb("xnT", [P, GN])
        Q = eb("Q", [P, 2, GN])
        K = eb("K", [P, 2, GN])
        G = eb("G", [P, 2, GN])
        V = eb("V", [P, 2, GT, P])
        AD = eb("AD", [P, GN])
        AXT = eb("AXT", [P, GB, P])
        OT = eb("OT", [P, GN])
        xf = eb("xf", [P, 2, GT, P])
        xfT = eb("xfT", [P, GN])
        Tm = [eb(f"T{m}", [P, GN // m]) for m in LEVELS[1:]]
        mask_in = eb("mask_in", [P, NL, P // 2])
        lg = eb("lg", [P, GT, E0])
        best = eb("best", [P, GT, 8])
        ix = eb("ix", [P, GT, 8], U32)
        ixf = eb("ixf", [P, GT, K0])
        oh = eb("oh", [P, GT, K0, E0])
        M = eb("M", [P, GT, E0])
        Mb = eb("Mb", [P, GT, E0], BF16)
        ohp = eb("ohp", [P, GT, K0, E0])
        pos = eb("pos", [P, GT, K0])
        r0 = eb("r0", [P, GT, K0])
        r1 = eb("r1", [P, GT, K0])
        r2 = eb("r2", [P, GT, K0])
        gcnt = eb("gcnt", [P, E0])
        sslot = eb("sslot", [P, 2, GT, K0], U32)

        w1r = eb("w1r", [P, RING, H0])
        w2r = eb("w2r", [P, RING, HC, P])
        xs = eb("xs", [P, NQ, P])
        xsT = eb("xsT", [P, 2, P])
        hs = eb("hs", [P, 2, H0])
        hT = eb("hT", [P, 2, HC, P])
        gT = eb("gT", [P, 2, HC, P])
        b1T = eb("b1T", [P, E0, HC])
        b2_b = eb("b2_b", [P, NPAIR, P])
        ys = eb("ys", [P, NQ, P])

        early.close()

        wkvd_sb, wku_sb, wvu_sb, wq1_sb, wo1_sb = (sb(n, [P, P]) for n in ("wkvd", "wku", "wvu", "wq1", "wo1"))
        wqr_sb, wkr_sb = sb("wqr", [P, 2 * DR]), sb("wkr", [P, 2 * DR])
        wr_sb = sb("wr", [P, E1])
        rope_sb = sb("rope", [2 * DR, T])
        identb = sb("identb", [P, P], BF16)
        ones8 = sb("ones8", [P, E1])
        maskq = sb("maskq", [P, 2, P], BF16)
        maskk = sb("maskk", [P, 2, P], BF16)
        gates = sb("gates", [P, NT, K0])
        gsum = sb("gsum", [P, NT])
        gidx = sb("gidx", [P, 2, GT, K0], U32)
        R = sb("R", [P, 2, GT * K0, P])
        xa = sb("xa", [P, GT, P])
        xaT = sb("xaT", [P, GN])
        ckvT = sb("ckvT", [P, GN])
        qkh = sb("qkh", [P, 2, GN], F32R)
        qkl = sb("qkl", [P, 2, GN], F32R)
        rt = sb("rt", [DR, 2, GN])
        rp = sb("rp", [KR, 2, GN], F32R)
        SQ = sb("SQ", [P, 2 * RD, GN], F32R)
        SK = sb("SK", [P, 2 * RD, GN], F32R)
        V1 = sb("V1", [P, 2, GT, NH, 32])
        mx = sb("mx", [P, 2, 2, GB, 2])
        ms = sb("ms", [P, 2, 2 * 8], F32R)
        mT = sb("mT", [2 * 8, 2, P])
        onerow = sb("onerow", [2 * RD, GN])
        PT = sb("PT", [P, 2, 4, 384])
        raw = sb("raw", [P, GN])
        rec = sb("rec", [P, 4, 4])
        att = sb("att", [P, GT, P])
        attT = sb("attT", [P, GN])
        xg = sb("xg", [P, 2, GT, P])
        xgT = sb("xgT", [P, GN])
        lg1 = sb("lg1", [P, GT, E1])
        best1 = sb("best1", [P, GT, 8])
        ix1 = sb("ix1", [P, GT, 8], U32)
        ixa = sb("ixa", [P, NT, K1])
        posa = sb("posa", [P, NT, K1])
        oh1 = sb("oh1", [P, GT, K1, E1])
        ohp1 = sb("ohp1", [P, GT, K1, E1])
        M1 = sb("M1", [P, GT, E1])
        M1b = sb("M1b", [P, GT, E1], BF16)
        gcnt1 = sb("gcnt1", [P, E1])
        count1 = sb("count1", [P, E1])
        count1b = sb("count1b", [P, E1], BF16)
        srow1 = sb("srow1", [P, 2, GT, K1], U32)
        w1d = sb("w1d", [P, E1, 2 * F1])
        w2d = sb("w2d", [P, E1, 2, P])
        ntile = sb("ntile", [P, E1])
        tend = sb("tend", [P, E1])
        tbase = sb("tbase", [P, E1])
        tw = sb("tw", [P, E1])
        cmp1 = sb("cmp1", [P, E1, NT])
        cmp2 = sb("cmp2", [P, ND1, E1])
        cmp3 = sb("cmp3", [P, ND1, E1])
        tl = sb("tl", [P, 2, ND1])
        tli = sb("tli", [P, 2, ND1], mybir.dt.int32)
        grow1 = sb("grow1", [P, NT, K1], U32)
        gt1 = sb("gt1", [P, NT, K1])
        gw1 = sb("gw1", [P, NT, K1])
        xd = sb("xd", [P, NQ1, P])
        xdT = sb("xdT", [P, 2, P])
        sg = sb("sg", [P, 2, F1])
        ac = sb("ac", [P, 2, F1])
        acT = sb("acT", [P, 2, F1])
        yd = sb("yd", [P, NQ1, P])

        s_const, s_x, s_zero = sem("s_const"), sem("s_x"), sem("s_zero")
        s_tri, s_step = sem("s_tri"), sem("s_step")
        s_ve = [sem(f"s_ve{i}") for i in range(3)]
        s_rs = [sem(f"s_rs{i}") for i in range(3)]
        s_xn = sem("s_xn")
        s_xnb = sem("s_xnb")
        s_xnTp, s_xnT = sem("s_xnTp"), sem("s_xnT")
        s_q, s_k, s_g, s_v = sem("s_q"), sem("s_k"), sem("s_g"), sem("s_v")
        s_qe, s_ge, s_ve_ = sem("s_qe"), sem("s_ge"), sem("s_vev")
        s_lev, s_upd, s_aev = sem("s_lev"), sem("s_upd"), sem("s_aev")
        s_cross, s_axt = sem("s_cross"), sem("s_axt")
        s_av, s_ot, s_wo, s_y = sem("s_av"), sem("s_ot"), sem("s_wo"), sem("s_y")
        s_xf, s_xfTp, s_xfT, s_lg = sem("s_xf"), sem("s_xfTp"), sem("s_xfT"), sem("s_lg")
        s_M, s_pos, s_posr, s_slot = sem("s_M"), sem("s_pos"), sem("s_posr"), sem("s_slot")
        s_scat = [sem("s_scat0"), sem("s_scat1")]
        c_F, c_G, c_H, c_W = sem("c_F"), sem("c_G"), sem("c_H"), sem("c_W")
        s_w = [sem(f"s_w{i}") for i in range(PAIRS)]
        s_b1 = sem("s_b1")
        s_xs = [sem(f"s_xs{i}") for i in range(NQ)]
        s_xsTp, s_xsT, s_h, s_hs, s_hTp, s_hT, s_gT, s_yp, s_ys = (
            sem(n) for n in ("s_xsTp", "s_xsT", "s_h", "s_hs", "s_hTp", "s_hT", "s_gT", "s_yp", "s_ys"))
        s_yo = [sem(f"s_yo{i}") for i in range(NQ)]
        s_out = sem("s_out")
        s_w2c, s_pre = sem("s_w2c"), sem("s_pre")
        s_gexp, s_gsub = sem("s_gexp"), sem("s_gsub")
        s_gat = [sem("s_gat0"), sem("s_gat1")]
        s_radd, s_gidx = sem("s_radd"), sem("s_gidx")
        s_ve += [sem("s_ve3"), sem("s_ve4")]
        s_rs += [sem("s_rs3"), sem("s_rs4")]
        (s_xa, s_xaTp, s_xaT, s_ckvp, s_ckv, s_q1p, s_qh, s_ql, s_qr, s_rq, s_kp, s_kh, s_kl, s_v1p, s_v1, s_kr, s_rk,
         s_parts, s_max, s_maxr, s_ms, s_mTp, s_mT, s_st, s_exp, s_pv, s_raw, s_rawTp, s_norm,
         s_attTp, s_attT, s_wo1, s_x3, s_xg, s_xgTp, s_xgT, s_lg1, s_M1, s_pos1, s_row1) = (
            sem(n) for n in ("s_xa s_xaTp s_xaT s_ckvp s_ckv s_q1p s_qh s_ql s_qr s_rq s_kp s_kh s_kl s_v1p s_v1 s_kr s_rk "
                             "s_parts s_max s_maxr s_ms s_mTp s_mT s_st s_exp s_pv s_raw s_rawTp s_norm "
                             "s_attTp s_attT s_wo1 s_x3 s_xg s_xgTp s_xgT s_lg1 s_M1 s_pos1 s_row1").split())
        s_fill = [sem(f"s_fill{i}") for i in range(RD)]
        s_shift = [sem(f"s_shift{i}") for i in range(RD)]
        s_scat1 = [sem("s_scat1_0"), sem("s_scat1_1")]
        c_C, c_N, c_R, c_T, c_Q = (sem(n) for n in ("c_C", "c_N", "c_R", "c_T", "c_Q"))
        s_fin1 = sem("s_fin1")
        s_tot, s_tiles = sem("s_tot"), sem("s_tiles")
        s_sg, s_ac, s_acTp, s_acT, s_ydp, s_yd = (sem(n) for n in "s_sg s_ac s_acTp s_acT s_ydp s_yd".split())
        s_fin = sem("s_fin")
        s_ones1 = sem("s_ones1")
        s_zero1 = sem("s_zero1")
        s_vinit, s_pinit = sem("s_vinit"), sem("s_pinit")


        block = ctx.enter_context(nc.Block())

        def stands_alone(eng):
            eng.sem_inc(s_step, 1)

        def blocks(ap2, m):
            return ap2.rearrange("p (c two m) -> p c two m", two=2, m=m)

        @block.sync
        def _(sp):
            sp.dma_start(X[:, 0:GT, :], x[0:GN, :].rearrange("(t p) d -> p t d", p=P)).then_inc(s_x, 16)
            for dst, src in ((cst[:], const[:, :]), (wq_sb[:], Wq[:, :]), (wk_sb[:], Wk[:, :]),
                             (wg_sb[:], Wg[:, :]), (wv_sb[:], Wv[:, :]), (wo_sb[:], Wo[:, :]),
                             (gw_sb[:], gate_w[:, :]), (mask_in[:], masks.rearrange("p (l n) -> p l n", l=NL))):
                sp.dma_start(dst, src).then_inc(s_const, 16)
            for dst, src in ((bq_c, bq), (bk_c, bk), (bg_c, bg)):
                sp.dma_start(dst[:], src.rearrange("(p o) -> p o", o=1)).then_inc(s_const, 16)
            for dst, src in ((bv_b, bv), (bo_b, bo), (gamma_b, gamma), (beta_b, beta), (gb_b, gate_b)):
                sp.dma_start(dst[:], src.partition_broadcast(P)).then_inc(s_const, 16)
            sp.dma_start(X[:, GT:NT, :], x[GN:NTOK, :].rearrange("(t p) d -> p t d", p=P)).then_inc(s_const, 16)
            sp.wait_ge(s_vinit, 1)
            sp.dma_start(slots_in.rearrange("(p t) d -> p (t d)", p=P)[:, 0:1024], zrow[:]).then_inc(s_zero, 16)
            sp.dma_start(slots_in.rearrange("(p t) d -> p (t d)", p=P)[:, 1024:2048], zrow[:]).then_inc(s_zero, 16)
            sp.dma_start(slots_in.rearrange("(p t) d -> p (t d)", p=P)[:, 2048:3072], zrow[:]).then_inc(s_zero, 16)
            sp.dma_start(slots_in.rearrange("(p t) d -> p (t d)", p=P)[:, 3072:4096], zrow[:]).then_inc(s_zero, 16)
            z1 = rows1_in.rearrange("(a p t) d -> a p (t d)", p=P, t=8)
            for a in range(8):
                sp.dma_start(z1[4 * a:4 * a + 4].rearrange("a p n -> p a n"), zrow[:].unsqueeze(1).broadcast_to([P, 4, 1024])).then_inc(s_zero1, 16)
            sp.dma_start(b1T[:], b1t.rearrange("p (e c) -> p e c", c=HC)).then_inc(s_b1, 16)
            for h in range(2):
                sp.dma_start(b2_b[h * CAP:(h + 1) * CAP], b2.rearrange("(a two) d -> two a d", two=2)[h].partition_broadcast(CAP)
                             ).then_inc(s_b1, 16)

            def weights(pair, i):
                e = pair * 2
                sp.dma_start(w1r[:, 2 * i:2 * i + 2, :], w1[bass.ds(e, 2)].rearrange("e d h -> d e h")).then_inc(s_w[i], 16)
                sp.dma_start(w2r[:, 2 * i:2 * i + 2].rearrange("p e c d -> p (e c) d"),
                             w2[bass.ds(e, 2)].rearrange("e (c p) d -> p (e c) d", p=P)).then_inc(s_w[i], 16)

            def slots(pair, q):
                sp.dma_start(xs[:, q, :], slots_in[bass.ds(pair * P, P), :]).then_inc(s_xs[q], 16)

            def store(pair, q):
                sp.wait_ge(s_ys, pair + 1)
                sp.dma_start(slots_out[bass.ds(pair * P, P), :], ys[:, q, :]).then_inc(s_yo[q], 16)

            for pair in range(PAIRS):
                weights(pair, pair)
            sp.wait_ge(s_zero, 16 * 4)
            for p in range(2):
                sp.wait_ge(s_scat[p], 16 * GT * K0 * (NG // 2))
            def slots_after(pair, q):
                sp.wait_ge(s_xsTp, pair - NQ + 1)
                slots(pair, q)

            for pair in range(NQ):
                slots(pair, pair)
            for pair in range(NQ, NQ + AHEAD):
                slots_after(pair, pair % NQ)
            with sp.Fori(0, NROUND - 1) as r:
                for i in range(PAIRS):
                    pair = r * PAIRS + i
                    slots_after(pair + NQ + AHEAD, (i + AHEAD) % NQ)
                    store(pair, i % NQ)
                    weights(pair + PAIRS, i)
            for pair in range(NPAIR - PAIRS, NPAIR):
                if pair + NQ + AHEAD < NPAIR:
                    slots_after(pair + NQ + AHEAD, (pair + AHEAD) % NQ)
                store(pair, pair % NQ)
            for q in range(NQ):
                sp.wait_ge(s_yo[q], 16 * (NPAIR // NQ))

            for dst, src in ((wkvd_sb[:], Wkvd[:, :]), (wku_sb[:], Wku[:, :]), (wvu_sb[:], Wvu[:, :]), (wq1_sb[:], Wq1[:, :]),
                             (wo1_sb[:], Wo1[:, :]), (wr_sb[:], Wr[:, :]), (rope_sb[:], rope[:, :]),
                             (wqr_sb[:, 0:DR], Wqr[:, :]), (wqr_sb[:, DR:DR + 16], Wqr[:, 16:32]), (wqr_sb[:, DR + 16:], Wqr[:, 0:16]),
                             (wkr_sb[:, 0:DR], Wkr[:, :]), (wkr_sb[:, DR:DR + 16], Wkr[:, 16:32]), (wkr_sb[:, DR + 16:], Wkr[:, 0:16])):
                sp.dma_start(dst, src).then_inc(s_w2c, 16)
            sp.wait_ge(s_pre, 1)
            for r in range(2):
                sp.dma_start(SK[KM + r:KM + r + 1].bitcast(F32), onerow[:]).then_inc(s_ones1, 16)
            sp.dma_start(w1d[:], W1t.rearrange("p (e n) -> p e n", e=E1)).then_inc(s_w2c, 16)
            sp.dma_start(w2d[:], W2t.rearrange("p (e c n) -> p e c n", e=E1, c=2)).then_inc(s_w2c, 16)

            def write_parts(grp):
                g, p = grp.g, grp.par
                sp.wait_ge(s_ql, g + 1)
                sp.wait_ge(s_kl, g + 1)
                for side, order in ((0, (qkh, qkh, qkl)), (1, (qkh, qkl, qkh))):
                    for r, src in enumerate(order):
                        sp.dma_start(parts[p, side, r * HD:(r + 1) * HD].rearrange("d h n -> (d h) n"),
                                     src[:, side].bitcast(F32)).then_inc(s_parts, 16)

            def fill(grp, i):
                g, p, r = grp.g, grp.par, i % RD
                if i == 0:
                    sp.wait_ge(s_parts, 96 * (g + 1))
                    sp.wait_ge(s_rk, g + 1)
                if after(g, 1) or i >= RD:
                    sp.wait_ge(s_st, 4 * (g * ND + i - RD + 1))
                for side, S in ((0, SQ), (1, SK)):
                    if i < RD:
                        sp.dma_start(S[0:KR, 2 * r:2 * r + 2, :].bitcast(F32),
                                     rp[:, side].bitcast(F32).unsqueeze(1).broadcast_to([KR, 2, GN])).then_inc(s_fill[r], 16)
                    sp.dma_start(S[KR:KM, 2 * r:2 * r + 2, :].bitcast(F32), parts[p, side, :, 2 * i:2 * i + 2, :]).then_inc(s_fill[r], 16)

            def shift(grp, i):
                g, r = grp.g, i % RD
                sp.wait_ge(s_mT, g * ND + i + 1)
                for h in range(2):
                    sp.dma_start(SQ[KM + h:KM + h + 1, 2 * r:2 * r + 2, :].bitcast(F32), mT[8 * h:8 * h + 8, i % 2, :]
                                 ).then_inc(s_shift[r], 16)

            def attention(grp, nxt):
                shift(grp, 0)
                shift(grp, 1)
                fill(grp, 3)
                if nxt is not None:
                    write_parts(nxt)
                for i in range(ND):
                    if 1 <= i < ND - 3:
                        fill(grp, i + 3)
                    elif i >= ND - 3 and nxt is not None:
                        fill(nxt, i + 3 - ND)
                    if i + 2 < ND:
                        shift(grp, i + 2)

            write_parts(Group(0, 0, 0))
            for i in range(3):
                fill(Group(0, 0, 0), i)
            with sp.Fori(0, NG // 2 - 1) as j:
                attention(Group(j, 0, 0), Group(j, 1, 0))
                attention(Group(j, 1, 0), Group(j + 1, 0, 0))
            attention(Group(NG // 2 - 1, 0, 0), Group(NG // 2 - 1, 1, 0))
            attention(Group(NG // 2 - 1, 1, 0), None)

            for p in range(2):
                sp.wait_ge(s_scat1[p], 16 * GT * K1 * (NG // 2))
            sp.wait_ge(s_zero1, 16 * 8)
            sp.wait_ge(s_tiles, 1)

            def tile_in(t, q):
                row = sp.value_load(tli[0:1, 1, bass.ds(t, 1)], min_val=0, max_val=E1 * REG - P)
                sp.dma_start(xd[:, q, :], rows1_in[bass.ds(row, P), :]).then_inc(s_xs[q], 16)

            def tile_out(t, q):
                sp.wait_ge(s_yd, t + 1)
                sp.dma_start(rows1_out[bass.ds(t * P, P), :], yd[:, q, :]).then_inc(s_yo[q], 16)

            def tile_after(t, q):
                sp.wait_ge(s_xsTp, NPAIR + t - NQ1 + 1)
                tile_in(t, q)

            for q in range(NQ1):
                tile_in(q, q)
            for t in range(NQ1, NQ1 + AHEAD):
                tile_after(t, t % NQ1)
            with sp.Fori(0, ND1 // NQ1 - 2) as lap:
                for q in range(NQ1):
                    tile_after(lap * NQ1 + q + NQ1 + AHEAD, (q + AHEAD) % NQ1)
                    tile_out(lap * NQ1 + q, q)
            for t in range(ND1 - 2 * NQ1, ND1):
                if t + NQ1 + AHEAD < ND1:
                    tile_after(t + NQ1 + AHEAD, (t + AHEAD) % NQ1)
                tile_out(t, t % NQ1)

            out_t = out.rearrange("(t p) d -> p t d", p=P)
            with sp.Fori(0, NG) as g:
                sp.wait_ge(s_fin, g + 1)
                sp.dma_start(out_t[:, bass.ds(g * GT, GT), :], X[:, bass.ds(g * GT, GT), :]).then_inc(s_out, 16)
            sp.wait_ge(s_out, 16 * NG)

        @block.gpsimd
        def _(pool):
            pool.wait_ge(s_const, 16 * NCONST)
            pool.wait_ge(s_x, 16)
            pool.wait_ge(s_vinit, 1)

            def power(i, grp):
                pool.wait_ge(s_ve[i], grp.g + 1)
                pool.tensor_tensor(rs[:, i, :], ve[:, i, :], mhalf[:], ALU.pow).then_inc(s_rs[i], 1)

            def residuals(grp):
                g = grp.g
                pool.wait_ge(s_xn, g + 1)
                if after(g, 2):
                    pool.wait_ge(s_y, g - 1)
                pool.tensor_tensor(xb[:, grp.par], xn[:, grp.par], bo_b[:].unsqueeze(1).broadcast_to([P, GT, P]),
                                   ALU.add).then_inc(s_xnb, 1)
                xt = X[:, bass.ds(g * GT, GT), :]
                pool.tensor_tensor(xt, xt, beta_b[:].unsqueeze(1).broadcast_to([P, GT, P]), ALU.add).then_inc(s_xnb, 1)

            def scatter0(grp):
                pool.wait_ge(s_slot, grp.g + 1)
                stands_alone(pool)
                for t in range(GT):
                    for k in range(K0):
                        pool.indirect_dma_start(
                            out=slots_in[:, :], out_offset=bass.IndirectOffsetOnAxis(ap=sslot[:, grp.par, t, k:k + 1], axis=0),
                            in_=xf[:, grp.par, t, :], in_offset=None, bounds_check=NSLOT0 - 1, oob_is_err=False,
                        ).then_inc(s_scat[grp.par], 16)

            pool.wait_ge(s_zero, 16 * 4)
            steps(pool, [(lambda grp: power(1, grp), 3), (lambda grp: power(2, grp), 3), (lambda grp: power(0, grp), 0),
                         (residuals, 1), (scatter0, 4)])

            for q in range(NQ):
                pool.wait_ge(s_yo[q], 16 * (NPAIR // NQ))

            def gather0(grp):
                if after(grp.g, 2):
                    pool.wait_ge(s_radd, grp.g - 1)
                pool.tensor_copy(gidx[:, grp.par, :, 0:K0], gslot[:, bass.ds(grp.g * GT, GT), :]).then_inc(s_gidx, 1)
                pool.wait_ge(s_gidx, grp.g + 1)
                stands_alone(pool)
                for t in range(GT):
                    for k in range(K0):
                        pool.indirect_dma_start(
                            out=R[:, grp.par, t * K0 + k, :], out_offset=None, in_=slots_out[:, :],
                            in_offset=bass.IndirectOffsetOnAxis(ap=gidx[:, grp.par, t, k:k + 1], axis=0),
                            bounds_check=NSLOT0 - 1, oob_is_err=False).then_inc(s_gat[grp.par], 16)
                power(3, grp)

            def power4(grp):
                power(4, grp)

            def scatter1(grp):
                pool.wait_ge(s_row1, grp.g + 1)
                stands_alone(pool)
                for t in range(GT):
                    for k in range(K1):
                        pool.indirect_dma_start(
                            out=rows1_in[:, :], out_offset=bass.IndirectOffsetOnAxis(ap=srow1[:, grp.par, t, k:k + 1], axis=0),
                            in_=xg[:, grp.par, t, :], in_offset=None, bounds_check=E1 * REG - 1, oob_is_err=False,
                        ).then_inc(s_scat1[grp.par], 16)

            pool.wait_ge(s_zero1, 16 * 8)
            steps(pool, [(power4, 3), (scatter1, 4), (gather0, 0)])

            for q in range(NQ1):
                pool.wait_ge(s_yo[q], 16 * (NPAIR // NQ + ND1 // NQ1))
            pool.wait_ge(s_tiles, 2)

            def gather1(g, p):
                pool.tensor_copy(gidx[:, p, :, 0:K1], grow1[:, bass.ds(g * GT, GT), :]).then_inc(s_gidx, 1)
                pool.wait_ge(s_gidx, NG + g + 1)
                stands_alone(pool)
                for t in range(GT):
                    for k in range(K1):
                        pool.indirect_dma_start(
                            out=R[:, p, t * K1 + k, :], out_offset=None, in_=rows1_out[:, :],
                            in_offset=bass.IndirectOffsetOnAxis(ap=gidx[:, p, t, k:k + 1], axis=0),
                            bounds_check=ND1 * P - 1, oob_is_err=False).then_inc(s_gat[p], 16)
            gather1(0, 0)
            gather1(1, 1)
            with pool.Fori(1, NG // 2) as j:
                for p in range(2):
                    pool.wait_ge(s_fin, 2 * j + p - 1)
                    gather1(2 * j + p, p)

        @block.scalar
        def _(act):
            act.wait_ge(s_const, 16 * NCONST)

            def norm_in(grp):
                act.wait_ge(s_xnTp, grp.g + 1)
                act.activation(xnT[:], bank[0][:], ACT.Copy).then_inc(s_xnT, 1)

            def queries_keys(grp):
                g, p = grp.g, grp.par
                act.wait_ge(s_q, g + 1)
                act.activation(Q[:, p], bank[1][:], ACT.Identity, bias=bq_c[:, 0:1])
                act.wait_ge(s_k, g + 1)
                act.activation(K[:, p], bank[0][:], ACT.Identity, bias=bk_c[:, 0:1]).then_inc(s_qe, 1)

            def gate(grp):
                act.wait_ge(s_g, grp.g + 1)
                act.activation(G[:, grp.par], bank[1][:], ACT.Sigmoid, bias=bg_c[:, 0:1]).then_inc(s_ge, 1)

            def cross(grp):
                act.wait_ge(s_cross, grp.g + 1)
                act.activation(AXT[:], bank[4][:, 0:GB * P].rearrange("p (b n) -> p b n", b=GB), ACT.Copy).then_inc(s_axt, 1)

            def attended(grp):
                act.wait_ge(s_av, grp.g + 1)
                act.activation(OT[:], bank[5][:], ACT.Copy).then_inc(s_ot, 1)

            def router_in0(grp):
                act.wait_ge(s_xfTp, grp.g + 1)
                act.activation(xfT[:], bank[7][:], ACT.Copy).then_inc(s_xfT, 1)

            steps(act, [(router_in0, 4), (attended, 3), (norm_in, 1), (queries_keys, 1), (gate, 1), (cross, 2)])

            def gelus(pair, par):
                act.wait_ge(s_hT, pair + 1)
                act.activation(gT[:, par], hT[:, par], ACT.Gelu).then_inc(s_gT, 1)

            gelus(0, 0)
            gelus(1, 1)
            with act.Fori(1, NPAIR // 2) as j:
                for p in range(2):
                    gelus(2 * j + p, p)

            act.wait_ge(s_gsub, 1)
            act.activation(gates[:], gates[:], ACT.Exp).then_inc(s_gexp, 1)

            def project(grp):
                g, p = grp.g, grp.par
                act.wait_ge(s_xaTp, g + 1)
                act.activation(xaT[:], bank[7][:], ACT.Copy).then_inc(s_xaT, 1)
                act.wait_ge(s_ckvp, g + 1)
                act.activation(ckvT[:], bank[4][:], ACT.Copy).then_inc(s_ckv, 1)
                if after(g, 1):
                    act.wait_ge(s_parts, 96 * g)
                act.wait_ge(s_q1p, g + 1)
                act.activation(qkh[:, 0], bank[5][:], ACT.Copy).then_inc(s_qh, 1)

            def project_b(grp):
                g, p = grp.g, grp.par
                act.wait_ge(s_kp, g + 1)
                act.activation(qkh[:, 1], bank[0][:], ACT.Copy).then_inc(s_kh, 1)
                act.wait_ge(s_v1p, g + 1)
                act.activation(V1[:, p, :, :, 0:HD], bank[1][:].rearrange("p (t h d) -> p t h d", t=GT, h=NH), ACT.Copy).then_inc(s_v1, 1)

            def shift_rows(grp, i):
                act.wait_ge(s_mTp, grp.g * ND + i + 1)
                if after(grp.g, 1) or i >= 2:
                    r = (i - 2) % RD
                    act.wait_ge(s_shift[r], 64 * grp.g + (32 * (1 + (i - 2) // RD) if i >= 2 else 0))
                act.activation(mT[:, i % 2, :], bank[7][0:16, 0:P], ACT.Copy).then_inc(s_mT, 1)

            def attend(grp):
                g = grp.g
                for i in range(ND):
                    for n in range(4):
                        act.wait_ge(s_st, (g * ND + i) * 4 + n + 1)
                        act.activation(PT[:, i % 2, n, :], bank[4 + n % 2][:, P:512], ACT.Exp, scale=SCORE_SCALE).then_inc(s_exp, 1)
                    if i + 2 < ND:
                        shift_rows(grp, i + 2)
                    if i % 2:
                        act.wait_ge(s_pv, g * (ND // 2) + i // 2 + 1)
                        act.activation(raw[:], bank[6][:], ACT.Copy).then_inc(s_raw, 1)

            def first_shifts(grp):
                shift_rows(grp, 0)
                shift_rows(grp, 1)

            def wo_in(grp):
                act.wait_ge(s_attTp, grp.g + 1)
                act.activation(attT[:], bank[3][:], ACT.Copy).then_inc(s_attT, 1)

            def router_in(grp):
                act.wait_ge(s_xgTp, grp.g + 1)
                act.activation(xgT[:], bank[5][:], ACT.Copy).then_inc(s_xgT, 1)

            steps(act, [(project, 1), (first_shifts, 2), (project_b, 1), (wo_in, 3), (router_in, 4), (attend, 2)])
            act.wait_ge(s_gsub, 2)
            act.activation(gt1[:], gw1[:], ACT.Exp).then_inc(s_gexp, 1)

            def d_in(t, p):
                act.wait_ge(s_xsTp, NPAIR + t + 1)
                act.activation(xdT[:, p], bank[p][:, 0:P], ACT.Copy).then_inc(s_xsT, 1)

            def d_silu(t, p):
                act.wait_ge(s_h, NPAIR + t + 1)
                act.activation(sg[:, p], bank[2 + p][:, F1:2 * F1], ACT.Silu).then_inc(s_sg, 1)

            def d_out(t, p, q, wait):
                act.wait_ge(s_ydp, t + 1)
                if wait is not None:
                    act.wait_ge(s_yo[q], 16 * (NPAIR // NQ + wait))
                act.activation(yd[:, q], bank[6 + p][:, 0:P], ACT.Copy).then_inc(s_yd, 1)

            def lap_of(lap, wait, left=ND1):
                for q in range(NQ1):
                    t, p = lap * NQ1 + q, q % 2
                    if q + AHEAD < left:
                        d_silu(t + AHEAD, p)
                    if q + AHEAD + 1 < left:
                        d_in(t + AHEAD + 1, 1 - p)
                    d_out(t, p, q, wait)

            d_in(0, 0)
            d_in(1, 1)
            d_silu(0, 0)
            d_in(2, 0)
            d_silu(1, 1)
            lap_of(0, None)
            with act.Fori(1, ND1 // NQ1 - 1) as lap:
                lap_of(lap, lap)
            lap_of(ND1 // NQ1 - 1, ND1 // NQ1 - 1, left=NQ1)

        @block.vector
        def _(dve):
            dve.memset(mhalf[:], -0.5)
            dve.memset(zrow[:], 0.0).then_inc(s_vinit, 1)
            dve.memset(count[:], 0.0)
            dve.memset(countb[:], 0.0).then_inc(s_pinit, 1)
            dve.wait_ge(s_pinit, 1)
            dve.wait_ge(s_const, 16 * NCONST)
            dve.wait_ge(s_x, 16)
            dve.tensor_copy(tri[:], cst[:, 128:256])
            dve.tensor_copy(mask_sb[:], mask_in[:].unsqueeze(2).broadcast_to([P, NL, GT, P // 2]))
            dve.memset(ones[:], 1.0).then_inc(s_tri, 1)
            dve.wait_ge(s_tri, 1)

            def variance(i, link, src):
                stands_alone(dve)
                for t in range(GT):
                    last = dve.bn_stats(st[:, i, t, :], src[:, t, :])
                link(last)
                stands_alone(dve)
                for t in range(GT):
                    last = dve.bn_aggr(mv[:, i, t, :], st[:, i, t, :])
                link(last)
                dve.tensor_scalar(ve[:, i, :], mv[:, i, :, 1], EPS, None, ALU.add).then_inc(s_ve[i], 1)

            def normalize(i, grp, src, dst):
                dve.wait_ge(s_rs[i], grp.g + 1)
                for t in range(GT):
                    last = dve.tensor_scalar(dst[:, t, :], src[:, t, :], mv[:, i, t, 0:1], rs[:, i, t:t + 1],
                                             ALU.subtract, ALU.mult)
                return last

            def layernorm(i, grp, link, src, dst):
                variance(i, link, src)
                return normalize(i, grp, src, dst)

            def norm_stats(grp):
                link = Chain(dve, c_F, grp.g, 2)
                variance(0, link, X[:, bass.ds(grp.g * GT, GT), :])
                link.end()

            def norm(grp):
                g, p = grp.g, grp.par
                if after(g, 2):
                    dve.wait_ge(s_xnb, 2 * (g - 1))
                    dve.wait_ge(s_xnTp, g - 1)
                normalize(0, grp, X[:, bass.ds(g * GT, GT), :], xn[:, p]).then_inc(s_xn, 1)

            def values(grp):
                g, p = grp.g, grp.par
                dve.wait_ge(s_v, g + 1)
                if after(g, 2):
                    dve.wait_ge(s_av, g - 1)
                dve.tensor_tensor(V[:, p], bank[3][:].rearrange("p (t n) -> p t n", t=GT),
                                  bv_b[:].unsqueeze(1).broadcast_to([P, GT, P]), ALU.add).then_inc(s_ve_, 1)

            def diagonal(grp):
                g, p = grp.g, grp.par
                q, k, gg = Q[:, p], K[:, p], G[:, p]
                dve.wait_ge(s_ge, g + 1)
                dve.wait_ge(s_lev, g * NLP + 1)
                dve.tensor_tensor(q, q, gg, ALU.mult).then_inc(s_upd, 1)
                if after(g, 1):
                    dve.wait_ge(s_av, g)
                dve.tensor_tensor(AD[:].rearrange("p (t n) -> p t n", t=GT), bank[6][:].rearrange("p (t n) -> p t n", t=GT),
                                  ident.unsqueeze(1).broadcast_to([P, GT, P]), ALU.mult).then_inc(s_aev, 1)
                dve.wait_ge(s_aev, g * NLP + 1)

            def level(grp, lo, hi):
                g, p = grp.g, grp.par
                link = Chain(dve, c_G, g, NL - 1, first=lo - 1)
                q, k = Q[:, p], K[:, p]
                for lv in range(lo, hi):
                    m = LEVELS[lv - 1]
                    tcur = Tm[lv - 2][:] if lv > 1 else G[:, p]
                    dve.wait_ge(s_lev, g * NLP + lv + 1)
                    if m < 64:
                        t3 = tcur.rearrange("p (c two) -> p c two", two=2)
                        dve.tensor_tensor(blocks(q, m)[:, :, 1], blocks(q, m)[:, :, 1],
                                          t3[:, :, 0:1].broadcast_to([P, GN // m // 2, m]), ALU.mult)
                        dve.tensor_tensor(blocks(k, m)[:, :, 0], blocks(k, m)[:, :, 0],
                                          t3[:, :, 1:2].broadcast_to([P, GN // m // 2, m]), ALU.mult).then_inc(s_upd, 1)
                    else:
                        q4 = q.rearrange("p (b s two m) -> p b s two m", b=GB, s=2, two=2)
                        k4 = k.rearrange("p (b s two m) -> p b s two m", b=GB, s=2, two=2)
                        t4 = tcur.rearrange("p (b s two) -> p b s two", b=GB, s=2)
                        dve.tensor_tensor(q4[:, :, 1, 1], q4[:, :, 1, 1], t4[:, :, 1, 0:1].broadcast_to([P, GB, m]), ALU.mult)
                        dve.tensor_tensor(k4[:, :, 0, 0], k4[:, :, 0, 0], t4[:, :, 0, 1:2].broadcast_to([P, GB, m]), ALU.mult
                                          ).then_inc(s_upd, 1)
                    dve.copy_predicated(blocks(AD[:], m)[:, :, 1], mask_sb[:, lv - 1].rearrange("p t n -> p (t n)").rearrange("p (c m) -> p c m", m=m),
                                        blocks(bank[2 if lv % 2 else 6][:], m)[:, :, 1]).then_inc(s_aev, 1)
                    if m < 64:
                        link(dve.tensor_tensor(Tm[lv - 1][:], t3[:, :, 0], t3[:, :, 1], ALU.mult))
                link.end(min(hi, NL) - 1)

            def post_a(grp):
                g, p = grp.g, grp.par
                link = Chain(dve, c_W, g, 7)
                dve.wait_ge(s_wo, g + 1)
                dve.wait_ge(s_xnb, 2 * (g + 1))
                dve.tensor_tensor(Y[:], bank[4][:].rearrange("p (t n) -> p t n", t=GT), xb[:, p], ALU.add).then_inc(s_y, 1)
                dve.wait_ge(s_y, g + 1)
                variance(1, link, Y[:])
                link.end(2)

            def post_b(grp):
                g, p = grp.g, grp.par
                link = Chain(dve, c_W, g, 7, first=2)
                link(normalize(1, grp, Y[:], Y[:]))
                link(dve.tensor_tensor(Y[:], Y[:], gamma_b[:].unsqueeze(1).broadcast_to([P, GT, P]), ALU.mult))
                xt = X[:, bass.ds(g * GT, GT), :]
                link(dve.tensor_tensor(xt, xt, Y[:], ALU.add))
                variance(2, link, xt)
                link.end(7)

            def post_c(grp):
                g, p = grp.g, grp.par
                if after(g, 2):
                    dve.wait_ge(s_scat[p], 16 * GT * K0 * grp.half)
                normalize(2, grp, X[:, bass.ds(g * GT, GT), :], xf[:, p]).then_inc(s_xf, 1)

            def choose(grp):
                g, p = grp.g, grp.par
                link = Chain(dve, c_H, g, 16)
                dve.wait_ge(s_lg, g + 1)
                link(dve.tensor_tensor(lg[:], bank[7][:, 0:GT * E0].rearrange("p (t e) -> p t e", t=GT),
                                       gb_b[:].unsqueeze(1).broadcast_to([P, GT, E0]), ALU.add))
                stands_alone(dve)
                for t in range(GT):
                    last = dve.max(best[:, t, :], lg[:, t, :])
                link(last)
                dve.tensor_copy(top0[:, bass.ds(g * GT, GT), :], best[:, :, 0:K0])
                for t in range(GT):
                    last = dve.max_index(ix[:, t, :], best[:, t, :], lg[:, t, :])
                link(last)
                link(dve.tensor_copy(ixf[:], ix[:, :, 0:K0]))
                for t in range(GT):
                    last = dve.tensor_tensor(oh[:, t], iota_e.unsqueeze(1).broadcast_to([P, K0, E0]),
                                         ixf[:, t, :].unsqueeze(2).broadcast_to([P, K0, E0]), ALU.is_equal)
                link(last)
                link(dve.tensor_reduce(M[:], oh[:].rearrange("p t k e -> p t e k"), AX.X, ALU.add))
                dve.tensor_copy(Mb[:], M[:]).then_inc(s_M, 1)
                link(dve.tensor_reduce(gcnt[:], M[:].rearrange("p t e -> p e t"), AX.X, ALU.add))
                link.end(7)

            def place(grp):
                g, p = grp.g, grp.par
                link = Chain(dve, c_H, g, 16, first=7)
                dve.wait_ge(s_pos, g + 1)
                for t in range(GT):
                    last = dve.tensor_tensor(ohp[:, t], oh[:, t],
                                     bank[7][:, 256 + t * E0:256 + (t + 1) * E0].unsqueeze(1).broadcast_to([P, K0, E0]), ALU.mult)
                link(last)
                dve.sem_inc(s_posr, 1)
                link(dve.tensor_tensor(count[:], count[:], gcnt[:], ALU.add))
                link(dve.tensor_copy(countb[:, 0, :], count[:]))
                link(dve.tensor_reduce(pos[:], ohp[:], AX.X, ALU.add))
                vg = valid[:, bass.ds(g * GT, GT), :]
                link(dve.tensor_scalar(vg, pos[:], float(CAP), None, ALU.is_lt))
                link(dve.tensor_scalar(r0[:], ixf[:], float(CAP), None, ALU.mult))
                link(dve.scalar_tensor_tensor(r1[:], vg, -float(NSLOT0), r0[:], ALU.mult, ALU.add))
                link(dve.scalar_tensor_tensor(sslot[:, p], pos[:], float(NSLOT0), r1[:], ALU.add, ALU.add))
                link(dve.scalar_tensor_tensor(gslot[:, bass.ds(g * GT, GT), :], pos[:], float(CAP - 1), r0[:], ALU.min, ALU.add))
                dve.sem_inc(s_slot, 1)
                link.end()

            steps(dve, [(diagonal, 2), (lambda grp: level(grp, 1, 2), 2), (choose, 4), (post_a, 3), (lambda grp: level(grp, 2, 4), 2),
                        (place, 4), (post_b, 3), (lambda grp: level(grp, 4, 6), 2), (norm_stats, 0), (post_c, 3),
                        (lambda grp: level(grp, 6, 8), 2), (values, 1), (norm, 0)])

            def tokens_in(pair, i):
                dve.wait_ge(s_xsTp, pair + 1)
                dve.tensor_copy(xsT[:, i % 2], bank[7 * (i % 2)][:, 0:P]).then_inc(s_xsT, 1)

            def hidden(pair, i):
                dve.wait_ge(s_h, pair + 1)
                dve.tensor_copy(hs[:, i % 2], bank[1 + i % 2][:]).then_inc(s_hs, 1)

            def turn(pair, i):
                p = i % 2
                dve.wait_ge(s_hTp, pair + 1)
                dve.tensor_tensor(hT[:, p].rearrange("p c (e s) -> p c e s", e=2),
                                  bank[3 + p][:].rearrange("p (c e s) -> p c e s", c=HC, e=2),
                                  b1T[:, bass.ds(2 * pair, 2), :].rearrange("p e c -> p c e").unsqueeze(3).broadcast_to([P, HC, 2, CAP]),
                                  ALU.add).then_inc(s_hT, 1)

            def outputs(pair, i, lap):
                q = i % NQ
                dve.wait_ge(s_yp, pair + 1)
                if not (isinstance(lap, int) and lap == 0):
                    dve.wait_ge(s_yo[q], 16 * lap)
                dve.tensor_tensor(ys[:, q], bank[5 + i % 2][:, 0:P],
                                  b2_b[:, bass.ds(pair, 1)].rearrange("p o d -> p (o d)"), ALU.add).then_inc(s_ys, 1)

            def pairs(lap, left=NPAIR):
                for i in range(NQ):
                    pair = lap * NQ + i
                    turn(pair, i)
                    if i + AHEAD < left:
                        hidden(pair + AHEAD, i + AHEAD)
                    if i + AHEAD + 1 < left:
                        tokens_in(pair + AHEAD + 1, i + AHEAD + 1)
                    outputs(pair, i, lap)

            dve.wait_ge(s_b1, 48)
            tokens_in(0, 0)
            tokens_in(1, 1)
            hidden(0, 0)
            tokens_in(2, 2)
            hidden(1, 1)
            pairs(0)
            with dve.Fori(1, NPAIR // NQ - 1) as lap:
                pairs(lap)
            pairs(NPAIR // NQ - 1, left=NQ)

            link = Chain(dve, c_T, 0, 8)
            for q in range(NQ):
                dve.wait_ge(s_yo[q], 16 * (NPAIR // NQ))
            dve.memset(onerow[:], 1.0)
            dve.memset(ones8[:], 1.0)
            dve.tensor_copy(identb[:], ident)
            for h in range(2):
                dve.tensor_scalar(maskq[:, h], cst[:, 128:256], MASKED, None, ALU.mult)
            dve.memset(count1[:], 0.0)
            dve.memset(count1b[:], 0.0)
            dve.memset(V1[:], 0.0)
            link(dve.tensor_tensor(Y[:, 0], cst[:, 128:256], ident, ALU.add))
            for h in range(2):
                last = dve.tensor_scalar(maskk[:, h], Y[:, 0], -MASKED, MASKED, ALU.mult, ALU.add)
            link(last)
            link(dve.memset(V1[:, :, :, :, HD:HD + 1], 1.0))
            dve.sem_inc(s_pre, 1)
            link(dve.tensor_tensor(gates[:], top0[:], top0[:, :, 0:1].broadcast_to([P, NT, K0]), ALU.subtract))
            dve.sem_inc(s_gsub, 1)
            dve.wait_ge(s_gexp, 1)
            link(dve.tensor_reduce(gsum[:], gates[:], AX.X, ALU.add))
            link(dve.reciprocal(gsum[:], gsum[:]))
            link(dve.tensor_tensor(gates[:], gates[:], gsum[:].unsqueeze(2).broadcast_to([P, NT, K0]), ALU.mult))
            link(dve.tensor_tensor(gates[:], gates[:], valid[:], ALU.mult))
            link.end()
            dve.wait_ge(s_w2c, 16 * 15)

            def combine(grp):
                g, p = grp.g, grp.par
                link = Chain(dve, c_C, g, 5)
                dve.wait_ge(s_gat[p], 16 * GT * K0 * (grp.half + 1))
                for k in range(K0):
                    for t in range(GT):
                        xt = X[:, bass.ds(g * GT + t, 1), :].rearrange("p o d -> p (o d)")
                        gate = gates[:, bass.ds(g * GT + t, 1), k:k + 1].rearrange("p o k -> p (o k)")
                        last = dve.scalar_tensor_tensor(xt, R[:, p, t * K0 + k, :], gate, xt, ALU.mult, ALU.add)
                    link(last)
                dve.sem_inc(s_radd, 1)
                if after(g, 1):
                    dve.wait_ge(s_xaTp, g)
                layernorm(3, grp, link, X[:, bass.ds(g * GT, GT), :], xa[:]).then_inc(s_xa, 1)
                link.end()

            def rotate(grp, side, bk, src_sem, out_sem, link):
                g = grp.g
                dve.wait_ge(src_sem, g + 1)
                for h in range(2):
                    last = dve.tensor_tensor(rt[:, h].rearrange("p (b t) -> p b t", b=GB),
                                      bank[bk][h * DR:(h + 1) * DR, :].rearrange("p (b t) -> p b t", b=GB),
                                      rope_sb[h * DR:(h + 1) * DR, :].unsqueeze(1).broadcast_to([DR, GB, T]), ALU.mult)
                link(last)
                link(dve.tensor_tensor(rt[:, 0], rt[:, 0], rt[:, 1], ALU.add))
                for r in ((0, 1), (0, 2))[side]:
                    last = dve.tensor_copy(rp[r * DR:(r + 1) * DR, side], rt[:, 0])
                link(last)
                r = (2, 1)[side]
                link(dve.tensor_tensor(rp[r * DR:(r + 1) * DR, side], rt[:, 0], rp[0:DR, side].bitcast(F32), ALU.subtract))
                dve.sem_inc(out_sem, 1)

            def project(grp):
                g = grp.g
                link = Chain(dve, c_N, g, 8)
                dve.wait_ge(s_qh, g + 1)
                dve.tensor_tensor(qkl[:, 0], bank[5][:], qkh[:, 0].bitcast(F32), ALU.subtract).then_inc(s_ql, 1)
                if after(g, 1):
                    for r in range(RD):
                        dve.wait_ge(s_fill[r], 96 * g - 32)
                rotate(grp, 0, 6, s_qr, s_rq, link)
                dve.wait_ge(s_kh, g + 1)
                dve.tensor_tensor(qkl[:, 1], bank[0][:], qkh[:, 1].bitcast(F32), ALU.subtract).then_inc(s_kl, 1)
                rotate(grp, 1, 2, s_kr, s_rk, link)
                link.end()

            def maxima(grp, i):
                u = grp.g * ND + i
                m = mx[:, i % 2]
                for h in range(2):
                    dve.wait_ge(s_max, u * 2 + h + 1)
                    for c, lo, hi in ((0, P, 2 * P), (1, 2 * P, 4 * P)):
                        last = dve.tensor_reduce(m[:, h, :, c], pairbank[h][:].rearrange("p (b n) -> p b n", b=GB)[:, :, lo:hi], AX.X, ALU.max)
                    last.then_inc(s_maxr, 1)
                dve.wait_ge(s_maxr, u * 2 + 2)
                mm = m.rearrange("p h b c -> p (h b c)")
                dve.tensor_scalar(ms[:, i % 2, 0:8], mm, -1.0, None, ALU.mult).then_inc(s_ms, 1)
                dve.wait_ge(s_ms, 2 * u + 1)
                dve.scalar_tensor_tensor(ms[:, i % 2, 8:16], mm, -1.0, ms[:, i % 2, 0:8].bitcast(F32), ALU.mult, ALU.subtract).then_inc(s_ms, 1)

            def first_maxima(grp):
                maxima(grp, 0)
                maxima(grp, 1)

            def attend(grp):
                g = grp.g
                for i in range(ND):
                    if i + 2 < ND:
                        maxima(grp, i + 2)
                    if i % 2:
                        n = g * (ND // 2) + i // 2
                        dve.wait_ge(s_rawTp, n + 1)
                        if i == 1 and after(g, 1):
                            dve.wait_ge(s_attTp, g)
                        v5 = bank[7][:].rearrange("p (u c h b d) -> p u c h b d", u=2, c=2, h=2, b=2)
                        dve.reciprocal(rec[:], bank[7][:].rearrange("p (u j d) -> p u j d", u=4, j=4)[:, :, :, HD]).then_inc(s_norm, 1)
                        dve.wait_ge(s_norm, 2 * n + 1)
                        r5 = rec[:].rearrange("p (u c) (h b) -> p u c h b", u=2, h=2)
                        for c in range(2):
                            for b in range(2):
                                h0 = 4 * (i // 2) * HD
                                last = dve.tensor_tensor(
                                    att[:, 2 * b + c, h0:h0 + 4 * HD].rearrange("p (u h d) -> p u h d", u=2, h=2),
                                    v5[:, :, c, :, b, 0:HD], r5[:, :, c, :, b].unsqueeze(3).broadcast_to([P, 2, 2, HD]), ALU.mult)
                        last.then_inc(s_norm, 1)

            def wo_out(grp):
                g, p = grp.g, grp.par
                link = Chain(dve, c_R, g, 3)
                dve.wait_ge(s_wo1, g + 1)
                xt = X[:, bass.ds(g * GT, GT), :]
                link(dve.tensor_tensor(xt, xt, bank[4][:].rearrange("p (t n) -> p t n", t=GT), ALU.add))
                dve.sem_inc(s_x3, 1)
                if after(g, 2):
                    dve.wait_ge(s_scat1[p], 16 * GT * K1 * grp.half)
                layernorm(4, grp, link, xt, xg[:, p]).then_inc(s_xg, 1)
                link.end()

            def route(grp):
                g, p = grp.g, grp.par
                link = Chain(dve, c_Q, g, 11)
                dve.wait_ge(s_lg1, g + 1)
                link(dve.tensor_copy(lg1[:], bank[6][:, 0:GT * E1].rearrange("p (t e) -> p t e", t=GT)))
                stands_alone(dve)
                for t in range(GT):
                    last = dve.max(best1[:, t, :], lg1[:, t, :])
                link(last)
                dve.tensor_copy(gt1[:, bass.ds(g * GT, GT), :], best1[:, :, 0:K1])
                for t in range(GT):
                    last = dve.max_index(ix1[:, t, :], best1[:, t, :], lg1[:, t, :])
                link(last)
                ixg, posg = ixa[:, bass.ds(g * GT, GT), :], posa[:, bass.ds(g * GT, GT), :]
                link(dve.tensor_copy(ixg, ix1[:, :, 0:K1]))
                for t in range(GT):
                    last = dve.tensor_tensor(oh1[:, t], iota_e[:, 0:E1].unsqueeze(1).broadcast_to([P, K1, E1]),
                                         ixa[:, bass.ds(g * GT + t, 1), :].rearrange("p o k -> p (o k)").unsqueeze(2).broadcast_to([P, K1, E1]), ALU.is_equal)
                link(last)
                dve.tensor_tensor(M1b[:], oh1[:, :, 0], oh1[:, :, 1], ALU.add).then_inc(s_M1, 1)
                link(dve.tensor_reduce(gcnt1[:], oh1[:].rearrange("p t k e -> p e (t k)"), AX.X, ALU.add))
                dve.wait_ge(s_pos1, g + 1)
                for t in range(GT):
                    last = dve.tensor_tensor(ohp1[:, t], oh1[:, t], bank[6][:, 256 + t * E1:256 + (t + 1) * E1].unsqueeze(1).broadcast_to([P, K1, E1]), ALU.mult)
                link(last)
                link(dve.tensor_tensor(count1[:], count1[:], gcnt1[:], ALU.add))
                link(dve.tensor_copy(count1b[:], count1[:]))
                link(dve.tensor_reduce(posg, ohp1[:], AX.X, ALU.add))
                if after(g, 2):
                    dve.wait_ge(s_scat1[p], 16 * GT * K1 * grp.half)
                link(dve.scalar_tensor_tensor(srow1[:, p], ixg, float(REG), posg, ALU.mult, ALU.add))
                dve.sem_inc(s_row1, 1)
                link.end()

            steps(dve, [(first_maxima, 2), (project, 1), (wo_out, 3), (route, 4), (attend, 2), (combine, 0)])

            link = Chain(dve, c_T, 0, 33, base=8)
            link(dve.tensor_tensor(gw1[:], gt1[:], gt1[:, :, 0:1].broadcast_to([P, NT, K1]), ALU.subtract))
            dve.sem_inc(s_gsub, 1)
            dve.wait_ge(s_tot, 1)
            link(dve.tensor_copy(ntile[:], bank[0][:, 0:E1]))
            link(dve.tensor_tensor(cmp1[:], ntile[:].unsqueeze(2).broadcast_to([P, E1, NT]),
                                   iota128.unsqueeze(1).broadcast_to([P, E1, NT]), ALU.is_gt))
            link(dve.tensor_reduce(ntile[:], cmp1[:], AX.X, ALU.add))
            link(dve.tensor_tensor_scan(tend[:], ones8[:], ntile[:], 0.0, ALU.mult, ALU.add))
            link(dve.tensor_tensor(tbase[:], tend[:], ntile[:], ALU.subtract))
            link(dve.tensor_scalar(tbase[:], tbase[:], float(P), None, ALU.mult))
            link(dve.tensor_scalar(tw[:], ntile[:], -float(P), float(REG), ALU.mult, ALU.add))
            link(dve.tensor_tensor(cmp2[:], tend[:].unsqueeze(1).broadcast_to([P, ND1, E1]),
                                   iota_t.unsqueeze(2).broadcast_to([P, ND1, E1]), ALU.is_le))
            link(dve.tensor_tensor(cmp3[:], cmp2[:], tw[:].unsqueeze(1).broadcast_to([P, ND1, E1]), ALU.mult))
            dve.tensor_reduce(tl[:, 0], cmp2[:], AX.X, ALU.add)
            link(dve.tensor_reduce(tl[:, 1], cmp3[:], AX.X, ALU.add))
            link(dve.scalar_tensor_tensor(tl[:, 1], iota_t, float(P), tl[:, 1], ALU.mult, ALU.add))
            dve.tensor_scalar(tli[:, 0], tl[:, 0], float(E1 - 1), None, ALU.min)
            link(dve.tensor_scalar(tli[:, 1], tl[:, 1], float(E1 * REG - P), None, ALU.min))
            dve.sem_inc(s_tiles, 1)
            tmp = gw1
            dve.wait_ge(s_gexp, 2)
            for e in range(E1):
                link(dve.tensor_scalar(tmp[:], ixa[:], float(e), tbase[:, e:e + 1], ALU.is_equal, ALU.mult))
                link(dve.tensor_tensor(posa[:], posa[:], tmp[:], ALU.add))
            link(dve.tensor_copy(grow1[:], posa[:]))
            link(dve.tensor_tensor(gsum[:], gt1[:, :, 0], gt1[:, :, 1], ALU.add))
            link(dve.reciprocal(gsum[:], gsum[:]))
            link(dve.tensor_tensor(gw1[:], gt1[:], gsum[:].unsqueeze(2).broadcast_to([P, NT, K1]), ALU.mult))
            dve.sem_inc(s_tiles, 1)
            link.end()

            def d_act(t, p):
                dve.wait_ge(s_sg, t + 1)
                dve.tensor_tensor(ac[:, p], bank[2 + p][:, 0:F1], sg[:, p], ALU.mult).then_inc(s_ac, 1)

            def d_turn(t, p):
                dve.wait_ge(s_acTp, t + 1)
                dve.tensor_copy(acT[:, p], bank[4 + p][:, 0:F1]).then_inc(s_acT, 1)

            def lap_of(lap, left=ND1):
                for q in range(NQ1):
                    d_turn(lap * NQ1 + q, q % 2)
                    if q + AHEAD < left:
                        d_act(lap * NQ1 + q + AHEAD, q % 2)

            d_act(0, 0)
            d_act(1, 1)
            with dve.Fori(0, ND1 // NQ1 - 1) as lap:
                lap_of(lap)
            lap_of(ND1 // NQ1 - 1, left=NQ1)

            def final(g, p, half):
                dve.wait_ge(s_gat[p], 16 * GT * (K0 * (NG // 2) + K1 * (half + 1)))
                for k in range(K1):
                    for t in range(GT):
                        xt = X[:, bass.ds(g * GT + t, 1), :].rearrange("p o d -> p (o d)")
                        gate = gw1[:, bass.ds(g * GT + t, 1), k:k + 1].rearrange("p o k -> p (o k)")
                        last = dve.scalar_tensor_tensor(xt, R[:, p, t * K1 + k, :], gate, xt, ALU.mult, ALU.add)
                    if k < K1 - 1:
                        last.then_inc(s_fin1, 1)
                        dve.wait_ge(s_fin1, g + 1)
                last.then_inc(s_fin, 1)

            with dve.Fori(0, NG // 2) as j:
                for p in range(2):
                    final(2 * j + p, p, j)

        @block.tensor
        def _(pe):
            pe.wait_ge(s_const, 16 * NCONST)
            pe.wait_ge(s_tri, 1)



            def norm_in(grp):
                g, p = grp.g, grp.par
                pe.wait_ge(s_xn, g + 1)
                if after(g, 1):
                    pe.wait_ge(s_qe, g)
                for t in range(GT):
                    last = pe.transpose(bank[0][:, t * P:(t + 1) * P], xn[:, p, t, :], ident)
                last.then_inc(s_xnTp, 1)

            def queries_keys(grp):
                g = grp.g
                pe.wait_ge(s_xnT, g + 1)
                if after(g, 1):
                    pe.wait_ge(s_ge, g)
                pe.matmul(bank[1][:], wq_sb[:], xnT[:], start=True, stop=True).then_inc(s_q, 1)
                pe.matmul(bank[0][:], wk_sb[:], xnT[:], start=True, stop=True).then_inc(s_k, 1)

            def state_values(grp):
                if after(grp.g, 1):
                    pe.wait_ge(s_ve_, grp.g)
                for t in range(GT):
                    last = pe.matmul(bank[3][:, t * P:(t + 1) * P], xnT[:, t * P:(t + 1) * P], wv_sb[:], start=True, stop=True)
                last.then_inc(s_v, 1)

            def gate(grp):
                pe.wait_ge(s_qe, grp.g + 1)
                pe.matmul(bank[1][:], wg_sb[:], xnT[:], start=True, stop=True).then_inc(s_g, 1)

            def level(grp, lo, hi):
                g, p = grp.g, grp.par
                for lv in range(lo, hi):
                    if lv == 0:
                        pe.wait_ge(s_ge, g + 1)
                    else:
                        pe.wait_ge(s_upd, g * NLP + lv)
                    if lv >= 2:
                        pe.wait_ge(s_aev, g * NLP + lv - 1)
                    for t in range(GT):
                        last = pe.matmul(bank[2 if lv % 2 else 6][:, t * P:(t + 1) * P], K[:, p, t * P:(t + 1) * P],
                                         Q[:, p, t * P:(t + 1) * P], start=True, stop=True)
                    last.then_inc(s_lev, 1)

            def cross(grp):
                g, p = grp.g, grp.par
                pe.wait_ge(s_upd, (g + 1) * NLP)
                if after(g, 1):
                    pe.wait_ge(s_y, g)
                for b in range(GB):
                    last = pe.matmul(bank[4][:, b * P:(b + 1) * P], K[:, p, 2 * b * P:(2 * b + 1) * P],
                                     Q[:, p, (2 * b + 1) * P:(2 * b + 2) * P], start=True, stop=True)
                last.then_inc(s_cross, 1)

            def attended(grp):
                g, p = grp.g, grp.par
                pe.wait_ge(s_ve_, g + 1)
                pe.wait_ge(s_axt, g + 1)
                pe.wait_ge(s_aev, (g + 1) * NLP)
                for b in range(GB):
                    v0, v1 = V[:, p, 2 * b], V[:, p, 2 * b + 1]
                    o0, o1 = (bank[5][:, (2 * b + s) * P:(2 * b + s + 1) * P] for s in range(2))
                    pe.matmul(o0, v0, AD[:, 2 * b * P:(2 * b + 1) * P], start=True, stop=True)
                    pe.matmul(o1, v0, AXT[:, b], start=True, stop=False)
                    last = pe.matmul(o1, v1, AD[:, (2 * b + 1) * P:(2 * b + 2) * P], start=False, stop=True)
                last.then_inc(s_av, 1)

            def output(grp):
                pe.wait_ge(s_ot, grp.g + 1)
                for t in range(GT):
                    last = pe.matmul(bank[4][:, t * P:(t + 1) * P], OT[:, t * P:(t + 1) * P], wo_sb[:], start=True, stop=True)
                last.then_inc(s_wo, 1)

            def router_in0(grp):
                g, p = grp.g, grp.par
                pe.wait_ge(s_xf, g + 1)
                if after(g, 1):
                    pe.wait_ge(s_posr, g)
                for t in range(GT):
                    last = pe.transpose(bank[7][:, t * P:(t + 1) * P], xf[:, p, t, :], ident)
                last.then_inc(s_xfTp, 1)

            def logits0(grp):
                pe.wait_ge(s_xfT, grp.g + 1)
                for t in range(GT):
                    last = pe.matmul(bank[7][:, t * E0:(t + 1) * E0], xfT[:, t * P:(t + 1) * P], gw_sb[:], start=True, stop=True)
                last.then_inc(s_lg, 1)

            def earlier0(grp):
                g = grp.g
                pe.wait_ge(s_M, g + 1)
                if after(g, 1):
                    pe.wait_ge(s_slot, g)
                for t in range(GT):
                    dst = bank[7][:, 256 + t * E0:256 + (t + 1) * E0]
                    pe.matmul(dst, tri[:], Mb[:, t], start=True, stop=False)
                    for u in range(t):
                        pe.matmul(dst, ones[:], Mb[:, u], start=False, stop=False)
                    last = pe.matmul(dst, ones[:], countb[:, 0], start=False, stop=True)
                last.then_inc(s_pos, 1)

            def lev(lo, hi):
                return lambda grp: level(grp, lo, hi), 2

            steps(pe, [(router_in0, 4), (attended, 3), lev(0, 1), (logits0, 4), (norm_in, 1), (output, 3), lev(1, 2),
                       (queries_keys, 1), lev(2, 3), (earlier0, 4), lev(3, 4), (state_values, 1), lev(4, 5), (gate, 1),
                       lev(5, 8), (cross, 2)])

            def tokens_in(pair, i, lap):
                p, q = i % 2, i % NQ
                pe.wait_ge(s_xs[q], 16 * (lap * (PAIRS // NQ) + i // NQ + 1))
                pe.transpose(bank[7 * p][:, 0:P], xs[:, q, :], ident).then_inc(s_xsTp, 1)

            def hidden(pair, i, lap):
                p = i % 2
                pe.wait_ge(s_w[i], 32 * (lap + 1))
                pe.wait_ge(s_xsT, pair + 1)
                for h in range(2):
                    last = pe.matmul(bank[1 + p][h * CAP:(h + 1) * CAP, :], xsT[:, p, h * CAP:(h + 1) * CAP],
                                     w1r[:, 2 * i + h, :], start=True, stop=True)
                last.then_inc(s_h, 1)

            def turn(pair, i):
                p = i % 2
                pe.wait_ge(s_hs, pair + 1)
                for c in range(HC):
                    last = pe.transpose(bank[3 + p][:, c * P:(c + 1) * P], hs[:, p, c * P:(c + 1) * P], ident)
                last.then_inc(s_hTp, 1)

            def outputs(pair, i, first=False):
                p = i % 2
                pe.wait_ge(s_gT, pair + 1)
                if not first:
                    pe.wait_ge(s_ys, pair - 1)
                for h in range(2):
                    for c in range(HC):
                        last = pe.matmul(bank[5 + p][h * CAP:(h + 1) * CAP, 0:P], gT[:, p, c, h * CAP:(h + 1) * CAP],
                                         w2r[:, 2 * i + h, c, :], start=(c == 0), stop=(c == HC - 1))
                last.then_inc(s_yp, 1)

            def ahead(lap, i, n):
                return (i + n) % PAIRS, lap + (i + n) // PAIRS

            def pairs(lap, last_lap=False, first_lap=False):
                for i in range(PAIRS):
                    pair = lap * PAIRS + i
                    turn(pair, i)
                    if not (last_lap and i + AHEAD >= PAIRS):
                        hidden(pair + AHEAD, *ahead(lap, i, AHEAD))
                    if not (last_lap and i + AHEAD + 1 >= PAIRS):
                        tokens_in(pair + AHEAD + 1, *ahead(lap, i, AHEAD + 1))
                    outputs(pair, i, first_lap and i < 2)

            tokens_in(0, 0, 0)
            tokens_in(1, 1, 0)
            hidden(0, 0, 0)
            tokens_in(2, 2, 0)
            hidden(1, 1, 0)
            pairs(0, first_lap=True)
            with pe.Fori(1, NROUND - 1) as lap:
                pairs(lap)
            pairs(NROUND - 1, last_lap=True)

            pe.wait_ge(s_w2c, 16 * 15)
            pe.wait_ge(s_pre, 1)
            pe.wait_ge(s_ones1, 32)

            def project_a(grp):
                g = grp.g
                pe.wait_ge(s_xa, g + 1)
                if after(g, 2):
                    pe.wait_ge(s_norm, 2 * (ND // 2) * (g - 1))
                for t in range(GT):
                    last = pe.transpose(bank[7][:, t * P:(t + 1) * P], xa[:, t, :], ident)
                last.then_inc(s_xaTp, 1)
                pe.wait_ge(s_xaT, g + 1)
                pe.matmul(bank[4][:], wkvd_sb[:], xaT[:], start=True, stop=True).then_inc(s_ckvp, 1)
                pe.matmul(bank[5][:], wq1_sb[:], xaT[:], start=True, stop=True).then_inc(s_q1p, 1)
                pe.matmul(bank[6][0:2 * DR, :], wqr_sb[:], xaT[:], start=True, stop=True).then_inc(s_qr, 1)

            def project_b(grp):
                g = grp.g
                pe.wait_ge(s_ckv, g + 1)
                if after(g, 1):
                    pe.wait_ge(s_maxr, 2 * ND * (g - 1) + 4)
                pe.matmul(bank[0][:], wku_sb[:], ckvT[:], start=True, stop=True).then_inc(s_kp, 1)
                for t in range(GT):
                    last = pe.matmul(bank[1][:, t * P:(t + 1) * P], ckvT[:, t * P:(t + 1) * P], wvu_sb[:], start=True, stop=True)
                last.then_inc(s_v1p, 1)
                pe.matmul(bank[2][0:2 * DR, :], wkr_sb[:], ckvT[:], start=True, stop=True).then_inc(s_kr, 1)

            def max_scores(grp, i):
                g, r = grp.g, i % RD
                u = g * ND + i
                pe.wait_ge(s_fill[r], 96 * g + (64 if i < RD else 96))
                for h in range(2):
                    if i >= 1 or after(g, 1):
                        pe.wait_ge(s_maxr, 2 * u + h - 1)
                    for b in range(GB):
                        bk = bank[2 * h + b]
                        keys = SK[0:KM, 2 * r + h, :].rearrange("p (b c n) -> p b c n", b=GB, c=2)[:, b, ::-1, :]
                        for c in range(2):
                            n0 = (2 * b + c) * P
                            pe.matmul(bk[:, c * 2 * P:(c + 1) * 2 * P], SQ[0:KM, 2 * r + h, n0:n0 + P], keys,
                                      start=(c == 0), stop=False, skip_group_check=True)
                        last = pe.matmul(bk[:, P:3 * P], identb[:], maskq[:].rearrange("p a b -> p (a b)"), start=False, stop=True,
                                         skip_group_check=True)
                    last.then_inc(s_max, 1)

            def turn_maxima(grp, i):
                g = grp.g
                u = g * ND + i
                pe.wait_ge(s_ms, 2 * u + 2)
                if i >= 1:
                    pe.wait_ge(s_mT, u)
                elif after(g, 1):
                    pe.wait_ge(s_norm, 2 * (ND // 2) * g)
                if i >= 4:
                    pe.wait_ge(s_norm, 2 * (g * (ND // 2) + (i - 2) // 2))
                pe.transpose(bank[7][0:16, 0:P], ms[:, i % 2, :].bitcast(F32), ident).then_inc(s_mTp, 1)

            def scores(grp, i, n):
                g, r = grp.g, i % RD
                h, b = n // 2, n % 2
                k = (g * ND + i) * 4 + n
                if n >= 2 or i >= 1 or after(g, 1):
                    pe.wait_ge(s_exp, k - 1)
                if n == 0:
                    pe.wait_ge(s_shift[r], 64 * g + (32 if i < RD else 64))
                bk = bank[4 + n % 2]
                q = SQ[0:KS, 2 * r + h, b * T:(b + 1) * T]
                k1, k0 = (SK[0:KS, 2 * r + h, b * T + c * P:b * T + (c + 1) * P] for c in (1, 0))
                pe.matmul(bk[:, 0:2 * P], k1, q, start=True, stop=False, skip_group_check=True)
                pe.matmul(bk[:, 2 * P:4 * P], k0, q, start=False, stop=False, skip_group_check=True)
                last = pe.matmul(bk[:, P:3 * P], identb[:], maskk[:].rearrange("p a b -> p (a b)"), start=False, stop=True, skip_group_check=True)
                last.then_inc(s_st, 1)

            def values(grp, i):
                g, p = grp.g, grp.par
                pe.wait_ge(s_exp, (g * ND + i + 1) * 4)
                if i % 2 == 0 and (i or after(g, 1)):
                    pe.wait_ge(s_raw, g * (ND // 2) + i // 2)
                c0 = (i % 2) * T
                for n in range(4):
                    h, b = n // 2, n % 2
                    pe.matmul(bank[6][32 * n:32 * n + 32, c0:c0 + T], V1[:, p, 2 * b, 2 * i + h, :], PT[:, i % 2, n, P:3 * P],
                              start=True, stop=False, tile_position=(0, 32 * n), skip_group_check=True)
                for n in range(4):
                    h, b = n // 2, n % 2
                    last = pe.matmul(bank[6][32 * n:32 * n + 32, c0 + P:c0 + T], V1[:, p, 2 * b + 1, 2 * i + h, :], PT[:, i % 2, n, 0:P],
                              start=False, stop=True, tile_position=(0, 32 * n), skip_group_check=True)
                if i % 2:
                    last.then_inc(s_pv, 1)

            def turn_values(grp, i):
                g = grp.g
                pe.wait_ge(s_raw, g * (ND // 2) + i // 2 + 1)
                pe.wait_ge(s_mT, g * ND + min(i + 3, ND))
                if i >= 3:
                    pe.wait_ge(s_norm, 2 * (g * (ND // 2) + i // 2))
                for c in range(4):
                    last = pe.transpose(bank[7][:, c * P:(c + 1) * P], raw[:, c * P:(c + 1) * P], ident)
                last.then_inc(s_rawTp, 1)

            def start_duos(grp):
                if not after(grp.g, 1):
                    for s_own in (s_kl, s_v1, s_rk):
                        pe.wait_ge(s_own, grp.g + 1)
                max_scores(grp, 0)
                max_scores(grp, 1)

            def first_turns(grp):
                turn_maxima(grp, 0)
                turn_maxima(grp, 1)

            def attend(grp):
                g = grp.g
                if within(g, NG - 1):
                    for s_next in (s_kl, s_v1, s_rk, s_ql, s_rq):
                        pe.wait_ge(s_next, g + 2)
                else:
                    pe.wait_ge(s_v1, g + 1)
                if after(g, 1):
                    pe.wait_ge(s_x3, g)
                if after(g, 2):
                    pe.wait_ge(s_row1, g - 1)
                for i in range(ND):
                    scores(grp, i, 0)
                    scores(grp, i, 1)
                    if i + 2 < ND:
                        max_scores(grp, i + 2)
                    scores(grp, i, 2)
                    scores(grp, i, 3)
                    values(grp, i)
                    if i + 2 < ND:
                        turn_maxima(grp, i + 2)
                    if i % 2:
                        turn_values(grp, i)

            def wo(grp):
                g = grp.g
                pe.wait_ge(s_norm, 2 * (g + 1) * (ND // 2))
                pe.wait_ge(s_maxr, wo_maxima(g))
                for t in range(GT):
                    last = pe.transpose(bank[3][:, t * P:(t + 1) * P], att[:, t, :], ident)
                last.then_inc(s_attTp, 1)
                pe.wait_ge(s_attT, g + 1)
                for t in range(GT):
                    last = pe.matmul(bank[4][:, t * P:(t + 1) * P], attT[:, t * P:(t + 1) * P], wo1_sb[:], start=True, stop=True)
                last.then_inc(s_wo1, 1)

            def wo_maxima(g):
                return 2 * ND * (g + 1) + 4 if within(g, NG - 1) else 2 * ND * NG

            def route(grp):
                g, p = grp.g, grp.par
                pe.wait_ge(s_xg, g + 1)
                ahead = g + 4 if within(g, NG - 3) else NG
                pe.wait_ge(s_ql, ahead)
                pe.wait_ge(s_rq, ahead)
                if after(g, 1):
                    pe.wait_ge(s_row1, g)
                for t in range(GT):
                    last = pe.transpose(bank[5][:, t * P:(t + 1) * P], xg[:, p, t, :], ident)
                last.then_inc(s_xgTp, 1)
                pe.wait_ge(s_xgT, g + 1)
                for t in range(GT):
                    last = pe.matmul(bank[6][:, t * E1:(t + 1) * E1], xgT[:, t * P:(t + 1) * P], wr_sb[:], start=True, stop=True)
                last.then_inc(s_lg1, 1)
                pe.wait_ge(s_M1, g + 1)
                for t in range(GT):
                    dst = bank[6][:, 256 + t * E1:256 + (t + 1) * E1]
                    pe.matmul(dst, tri[:], M1b[:, t], start=True, stop=False)
                    for u in range(t):
                        pe.matmul(dst, ones[:], M1b[:, u], start=False, stop=False)
                    last = pe.matmul(dst, ones[:], count1b[:], start=False, stop=True)
                last.then_inc(s_pos1, 1)

            steps(pe, [(start_duos, 2), (project_a, 1), (first_turns, 2), (project_b, 1), (wo, 3), (route, 4), (attend, 2)])

            pe.wait_ge(s_row1, NG)
            pe.matmul(bank[0][:, 0:E1], ones[:], count1b[:], start=True, stop=True).then_inc(s_tot, 1)

            pe.wait_ge(s_w2c, 16 * 15)
            pe.wait_ge(s_tiles, 1)

            def d_in(t, q, lap):
                p = q % 2
                pe.wait_ge(s_xs[q], 16 * (NPAIR // NQ + lap + 1))
                pe.transpose(bank[p][:, 0:P], xd[:, q, :], ident).then_inc(s_xsTp, 1)

            def d_hidden(t, p, e):
                pe.wait_ge(s_xsT, NPAIR + t + 1)
                pe.matmul(bank[2 + p][:], xdT[:, p], w1d[:, bass.ds(e, 1), :].rearrange("p o n -> p (o n)"), start=True, stop=True
                          ).then_inc(s_h, 1)

            def d_turn(t, p):
                pe.wait_ge(s_ac, t + 1)
                for c in range(2):
                    last = pe.transpose(bank[4 + p][:, c * P:(c + 1) * P], ac[:, p, c * P:(c + 1) * P], ident)
                last.then_inc(s_acTp, 1)

            def d_out(t, p, e, first):
                pe.wait_ge(s_acT, t + 1)
                if not first:
                    pe.wait_ge(s_yd, t - 1)
                for c in range(2):
                    last = pe.matmul(bank[6 + p][:, 0:P], acT[:, p, c * P:(c + 1) * P],
                                     w2d[:, bass.ds(e, 1), c, :].rearrange("p o n -> p (o n)"), start=(c == 0), stop=(c == 1))
                last.then_inc(s_ydp, 1)

            def expert(t):
                return pe.value_load(tli[0:1, 0, bass.ds(t, 1)], min_val=0, max_val=E1 - 1)

            def lap_of(lap, first=False, left=ND1):
                base = lap * LAP1
                experts = [expert(base + q) for q in range(AHEAD + 1)]
                for q in range(LAP1):
                    t, p = base + q, q % 2
                    d_turn(t, p)
                    if q + AHEAD < left:
                        d_hidden(t + AHEAD, p, experts[q + AHEAD])
                    if q + AHEAD + 1 < left:
                        d_in(t + AHEAD + 1, (q + AHEAD + 1) % NQ1, lap * (LAP1 // NQ1) + (q + AHEAD + 1) // NQ1)
                        if q + 1 < LAP1:
                            experts.append(expert(t + AHEAD + 1))
                    d_out(t, p, experts[q], first and q < 2)

            d_in(0, 0, 0)
            d_in(1, 1, 0)
            d_hidden(0, 0, expert(0))
            d_in(2, 2, 0)
            d_hidden(1, 1, expert(1))
            lap_of(0, first=True)
            with pe.Fori(1, ND1 // LAP1 - 1) as lap:
                lap_of(lap)
            lap_of(ND1 // LAP1 - 1, left=LAP1)


def constants():
    cst = np.zeros((P, 2 * P + E0 + ND1 + NT), np.float32)
    cst[:, 0:P] = np.eye(P)
    cst[:, P:2 * P] = np.triu(np.ones((P, P)), 1)
    cst[:, 2 * P:2 * P + E0] = np.arange(E0)
    cst[:, 2 * P + E0:2 * P + E0 + ND1] = np.arange(ND1)
    cst[:, 2 * P + E0 + ND1:] = np.arange(NT) * P
    masks = np.zeros((P, NL, P // 2), np.float32)
    for level, m in enumerate(LEVELS):
        j = np.arange(P)[:, None]
        i = np.array([i for i in range(P) if i // m % 2 == 1])[None]
        masks[:, level] = (j // m % 2 == 0) & (i // m == j // m + 1)
    inv = (1.0 / 10000.0 ** (np.arange(0, DR, 2, dtype=np.float32) / np.float32(DR))).astype(np.float32)
    angle = np.outer(np.arange(T, dtype=np.float32), inv).astype(np.float32)
    cos, sin = np.cos(angle).T, np.sin(angle).T
    rope = np.ascontiguousarray(np.concatenate([cos, cos, -sin, sin], 0).astype(np.float32))
    return {"const": cst, "masks": masks.reshape(P, -1), "rope": rope}


def layout(a):
    def by_dim(w):
        return w.reshape(P, NH, HD).transpose(0, 2, 1).reshape(P, NH * HD)

    out = {"x": a["L0_attn_x"].reshape(NTOK, P)}
    for n in ("Wq", "bq", "Wk", "bk", "Wv", "bv", "Wg", "bg", "Wo", "bo", "gamma", "beta"):
        out[n] = a["L0_attn_" + n]
    for n in ("gate_w", "gate_b", "w1", "w2", "b2"):
        out[n] = a["L0_ffn_" + n]
    out["b1t"] = a["L0_ffn_b1"].reshape(E0, HC, P).transpose(2, 0, 1).reshape(P, E0 * HC)
    out["Wkvd"] = a["L1_attn_W_kv_down"]
    out["Wku"] = by_dim(a["L1_attn_W_k_up"])
    out["Wvu"] = a["L1_attn_W_v_up"]
    out["Wq1"] = by_dim(a["L1_attn_W_q"])
    out["Wqr"] = a["L1_attn_W_q_rope"]
    out["Wkr"] = a["L1_attn_W_k_rope"]
    out["Wo1"] = a["L1_attn_W_o"]
    out["Wr"] = a["L1_ffn_Wr"].T
    out["W1t"] = a["L1_ffn_W1"].transpose(2, 0, 1).reshape(P, E1 * 2 * F1)
    out["W2t"] = a["L1_ffn_W2"].reshape(E1, P, 2, F1 // 2).transpose(3, 0, 2, 1).reshape(P, E1 * F1)
    return {n: np.ascontiguousarray(v) for n, v in out.items()}


def kernel(**inputs):
    import concourse.bacc as bacc
    from concourse.bass_utils import run_bass_kernel_spmd

    nc = bacc.Bacc("TRN2", target_bir_lowering=False, num_devices=1)
    arrays = {**layout({n: np.asarray(a) for n, a in inputs.items()}), **constants()}
    args = {n: nc.dram_tensor(n, a.shape, mybir.dt.from_np(a.dtype), kind="ExternalInput").ap() for n, a in arrays.items()}
    out = nc.dram_tensor("out", [NTOK, P], F32, kind="ExternalOutput").ap()
    build(nc, out=out, **args)
    r = run_bass_kernel_spmd(nc, [arrays], core_ids=[0])
    return r.results[0]["out"].reshape(B, T, P)
```

```python
from contextlib import ExitStack

import numpy as np

import concourse.bass as bass
from concourse import mybir

ALU = mybir.AluOpType
ACT = mybir.ActivationFunctionType
AX = mybir.AxisListType
F32 = mybir.dt.float32
BF16 = mybir.dt.bfloat16
U32 = mybir.dt.uint32
U8 = mybir.dt.uint8

P = 128
B, T = 16, 256
NTOK = B * T
NT = NTOK // P
GT = 4
GN = GT * P
NG = NT // GT
GB = GN // T
LEVELS = [1, 2, 4, 8, 16, 32, 64]
NL = len(LEVELS)
EPS = 1e-5
NLP = NL + 1
NCONST = 17

E0, K0, CAP, H0 = 64, 3, 64, 512
HC = H0 // P
NSLOT0 = E0 * CAP
RING = 16
NPAIR = E0 // 2
NH, HD, DR = 16, 8, 32
SCORE_SCALE = float(1.0 / np.sqrt(HD + DR))
ND = NH // 2
RD = 4
KR = 3 * DR
KN = 3 * HD
KM = KR + KN
KS = KM + 2
MASKED = -1e30
E1, K1, F1 = 8, 2, 256
REG = NTOK
ND1 = NTOK * K1 // P + E1
ND1 = (ND1 + 7) // 8 * 8
LAP1 = 8
NQ1 = 4
AHEAD = 2
F32R = mybir.dt.float32r
NROUND = E0 // RING
PAIRS = RING // 2
NQ = 4


class Chain:

    def __init__(self, eng, sem, group, n, base=0, first=0):
        self.eng, self.sem, self.base, self.n, self.k = eng, sem, group * n + base, n, first

    def __call__(self, ins):
        self.k += 1
        ins.then_inc(self.sem, 1)
        self.eng.wait_ge(self.sem, self.base + self.k)

    def end(self, last=None):
        last = self.n if last is None else last
        assert self.k == last, (self.k, last)


def after(g, n):
    return not isinstance(g, int) or g >= n


def within(g, n):
    return not isinstance(g, int) or g < n


class Group:

    def __init__(self, j, p, k):
        self.par, self.half = (p - k) % 2, j + (p - k) // 2
        self.g = self.half * 2 + self.par


def steps(eng, stages):
    lags = 1 + max(k for _, k in stages)

    def step(j, p, there):
        for stage, k in stages:
            if there(k):
                stage(Group(j, p, k))

    full = lags // 2
    for s in range(2 * full):
        step(s // 2, s % 2, lambda k: 0 <= s - k)
    with eng.Fori(full, NG // 2) as j:
        for p in range(2):
            step(j, p, lambda k: True)
    for s in range(NG, NG + lags - 1):
        step(s // 2, s % 2, lambda k: s - k < NG)


def next_duo(i, n):
    return ((i + n) % ND, 2 if i + n < ND else 1)


def turned_pairs(g, i):
    return g * (ND // 2) + i // 2 - 1


def build(nc, x, Wq, bq, Wk, bk, Wv, bv, Wg, bg, Wo, bo, gamma, beta, gate_w, gate_b, w1, b1t, w2, b2,
          Wkvd, Wku, Wvu, Wq1, Wqr, Wkr, Wo1, Wr, W1t, W2t, out, const, masks, rope):
    with ExitStack() as ctx:
        def sb(name, shape, dt=F32):
            return ctx.enter_context(nc.sbuf_tensor("sb_" + name, shape, dt))

        def sem(name):
            return ctx.enter_context(nc.semaphore(name))

        slots_in = nc.dram_tensor("slots_in", [NSLOT0, P], F32).ap()
        slots_out = nc.dram_tensor("slots_out", [NSLOT0, P], F32).ap()
        parts = nc.dram_tensor("parts", [2, 2, KN, NH, GN], F32).ap()
        rows1_in = nc.dram_tensor("rows1_in", [E1 * REG, P], F32).ap()
        rows1_out = nc.dram_tensor("rows1_out", [ND1 * P, P], F32).ap()

        pairbank = [ctx.enter_context(nc.psum_tensor(f"banks{i}", [P, 1024], F32)) for i in range(2)]
        bank = [pairbank[i // 2][:, i % 2 * 512:(i % 2 + 1) * 512] for i in range(4)]
        bank += [ctx.enter_context(nc.psum_tensor(f"bank{i}", [P, 512], F32)) for i in range(4, 8)]

        X = sb("X", [P, NT, P])
        cst = sb("cst", [P, 2 * P + E0 + ND1 + NT])
        iota_t = cst[:, 2 * P + E0:2 * P + E0 + ND1]
        iota128 = cst[:, 2 * P + E0 + ND1:]
        ident = cst[:, 0:128]
        iota_e = cst[:, 256:320]
        mask_sb = sb("mask_sb", [P, NL, GT, P // 2], U8)
        tri = sb("tri", [P, P], BF16)
        ones = sb("ones", [P, P], BF16)
        wq_sb, wk_sb, wv_sb, wg_sb, wo_sb = (sb(n, [P, P]) for n in ("wq", "wk", "wv", "wg", "wo"))
        gw_sb = sb("gw", [P, E0])
        bq_c, bk_c, bg_c = (sb(n, [P, 1]) for n in ("bq", "bk", "bg"))
        bv_b, bo_b, gamma_b, beta_b = (sb(n, [P, P]) for n in ("bv_b", "bo_b", "gamma_b", "beta_b"))
        gb_b = sb("gb_b", [P, E0])
        mhalf = sb("mhalf", [P, GT])
        zrow = sb("zrow", [P, 1024])
        top0 = sb("top0", [P, NT, K0])
        gslot = sb("gslot", [P, NT, K0], U32)
        valid = sb("valid", [P, NT, K0])
        count = sb("count", [P, E0])
        countb = sb("countb", [P, 2, E0], BF16)

        Y = sb("Y", [P, GT, P])
        st = sb("st", [P, 5, GT, 6])
        mv = sb("mv", [P, 5, GT, 2])
        ve = sb("ve", [P, 5, GT])
        rs = sb("rs", [P, 5, GT])

        early = ExitStack()

        def eb(name, shape, dt=F32):
            return early.enter_context(nc.sbuf_tensor("sb_" + name, shape, dt))

        xn = eb("xn", [P, 2, GT, P])
        xb = eb("xb", [P, 2, GT, P])
        xnT = eb("xnT", [P, GN])
        Q = eb("Q", [P, 2, GN])
        K = eb("K", [P, 2, GN])
        G = eb("G", [P, 2, GN])
        V = eb("V", [P, 2, GT, P])
        AD = eb("AD", [P, GN])
        AXT = eb("AXT", [P, GB, P])
        OT = eb("OT", [P, GN])
        xf = eb("xf", [P, 2, GT, P])
        xfT = eb("xfT", [P, GN])
        Tm = [eb(f"T{m}", [P, GN // m]) for m in LEVELS[1:]]
        mask_in = eb("mask_in", [P, NL, P // 2])
        lg = eb("lg", [P, GT, E0])
        best = eb("best", [P, GT, 8])
        ix = eb("ix", [P, GT, 8], U32)
        ixf = eb("ixf", [P, GT, K0])
        oh = eb("oh", [P, GT, K0, E0])
        M = eb("M", [P, GT, E0])
        Mb = eb("Mb", [P, GT, E0], BF16)
        ohp = eb("ohp", [P, GT, K0, E0])
        pos = eb("pos", [P, GT, K0])
        r0 = eb("r0", [P, GT, K0])
        r1 = eb("r1", [P, GT, K0])
        r2 = eb("r2", [P, GT, K0])
        gcnt = eb("gcnt", [P, E0])
        sslot = eb("sslot", [P, 2, GT, K0], U32)

        w1r = eb("w1r", [P, RING, H0])
        w2r = eb("w2r", [P, RING, HC, P])
        xs = eb("xs", [P, NQ, P])
        xsT = eb("xsT", [P, 2, P])
        hs = eb("hs", [P, 2, H0])
        hT = eb("hT", [P, 2, HC, P])
        gT = eb("gT", [P, 2, HC, P])
        b1T = eb("b1T", [P, E0, HC])
        b2_b = eb("b2_b", [P, NPAIR, P])
        ys = eb("ys", [P, NQ, P])

        early.close()

        wkvd_sb, wku_sb, wvu_sb, wq1_sb, wo1_sb = (sb(n, [P, P]) for n in ("wkvd", "wku", "wvu", "wq1", "wo1"))
        wqr_sb, wkr_sb = sb("wqr", [P, 2 * DR]), sb("wkr", [P, 2 * DR])
        wr_sb = sb("wr", [P, E1])
        rope_sb = sb("rope", [2 * DR, T])
        identb = sb("identb", [P, P], BF16)
        ones8 = sb("ones8", [P, E1])
        maskq = sb("maskq", [P, 2, P], BF16)
        maskk = sb("maskk", [P, 2, P], BF16)
        gates = sb("gates", [P, NT, K0])
        gsum = sb("gsum", [P, NT])
        gidx = sb("gidx", [P, 2, GT, K0], U32)
        R = sb("R", [P, 2, GT * K0, P])
        xa = sb("xa", [P, GT, P])
        xaT = sb("xaT", [P, GN])
        ckvT = sb("ckvT", [P, GN])
        qkh = sb("qkh", [P, 2, GN], F32R)
        qkl = sb("qkl", [P, 2, GN], F32R)
        rt = sb("rt", [DR, 2, GN])
        rp = sb("rp", [KR, 2, GN], F32R)
        SQ = sb("SQ", [P, 2 * RD, GN], F32R)
        SK = sb("SK", [P, 2 * RD, GN], F32R)
        V1 = sb("V1", [P, 2, GT, NH, 32])
        mx = sb("mx", [P, 2, 2, GB, 2])
        ms = sb("ms", [P, 2, 2 * 8], F32R)
        mT = sb("mT", [2 * 8, 2, P])
        onerow = sb("onerow", [2 * RD, GN])
        PT = sb("PT", [P, 2, 4, 384])
        raw = sb("raw", [P, GN])
        rec = sb("rec", [P, 4, 4])
        att = sb("att", [P, GT, P])
        attT = sb("attT", [P, GN])
        xg = sb("xg", [P, 2, GT, P])
        xgT = sb("xgT", [P, GN])
        lg1 = sb("lg1", [P, GT, E1])
        best1 = sb("best1", [P, GT, 8])
        ix1 = sb("ix1", [P, GT, 8], U32)
        ixa = sb("ixa", [P, NT, K1])
        posa = sb("posa", [P, NT, K1])
        oh1 = sb("oh1", [P, GT, K1, E1])
        ohp1 = sb("ohp1", [P, GT, K1, E1])
        M1 = sb("M1", [P, GT, E1])
        M1b = sb("M1b", [P, GT, E1], BF16)
        gcnt1 = sb("gcnt1", [P, E1])
        count1 = sb("count1", [P, E1])
        count1b = sb("count1b", [P, E1], BF16)
        srow1 = sb("srow1", [P, 2, GT, K1], U32)
        w1d = sb("w1d", [P, E1, 2 * F1])
        w2d = sb("w2d", [P, E1, 2, P])
        ntile = sb("ntile", [P, E1])
        tend = sb("tend", [P, E1])
        tbase = sb("tbase", [P, E1])
        tw = sb("tw", [P, E1])
        cmp1 = sb("cmp1", [P, E1, NT])
        cmp2 = sb("cmp2", [P, ND1, E1])
        cmp3 = sb("cmp3", [P, ND1, E1])
        tl = sb("tl", [P, 2, ND1])
        tli = sb("tli", [P, 2, ND1], mybir.dt.int32)
        grow1 = sb("grow1", [P, NT, K1], U32)
        gt1 = sb("gt1", [P, NT, K1])
        gw1 = sb("gw1", [P, NT, K1])
        xd = sb("xd", [P, NQ1, P])
        xdT = sb("xdT", [P, 2, P])
        sg = sb("sg", [P, 2, F1])
        ac = sb("ac", [P, 2, F1])
        acT = sb("acT", [P, 2, F1])
        yd = sb("yd", [P, NQ1, P])

        s_const, s_x, s_zero = sem("s_const"), sem("s_x"), sem("s_zero")
        s_tri, s_step = sem("s_tri"), sem("s_step")
        s_ve = [sem(f"s_ve{i}") for i in range(3)]
        s_rs = [sem(f"s_rs{i}") for i in range(3)]
        s_xn = sem("s_xn")
        s_xnb = sem("s_xnb")
        s_xnTp, s_xnT = sem("s_xnTp"), sem("s_xnT")
        s_q, s_k, s_g, s_v = sem("s_q"), sem("s_k"), sem("s_g"), sem("s_v")
        s_qe, s_ge, s_ve_ = sem("s_qe"), sem("s_ge"), sem("s_vev")
        s_lev, s_upd, s_aev = sem("s_lev"), sem("s_upd"), sem("s_aev")
        s_cross, s_axt = sem("s_cross"), sem("s_axt")
        s_av, s_ot, s_wo, s_y = sem("s_av"), sem("s_ot"), sem("s_wo"), sem("s_y")
        s_xf, s_xfTp, s_xfT, s_lg = sem("s_xf"), sem("s_xfTp"), sem("s_xfT"), sem("s_lg")
        s_M, s_pos, s_posr, s_slot = sem("s_M"), sem("s_pos"), sem("s_posr"), sem("s_slot")
        s_scat = [sem("s_scat0"), sem("s_scat1")]
        c_F, c_G, c_H, c_W = sem("c_F"), sem("c_G"), sem("c_H"), sem("c_W")
        s_w = [sem(f"s_w{i}") for i in range(PAIRS)]
        s_b1 = sem("s_b1")
        s_xs = [sem(f"s_xs{i}") for i in range(NQ)]
        s_xsTp, s_xsT, s_h, s_hs, s_hTp, s_hT, s_gT, s_yp, s_ys = (
            sem(n) for n in ("s_xsTp", "s_xsT", "s_h", "s_hs", "s_hTp", "s_hT", "s_gT", "s_yp", "s_ys"))
        s_yo = [sem(f"s_yo{i}") for i in range(NQ)]
        s_out = sem("s_out")
        s_w2c, s_pre = sem("s_w2c"), sem("s_pre")
        s_gexp, s_gsub = sem("s_gexp"), sem("s_gsub")
        s_gat = [sem("s_gat0"), sem("s_gat1")]
        s_radd, s_gidx = sem("s_radd"), sem("s_gidx")
        s_ve += [sem("s_ve3"), sem("s_ve4")]
        s_rs += [sem("s_rs3"), sem("s_rs4")]
        (s_xa, s_xaTp, s_xaT, s_ckvp, s_ckv, s_q1p, s_qh, s_ql, s_qr, s_rq, s_kp, s_kh, s_kl, s_v1p, s_v1, s_kr, s_rk,
         s_parts, s_max, s_maxr, s_ms, s_mTp, s_mT, s_st, s_exp, s_pv, s_raw, s_rawTp, s_norm,
         s_attTp, s_attT, s_wo1, s_x3, s_xg, s_xgTp, s_xgT, s_lg1, s_M1, s_pos1, s_row1) = (
            sem(n) for n in ("s_xa s_xaTp s_xaT s_ckvp s_ckv s_q1p s_qh s_ql s_qr s_rq s_kp s_kh s_kl s_v1p s_v1 s_kr s_rk "
                             "s_parts s_max s_maxr s_ms s_mTp s_mT s_st s_exp s_pv s_raw s_rawTp s_norm "
                             "s_attTp s_attT s_wo1 s_x3 s_xg s_xgTp s_xgT s_lg1 s_M1 s_pos1 s_row1").split())
        s_fill = [sem(f"s_fill{i}") for i in range(RD)]
        s_shift = [sem(f"s_shift{i}") for i in range(RD)]
        s_scat1 = [sem("s_scat1_0"), sem("s_scat1_1")]
        c_C, c_N, c_R, c_T, c_Q = (sem(n) for n in ("c_C", "c_N", "c_R", "c_T", "c_Q"))
        s_fin1 = sem("s_fin1")
        s_tot, s_tiles = sem("s_tot"), sem("s_tiles")
        s_sg, s_ac, s_acTp, s_acT, s_ydp, s_yd = (sem(n) for n in "s_sg s_ac s_acTp s_acT s_ydp s_yd".split())
        s_fin = sem("s_fin")
        s_ones1 = sem("s_ones1")
        s_zero1 = sem("s_zero1")
        s_vinit, s_pinit = sem("s_vinit"), sem("s_pinit")


        block = ctx.enter_context(nc.Block())

        def stands_alone(eng):
            eng.sem_inc(s_step, 1)

        def blocks(ap2, m):
            return ap2.rearrange("p (c two m) -> p c two m", two=2, m=m)

        @block.sync
        def _(sp):
            sp.dma_start(X[:, 0:GT, :], x[0:GN, :].rearrange("(t p) d -> p t d", p=P)).then_inc(s_x, 16)
            for dst, src in ((cst[:], const[:, :]), (wq_sb[:], Wq[:, :]), (wk_sb[:], Wk[:, :]),
                             (wg_sb[:], Wg[:, :]), (wv_sb[:], Wv[:, :]), (wo_sb[:], Wo[:, :]),
                             (gw_sb[:], gate_w[:, :]), (mask_in[:], masks.rearrange("p (l n) -> p l n", l=NL))):
                sp.dma_start(dst, src).then_inc(s_const, 16)
            for dst, src in ((bq_c, bq), (bk_c, bk), (bg_c, bg)):
                sp.dma_start(dst[:], src.rearrange("(p o) -> p o", o=1)).then_inc(s_const, 16)
            for dst, src in ((bv_b, bv), (bo_b, bo), (gamma_b, gamma), (beta_b, beta), (gb_b, gate_b)):
                sp.dma_start(dst[:], src.partition_broadcast(P)).then_inc(s_const, 16)
            sp.dma_start(X[:, GT:NT, :], x[GN:NTOK, :].rearrange("(t p) d -> p t d", p=P)).then_inc(s_const, 16)
            sp.wait_ge(s_vinit, 1)
            sp.dma_start(slots_in.rearrange("(p t) d -> p (t d)", p=P)[:, 0:1024], zrow[:]).then_inc(s_zero, 16)
            sp.dma_start(slots_in.rearrange("(p t) d -> p (t d)", p=P)[:, 1024:2048], zrow[:]).then_inc(s_zero, 16)
            sp.dma_start(slots_in.rearrange("(p t) d -> p (t d)", p=P)[:, 2048:3072], zrow[:]).then_inc(s_zero, 16)
            sp.dma_start(slots_in.rearrange("(p t) d -> p (t d)", p=P)[:, 3072:4096], zrow[:]).then_inc(s_zero, 16)
            z1 = rows1_in.rearrange("(a p t) d -> a p (t d)", p=P, t=8)
            for a in range(8):
                sp.dma_start(z1[4 * a:4 * a + 4].rearrange("a p n -> p a n"), zrow[:].unsqueeze(1).broadcast_to([P, 4, 1024])).then_inc(s_zero1, 16)
            sp.dma_start(b1T[:], b1t.rearrange("p (e c) -> p e c", c=HC)).then_inc(s_b1, 16)
            for h in range(2):
                sp.dma_start(b2_b[h * CAP:(h + 1) * CAP], b2.rearrange("(a two) d -> two a d", two=2)[h].partition_broadcast(CAP)
                             ).then_inc(s_b1, 16)

            def weights(pair, i):
                e = pair * 2
                sp.dma_start(w1r[:, 2 * i:2 * i + 2, :], w1[bass.ds(e, 2)].rearrange("e d h -> d e h")).then_inc(s_w[i], 16)
                sp.dma_start(w2r[:, 2 * i:2 * i + 2].rearrange("p e c d -> p (e c) d"),
                             w2[bass.ds(e, 2)].rearrange("e (c p) d -> p (e c) d", p=P)).then_inc(s_w[i], 16)

            def slots(pair, q):
                sp.dma_start(xs[:, q, :], slots_in[bass.ds(pair * P, P), :]).then_inc(s_xs[q], 16)

            def store(pair, q):
                sp.wait_ge(s_ys, pair + 1)
                sp.dma_start(slots_out[bass.ds(pair * P, P), :], ys[:, q, :]).then_inc(s_yo[q], 16)

            for pair in range(PAIRS):
                weights(pair, pair)
            sp.wait_ge(s_zero, 16 * 4)
            for p in range(2):
                sp.wait_ge(s_scat[p], 16 * GT * K0 * (NG // 2))
            def slots_after(pair, q):
                sp.wait_ge(s_xsTp, pair - NQ + 1)
                slots(pair, q)

            for pair in range(NQ):
                slots(pair, pair)
            for pair in range(NQ, NQ + AHEAD):
                slots_after(pair, pair % NQ)
            with sp.Fori(0, NROUND - 1) as r:
                for i in range(PAIRS):
                    pair = r * PAIRS + i
                    slots_after(pair + NQ + AHEAD, (i + AHEAD) % NQ)
                    store(pair, i % NQ)
                    weights(pair + PAIRS, i)
            for pair in range(NPAIR - PAIRS, NPAIR):
                if pair + NQ + AHEAD < NPAIR:
                    slots_after(pair + NQ + AHEAD, (pair + AHEAD) % NQ)
                store(pair, pair % NQ)
            for q in range(NQ):
                sp.wait_ge(s_yo[q], 16 * (NPAIR // NQ))

            for dst, src in ((wkvd_sb[:], Wkvd[:, :]), (wku_sb[:], Wku[:, :]), (wvu_sb[:], Wvu[:, :]), (wq1_sb[:], Wq1[:, :]),
                             (wo1_sb[:], Wo1[:, :]), (wr_sb[:], Wr[:, :]), (rope_sb[:], rope[:, :]),
                             (wqr_sb[:, 0:DR], Wqr[:, :]), (wqr_sb[:, DR:DR + 16], Wqr[:, 16:32]), (wqr_sb[:, DR + 16:], Wqr[:, 0:16]),
                             (wkr_sb[:, 0:DR], Wkr[:, :]), (wkr_sb[:, DR:DR + 16], Wkr[:, 16:32]), (wkr_sb[:, DR + 16:], Wkr[:, 0:16])):
                sp.dma_start(dst, src).then_inc(s_w2c, 16)
            sp.wait_ge(s_pre, 1)
            for r in range(2):
                sp.dma_start(SK[KM + r:KM + r + 1].bitcast(F32), onerow[:]).then_inc(s_ones1, 16)
            sp.dma_start(w1d[:], W1t.rearrange("p (e n) -> p e n", e=E1)).then_inc(s_w2c, 16)
            sp.dma_start(w2d[:], W2t.rearrange("p (e c n) -> p e c n", e=E1, c=2)).then_inc(s_w2c, 16)

            def write_parts(grp, side):
                g, p = grp.g, grp.par
                sp.wait_ge((s_ql, s_kl)[side], g + 1)
                for r, src in enumerate(((qkh, qkh, qkl), (qkh, qkl, qkh))[side]):
                    sp.dma_start(parts[p, side, r * HD:(r + 1) * HD].rearrange("d h n -> (d h) n"),
                                 src[:, side].bitcast(F32)).then_inc(s_parts, 16)

            def fill(grp, i):
                g, p, r = grp.g, grp.par, i % RD
                if i == 0:
                    sp.wait_ge(s_parts, 96 * (g + 1))
                    sp.wait_ge(s_rk, g + 1)
                if after(g, 1) or i >= RD:
                    sp.wait_ge(s_st, 4 * (g * ND + i - RD + 1))
                for side, S in ((0, SQ), (1, SK)):
                    if i < RD:
                        sp.dma_start(S[0:KR, 2 * r:2 * r + 2, :].bitcast(F32),
                                     rp[:, side].bitcast(F32).unsqueeze(1).broadcast_to([KR, 2, GN])).then_inc(s_fill[r], 16)
                    sp.dma_start(S[KR:KM, 2 * r:2 * r + 2, :].bitcast(F32), parts[p, side, :, 2 * i:2 * i + 2, :]).then_inc(s_fill[r], 16)

            def shift(grp, i):
                g, r = grp.g, i % RD
                sp.wait_ge(s_mT, g * ND + i + 1)
                for h in range(2):
                    sp.dma_start(SQ[KM + h:KM + h + 1, 2 * r:2 * r + 2, :].bitcast(F32), mT[8 * h:8 * h + 8, i % 2, :]
                                 ).then_inc(s_shift[r], 16)

            def on(i, n, stage):
                k, lag = next_duo(i, n)
                return lambda grp: stage(grp, k), lag

            slots_of = []
            for i in range(ND):
                slots_of += [on(i, 1, shift), on(i, 3, fill)]
                if i in (3, 4):
                    slots_of.append(((lambda side: lambda grp: write_parts(grp, side))(i - 3), 1))
            steps(sp, slots_of)

            for p in range(2):
                sp.wait_ge(s_scat1[p], 16 * GT * K1 * (NG // 2))
            sp.wait_ge(s_zero1, 16 * 8)
            sp.wait_ge(s_tiles, 1)

            def tile_in(t, q):
                row = sp.value_load(tli[0:1, 1, bass.ds(t, 1)], min_val=0, max_val=E1 * REG - P)
                sp.dma_start(xd[:, q, :], rows1_in[bass.ds(row, P), :]).then_inc(s_xs[q], 16)

            def tile_out(t, q):
                sp.wait_ge(s_yd, t + 1)
                sp.dma_start(rows1_out[bass.ds(t * P, P), :], yd[:, q, :]).then_inc(s_yo[q], 16)

            def tile_after(t, q):
                sp.wait_ge(s_xsTp, NPAIR + t - NQ1 + 1)
                tile_in(t, q)

            for q in range(NQ1):
                tile_in(q, q)
            for t in range(NQ1, NQ1 + AHEAD):
                tile_after(t, t % NQ1)
            with sp.Fori(0, ND1 // NQ1 - 2) as lap:
                for q in range(NQ1):
                    tile_after(lap * NQ1 + q + NQ1 + AHEAD, (q + AHEAD) % NQ1)
                    tile_out(lap * NQ1 + q, q)
            for t in range(ND1 - 2 * NQ1, ND1):
                if t + NQ1 + AHEAD < ND1:
                    tile_after(t + NQ1 + AHEAD, (t + AHEAD) % NQ1)
                tile_out(t, t % NQ1)

            out_t = out.rearrange("(t p) d -> p t d", p=P)
            with sp.Fori(0, NG) as g:
                sp.wait_ge(s_fin, g + 1)
                sp.dma_start(out_t[:, bass.ds(g * GT, GT), :], X[:, bass.ds(g * GT, GT), :]).then_inc(s_out, 16)
            sp.wait_ge(s_out, 16 * NG)

        @block.gpsimd
        def _(pool):
            pool.wait_ge(s_const, 16 * NCONST)
            pool.wait_ge(s_x, 16)
            pool.wait_ge(s_vinit, 1)

            def power(i, grp):
                pool.wait_ge(s_ve[i], grp.g + 1)
                pool.tensor_tensor(rs[:, i, :], ve[:, i, :], mhalf[:], ALU.pow).then_inc(s_rs[i], 1)

            def residuals(grp):
                g = grp.g
                pool.wait_ge(s_xn, g + 1)
                if after(g, 2):
                    pool.wait_ge(s_y, g - 1)
                pool.tensor_tensor(xb[:, grp.par], xn[:, grp.par], bo_b[:].unsqueeze(1).broadcast_to([P, GT, P]),
                                   ALU.add).then_inc(s_xnb, 1)
                xt = X[:, bass.ds(g * GT, GT), :]
                pool.tensor_tensor(xt, xt, beta_b[:].unsqueeze(1).broadcast_to([P, GT, P]), ALU.add).then_inc(s_xnb, 1)

            def scatter0(grp):
                pool.wait_ge(s_slot, grp.g + 1)
                stands_alone(pool)
                for t in range(GT):
                    for k in range(K0):
                        pool.indirect_dma_start(
                            out=slots_in[:, :], out_offset=bass.IndirectOffsetOnAxis(ap=sslot[:, grp.par, t, k:k + 1], axis=0),
                            in_=xf[:, grp.par, t, :], in_offset=None, bounds_check=NSLOT0 - 1, oob_is_err=False,
                        ).then_inc(s_scat[grp.par], 16)

            pool.wait_ge(s_zero, 16 * 4)
            steps(pool, [(lambda grp: power(1, grp), 3), (lambda grp: power(2, grp), 3), (lambda grp: power(0, grp), 0),
                         (residuals, 1), (scatter0, 4)])

            for q in range(NQ):
                pool.wait_ge(s_yo[q], 16 * (NPAIR // NQ))

            def gather0(grp):
                if after(grp.g, 2):
                    pool.wait_ge(s_radd, grp.g - 1)
                pool.tensor_copy(gidx[:, grp.par, :, 0:K0], gslot[:, bass.ds(grp.g * GT, GT), :]).then_inc(s_gidx, 1)
                pool.wait_ge(s_gidx, grp.g + 1)
                stands_alone(pool)
                for t in range(GT):
                    for k in range(K0):
                        pool.indirect_dma_start(
                            out=R[:, grp.par, t * K0 + k, :], out_offset=None, in_=slots_out[:, :],
                            in_offset=bass.IndirectOffsetOnAxis(ap=gidx[:, grp.par, t, k:k + 1], axis=0),
                            bounds_check=NSLOT0 - 1, oob_is_err=False).then_inc(s_gat[grp.par], 16)

            def power3(grp):
                power(3, grp)

            def power4(grp):
                power(4, grp)

            def scatter1(grp):
                pool.wait_ge(s_row1, grp.g + 1)
                stands_alone(pool)
                for t in range(GT):
                    for k in range(K1):
                        pool.indirect_dma_start(
                            out=rows1_in[:, :], out_offset=bass.IndirectOffsetOnAxis(ap=srow1[:, grp.par, t, k:k + 1], axis=0),
                            in_=xg[:, grp.par, t, :], in_offset=None, bounds_check=E1 * REG - 1, oob_is_err=False,
                        ).then_inc(s_scat1[grp.par], 16)

            pool.wait_ge(s_zero1, 16 * 8)
            steps(pool, [(gather0, 0), (power4, 3), (power3, 0), (scatter1, 3)])

            for q in range(NQ1):
                pool.wait_ge(s_yo[q], 16 * (NPAIR // NQ + ND1 // NQ1))
            pool.wait_ge(s_tiles, 2)

            def gather1(g, p):
                pool.tensor_copy(gidx[:, p, :, 0:K1], grow1[:, bass.ds(g * GT, GT), :]).then_inc(s_gidx, 1)
                pool.wait_ge(s_gidx, NG + g + 1)
                stands_alone(pool)
                for t in range(GT):
                    for k in range(K1):
                        pool.indirect_dma_start(
                            out=R[:, p, t * K1 + k, :], out_offset=None, in_=rows1_out[:, :],
                            in_offset=bass.IndirectOffsetOnAxis(ap=gidx[:, p, t, k:k + 1], axis=0),
                            bounds_check=ND1 * P - 1, oob_is_err=False).then_inc(s_gat[p], 16)
            gather1(0, 0)
            gather1(1, 1)
            with pool.Fori(1, NG // 2) as j:
                for p in range(2):
                    pool.wait_ge(s_fin, 2 * j + p - 1)
                    gather1(2 * j + p, p)

        @block.scalar
        def _(act):
            act.wait_ge(s_const, 16 * NCONST)

            def norm_in(grp):
                act.wait_ge(s_xnTp, grp.g + 1)
                act.activation(xnT[:], bank[0][:], ACT.Copy).then_inc(s_xnT, 1)

            def queries_keys(grp):
                g, p = grp.g, grp.par
                act.wait_ge(s_q, g + 1)
                act.activation(Q[:, p], bank[1][:], ACT.Identity, bias=bq_c[:, 0:1])
                act.wait_ge(s_k, g + 1)
                act.activation(K[:, p], bank[0][:], ACT.Identity, bias=bk_c[:, 0:1]).then_inc(s_qe, 1)

            def gate(grp):
                act.wait_ge(s_g, grp.g + 1)
                act.activation(G[:, grp.par], bank[1][:], ACT.Sigmoid, bias=bg_c[:, 0:1]).then_inc(s_ge, 1)

            def cross(grp):
                act.wait_ge(s_cross, grp.g + 1)
                act.activation(AXT[:], bank[4][:, 0:GB * P].rearrange("p (b n) -> p b n", b=GB), ACT.Copy).then_inc(s_axt, 1)

            def attended(grp):
                act.wait_ge(s_av, grp.g + 1)
                act.activation(OT[:], bank[5][:], ACT.Copy).then_inc(s_ot, 1)

            def router_in0(grp):
                act.wait_ge(s_xfTp, grp.g + 1)
                act.activation(xfT[:], bank[7][:], ACT.Copy).then_inc(s_xfT, 1)

            steps(act, [(router_in0, 4), (attended, 3), (norm_in, 1), (queries_keys, 1), (gate, 1), (cross, 2)])

            def gelus(pair, par):
                act.wait_ge(s_hT, pair + 1)
                act.activation(gT[:, par], hT[:, par], ACT.Gelu).then_inc(s_gT, 1)

            gelus(0, 0)
            gelus(1, 1)
            with act.Fori(1, NPAIR // 2) as j:
                for p in range(2):
                    gelus(2 * j + p, p)

            act.wait_ge(s_gsub, 1)
            act.activation(gates[:], gates[:], ACT.Exp).then_inc(s_gexp, 1)

            def norm1_in(grp):
                act.wait_ge(s_xaTp, grp.g + 1)
                act.activation(xaT[:], bank[2][:], ACT.Copy).then_inc(s_xaT, 1)

            def latent(grp):
                act.wait_ge(s_ckvp, grp.g + 1)
                act.activation(ckvT[:], bank[2][:], ACT.Copy).then_inc(s_ckv, 1)

            def upper(grp, side):
                if after(grp.g, 1):
                    act.wait_ge(s_parts, 96 * grp.g)
                act.wait_ge((s_q1p, s_kp)[side], grp.g + 1)
                act.activation(qkh[:, side], bank[2][:], ACT.Copy).then_inc((s_qh, s_kh)[side], 1)

            def values_in(grp):
                act.wait_ge(s_v1p, grp.g + 1)
                act.activation(V1[:, grp.par, :, :, 0:HD], bank[2][:].rearrange("p (t h d) -> p t h d", t=GT, h=NH), ACT.Copy).then_inc(s_v1, 1)

            def shift_rows(grp, i):
                act.wait_ge(s_mTp, grp.g * ND + i + 1)
                if after(grp.g, 1) or i >= 2:
                    r = (i - 2) % RD
                    act.wait_ge(s_shift[r], 64 * grp.g + (32 * (1 + (i - 2) // RD) if i >= 2 else 0))
                act.activation(mT[:, i % 2, :], bank[7][0:16, 0:P], ACT.Copy).then_inc(s_mT, 1)

            def exponentials(grp, i, n):
                act.wait_ge(s_st, (grp.g * ND + i) * 4 + n + 1)
                act.activation(PT[:, i % 2, n, :], bank[4 + n % 2][:, P:512], ACT.Exp, scale=SCORE_SCALE).then_inc(s_exp, 1)

            def raw_out(grp, i):
                act.wait_ge(s_pv, grp.g * (ND // 2) + i // 2 + 1)
                act.activation(raw[:], bank[6][:], ACT.Copy).then_inc(s_raw, 1)

            def attended_in(grp):
                act.wait_ge(s_attTp, grp.g + 1)
                act.activation(attT[:], bank[3][:], ACT.Copy).then_inc(s_attT, 1)

            def router_in(grp):
                act.wait_ge(s_xgTp, grp.g + 1)
                act.activation(xgT[:], bank[3][:], ACT.Copy).then_inc(s_xgT, 1)

            def first(i):
                return lambda grp: exponentials(grp, i, 0)

            def others(i):
                def stage(grp):
                    for n in range(1, 4):
                        exponentials(grp, i, n)
                    if i % 2:
                        raw_out(grp, i)
                return stage

            def shifts(i):
                return lambda grp: shift_rows(grp, i)

            more = {0: [(norm1_in, 1), (attended_in, 3)], 1: [(latent, 1)], 2: [(lambda grp: upper(grp, 0), 1)],
                    3: [(lambda grp: upper(grp, 1), 1)], 4: [(values_in, 1)], 5: [(router_in, 3)]}
            slots_of = []
            for i in range(ND):
                k, lag = next_duo(i, 1)
                slots_of += [(first(i), 2), (shifts(k), lag), (others(i), 2)] + more.get(i, [])
            steps(act, slots_of)
            act.wait_ge(s_gsub, 2)
            act.activation(gt1[:], gw1[:], ACT.Exp).then_inc(s_gexp, 1)

            def d_in(t, p):
                act.wait_ge(s_xsTp, NPAIR + t + 1)
                act.activation(xdT[:, p], bank[p][:, 0:P], ACT.Copy).then_inc(s_xsT, 1)

            def d_silu(t, p):
                act.wait_ge(s_h, NPAIR + t + 1)
                act.activation(sg[:, p], bank[2 + p][:, F1:2 * F1], ACT.Silu).then_inc(s_sg, 1)

            def d_out(t, p, q, wait):
                act.wait_ge(s_ydp, t + 1)
                if wait is not None:
                    act.wait_ge(s_yo[q], 16 * (NPAIR // NQ + wait))
                act.activation(yd[:, q], bank[6 + p][:, 0:P], ACT.Copy).then_inc(s_yd, 1)

            def lap_of(lap, wait, left=ND1):
                for q in range(NQ1):
                    t, p = lap * NQ1 + q, q % 2
                    if q + AHEAD < left:
                        d_silu(t + AHEAD, p)
                    if q + AHEAD + 1 < left:
                        d_in(t + AHEAD + 1, 1 - p)
                    d_out(t, p, q, wait)

            d_in(0, 0)
            d_in(1, 1)
            d_silu(0, 0)
            d_in(2, 0)
            d_silu(1, 1)
            lap_of(0, None)
            with act.Fori(1, ND1 // NQ1 - 1) as lap:
                lap_of(lap, lap)
            lap_of(ND1 // NQ1 - 1, ND1 // NQ1 - 1, left=NQ1)

        @block.vector
        def _(dve):
            dve.memset(mhalf[:], -0.5)
            dve.memset(zrow[:], 0.0).then_inc(s_vinit, 1)
            dve.memset(count[:], 0.0)
            dve.memset(countb[:], 0.0).then_inc(s_pinit, 1)
            dve.wait_ge(s_pinit, 1)
            dve.wait_ge(s_const, 16 * NCONST)
            dve.wait_ge(s_x, 16)
            dve.tensor_copy(tri[:], cst[:, 128:256])
            dve.tensor_copy(mask_sb[:], mask_in[:].unsqueeze(2).broadcast_to([P, NL, GT, P // 2]))
            dve.memset(ones[:], 1.0).then_inc(s_tri, 1)
            dve.wait_ge(s_tri, 1)

            def variance(i, link, src):
                stands_alone(dve)
                for t in range(GT):
                    last = dve.bn_stats(st[:, i, t, :], src[:, t, :])
                link(last)
                stands_alone(dve)
                for t in range(GT):
                    last = dve.bn_aggr(mv[:, i, t, :], st[:, i, t, :])
                link(last)
                dve.tensor_scalar(ve[:, i, :], mv[:, i, :, 1], EPS, None, ALU.add).then_inc(s_ve[i], 1)

            def normalize(i, grp, src, dst):
                dve.wait_ge(s_rs[i], grp.g + 1)
                for t in range(GT):
                    last = dve.tensor_scalar(dst[:, t, :], src[:, t, :], mv[:, i, t, 0:1], rs[:, i, t:t + 1],
                                             ALU.subtract, ALU.mult)
                return last

            def layernorm(i, grp, link, src, dst):
                variance(i, link, src)
                return normalize(i, grp, src, dst)

            def norm_stats(grp):
                link = Chain(dve, c_F, grp.g, 2)
                variance(0, link, X[:, bass.ds(grp.g * GT, GT), :])
                link.end()

            def norm(grp):
                g, p = grp.g, grp.par
                if after(g, 2):
                    dve.wait_ge(s_xnb, 2 * (g - 1))
                    dve.wait_ge(s_xnTp, g - 1)
                normalize(0, grp, X[:, bass.ds(g * GT, GT), :], xn[:, p]).then_inc(s_xn, 1)

            def values(grp):
                g, p = grp.g, grp.par
                dve.wait_ge(s_v, g + 1)
                if after(g, 2):
                    dve.wait_ge(s_av, g - 1)
                dve.tensor_tensor(V[:, p], bank[3][:].rearrange("p (t n) -> p t n", t=GT),
                                  bv_b[:].unsqueeze(1).broadcast_to([P, GT, P]), ALU.add).then_inc(s_ve_, 1)

            def diagonal(grp):
                g, p = grp.g, grp.par
                q, k, gg = Q[:, p], K[:, p], G[:, p]
                dve.wait_ge(s_ge, g + 1)
                dve.wait_ge(s_lev, g * NLP + 1)
                dve.tensor_tensor(q, q, gg, ALU.mult).then_inc(s_upd, 1)
                if after(g, 1):
                    dve.wait_ge(s_av, g)
                dve.tensor_tensor(AD[:].rearrange("p (t n) -> p t n", t=GT), bank[6][:].rearrange("p (t n) -> p t n", t=GT),
                                  ident.unsqueeze(1).broadcast_to([P, GT, P]), ALU.mult).then_inc(s_aev, 1)
                dve.wait_ge(s_aev, g * NLP + 1)

            def level(grp, lo, hi):
                g, p = grp.g, grp.par
                link = Chain(dve, c_G, g, NL - 1, first=lo - 1)
                q, k = Q[:, p], K[:, p]
                for lv in range(lo, hi):
                    m = LEVELS[lv - 1]
                    tcur = Tm[lv - 2][:] if lv > 1 else G[:, p]
                    dve.wait_ge(s_lev, g * NLP + lv + 1)
                    if m < 64:
                        t3 = tcur.rearrange("p (c two) -> p c two", two=2)
                        dve.tensor_tensor(blocks(q, m)[:, :, 1], blocks(q, m)[:, :, 1],
                                          t3[:, :, 0:1].broadcast_to([P, GN // m // 2, m]), ALU.mult)
                        dve.tensor_tensor(blocks(k, m)[:, :, 0], blocks(k, m)[:, :, 0],
                                          t3[:, :, 1:2].broadcast_to([P, GN // m // 2, m]), ALU.mult).then_inc(s_upd, 1)
                    else:
                        q4 = q.rearrange("p (b s two m) -> p b s two m", b=GB, s=2, two=2)
                        k4 = k.rearrange("p (b s two m) -> p b s two m", b=GB, s=2, two=2)
                        t4 = tcur.rearrange("p (b s two) -> p b s two", b=GB, s=2)
                        dve.tensor_tensor(q4[:, :, 1, 1], q4[:, :, 1, 1], t4[:, :, 1, 0:1].broadcast_to([P, GB, m]), ALU.mult)
                        dve.tensor_tensor(k4[:, :, 0, 0], k4[:, :, 0, 0], t4[:, :, 0, 1:2].broadcast_to([P, GB, m]), ALU.mult
                                          ).then_inc(s_upd, 1)
                    dve.copy_predicated(blocks(AD[:], m)[:, :, 1], mask_sb[:, lv - 1].rearrange("p t n -> p (t n)").rearrange("p (c m) -> p c m", m=m),
                                        blocks(bank[2 if lv % 2 else 6][:], m)[:, :, 1]).then_inc(s_aev, 1)
                    if m < 64:
                        link(dve.tensor_tensor(Tm[lv - 1][:], t3[:, :, 0], t3[:, :, 1], ALU.mult))
                link.end(min(hi, NL) - 1)

            def post_a(grp):
                g, p = grp.g, grp.par
                link = Chain(dve, c_W, g, 7)
                dve.wait_ge(s_wo, g + 1)
                dve.wait_ge(s_xnb, 2 * (g + 1))
                dve.tensor_tensor(Y[:], bank[4][:].rearrange("p (t n) -> p t n", t=GT), xb[:, p], ALU.add).then_inc(s_y, 1)
                dve.wait_ge(s_y, g + 1)
                variance(1, link, Y[:])
                link.end(2)

            def post_b(grp):
                g, p = grp.g, grp.par
                link = Chain(dve, c_W, g, 7, first=2)
                link(normalize(1, grp, Y[:], Y[:]))
                link(dve.tensor_tensor(Y[:], Y[:], gamma_b[:].unsqueeze(1).broadcast_to([P, GT, P]), ALU.mult))
                xt = X[:, bass.ds(g * GT, GT), :]
                link(dve.tensor_tensor(xt, xt, Y[:], ALU.add))
                variance(2, link, xt)
                link.end(7)

            def post_c(grp):
                g, p = grp.g, grp.par
                if after(g, 2):
                    dve.wait_ge(s_scat[p], 16 * GT * K0 * grp.half)
                normalize(2, grp, X[:, bass.ds(g * GT, GT), :], xf[:, p]).then_inc(s_xf, 1)

            def choose(grp):
                g, p = grp.g, grp.par
                link = Chain(dve, c_H, g, 16)
                dve.wait_ge(s_lg, g + 1)
                link(dve.tensor_tensor(lg[:], bank[7][:, 0:GT * E0].rearrange("p (t e) -> p t e", t=GT),
                                       gb_b[:].unsqueeze(1).broadcast_to([P, GT, E0]), ALU.add))
                stands_alone(dve)
                for t in range(GT):
                    last = dve.max(best[:, t, :], lg[:, t, :])
                link(last)
                dve.tensor_copy(top0[:, bass.ds(g * GT, GT), :], best[:, :, 0:K0])
                for t in range(GT):
                    last = dve.max_index(ix[:, t, :], best[:, t, :], lg[:, t, :])
                link(last)
                link(dve.tensor_copy(ixf[:], ix[:, :, 0:K0]))
                for t in range(GT):
                    last = dve.tensor_tensor(oh[:, t], iota_e.unsqueeze(1).broadcast_to([P, K0, E0]),
                                         ixf[:, t, :].unsqueeze(2).broadcast_to([P, K0, E0]), ALU.is_equal)
                link(last)
                link(dve.tensor_reduce(M[:], oh[:].rearrange("p t k e -> p t e k"), AX.X, ALU.add))
                dve.tensor_copy(Mb[:], M[:]).then_inc(s_M, 1)
                link(dve.tensor_reduce(gcnt[:], M[:].rearrange("p t e -> p e t"), AX.X, ALU.add))
                link.end(7)

            def place(grp):
                g, p = grp.g, grp.par
                link = Chain(dve, c_H, g, 16, first=7)
                dve.wait_ge(s_pos, g + 1)
                for t in range(GT):
                    last = dve.tensor_tensor(ohp[:, t], oh[:, t],
                                     bank[7][:, 256 + t * E0:256 + (t + 1) * E0].unsqueeze(1).broadcast_to([P, K0, E0]), ALU.mult)
                link(last)
                dve.sem_inc(s_posr, 1)
                link(dve.tensor_tensor(count[:], count[:], gcnt[:], ALU.add))
                link(dve.tensor_copy(countb[:, 0, :], count[:]))
                link(dve.tensor_reduce(pos[:], ohp[:], AX.X, ALU.add))
                vg = valid[:, bass.ds(g * GT, GT), :]
                link(dve.tensor_scalar(vg, pos[:], float(CAP), None, ALU.is_lt))
                link(dve.tensor_scalar(r0[:], ixf[:], float(CAP), None, ALU.mult))
                link(dve.scalar_tensor_tensor(r1[:], vg, -float(NSLOT0), r0[:], ALU.mult, ALU.add))
                link(dve.scalar_tensor_tensor(sslot[:, p], pos[:], float(NSLOT0), r1[:], ALU.add, ALU.add))
                link(dve.scalar_tensor_tensor(gslot[:, bass.ds(g * GT, GT), :], pos[:], float(CAP - 1), r0[:], ALU.min, ALU.add))
                dve.sem_inc(s_slot, 1)
                link.end()

            steps(dve, [(diagonal, 2), (lambda grp: level(grp, 1, 2), 2), (choose, 4), (post_a, 3), (lambda grp: level(grp, 2, 4), 2),
                        (place, 4), (post_b, 3), (lambda grp: level(grp, 4, 6), 2), (norm_stats, 0), (post_c, 3),
                        (lambda grp: level(grp, 6, 8), 2), (values, 1), (norm, 0)])

            def tokens_in(pair, i):
                dve.wait_ge(s_xsTp, pair + 1)
                dve.tensor_copy(xsT[:, i % 2], bank[7 * (i % 2)][:, 0:P]).then_inc(s_xsT, 1)

            def hidden(pair, i):
                dve.wait_ge(s_h, pair + 1)
                dve.tensor_copy(hs[:, i % 2], bank[1 + i % 2][:]).then_inc(s_hs, 1)

            def turn(pair, i):
                p = i % 2
                dve.wait_ge(s_hTp, pair + 1)
                dve.tensor_tensor(hT[:, p].rearrange("p c (e s) -> p c e s", e=2),
                                  bank[3 + p][:].rearrange("p (c e s) -> p c e s", c=HC, e=2),
                                  b1T[:, bass.ds(2 * pair, 2), :].rearrange("p e c -> p c e").unsqueeze(3).broadcast_to([P, HC, 2, CAP]),
                                  ALU.add).then_inc(s_hT, 1)

            def outputs(pair, i, lap):
                q = i % NQ
                dve.wait_ge(s_yp, pair + 1)
                if not (isinstance(lap, int) and lap == 0):
                    dve.wait_ge(s_yo[q], 16 * lap)
                dve.tensor_tensor(ys[:, q], bank[5 + i % 2][:, 0:P],
                                  b2_b[:, bass.ds(pair, 1)].rearrange("p o d -> p (o d)"), ALU.add).then_inc(s_ys, 1)

            def pairs(lap, left=NPAIR):
                for i in range(NQ):
                    pair = lap * NQ + i
                    turn(pair, i)
                    if i + AHEAD < left:
                        hidden(pair + AHEAD, i + AHEAD)
                    if i + AHEAD + 1 < left:
                        tokens_in(pair + AHEAD + 1, i + AHEAD + 1)
                    outputs(pair, i, lap)

            dve.wait_ge(s_b1, 48)
            tokens_in(0, 0)
            tokens_in(1, 1)
            hidden(0, 0)
            tokens_in(2, 2)
            hidden(1, 1)
            pairs(0)
            with dve.Fori(1, NPAIR // NQ - 1) as lap:
                pairs(lap)
            pairs(NPAIR // NQ - 1, left=NQ)

            link = Chain(dve, c_T, 0, 8)
            for q in range(NQ):
                dve.wait_ge(s_yo[q], 16 * (NPAIR // NQ))
            dve.memset(onerow[:], 1.0)
            dve.memset(ones8[:], 1.0)
            dve.tensor_copy(identb[:], ident)
            for h in range(2):
                dve.tensor_scalar(maskq[:, h], cst[:, 128:256], MASKED, None, ALU.mult)
            dve.memset(count1[:], 0.0)
            dve.memset(count1b[:], 0.0)
            dve.memset(V1[:], 0.0)
            link(dve.tensor_tensor(Y[:, 0], cst[:, 128:256], ident, ALU.add))
            for h in range(2):
                last = dve.tensor_scalar(maskk[:, h], Y[:, 0], -MASKED, MASKED, ALU.mult, ALU.add)
            link(last)
            link(dve.memset(V1[:, :, :, :, HD:HD + 1], 1.0))
            dve.sem_inc(s_pre, 1)
            link(dve.tensor_tensor(gates[:], top0[:], top0[:, :, 0:1].broadcast_to([P, NT, K0]), ALU.subtract))
            dve.sem_inc(s_gsub, 1)
            dve.wait_ge(s_gexp, 1)
            link(dve.tensor_reduce(gsum[:], gates[:], AX.X, ALU.add))
            link(dve.reciprocal(gsum[:], gsum[:]))
            link(dve.tensor_tensor(gates[:], gates[:], gsum[:].unsqueeze(2).broadcast_to([P, NT, K0]), ALU.mult))
            link(dve.tensor_tensor(gates[:], gates[:], valid[:], ALU.mult))
            link.end()
            dve.wait_ge(s_w2c, 16 * 15)

            def combine(grp):
                g, p = grp.g, grp.par
                link = Chain(dve, c_C, g, 5)
                dve.wait_ge(s_gat[p], 16 * GT * K0 * (grp.half + 1))
                for k in range(K0):
                    for t in range(GT):
                        xt = X[:, bass.ds(g * GT + t, 1), :].rearrange("p o d -> p (o d)")
                        gate = gates[:, bass.ds(g * GT + t, 1), k:k + 1].rearrange("p o k -> p (o k)")
                        last = dve.scalar_tensor_tensor(xt, R[:, p, t * K0 + k, :], gate, xt, ALU.mult, ALU.add)
                    link(last)
                dve.sem_inc(s_radd, 1)
                link.end(3)

            def combined_stats(grp):
                link = Chain(dve, c_C, grp.g, 5, first=3)
                variance(3, link, X[:, bass.ds(grp.g * GT, GT), :])
                link.end()

            def combined_norm(grp):
                if after(grp.g, 1):
                    dve.wait_ge(s_xaTp, grp.g)
                normalize(3, grp, X[:, bass.ds(grp.g * GT, GT), :], xa[:]).then_inc(s_xa, 1)

            def rotate(grp, side, bk, src_sem, out_sem, link):
                g = grp.g
                dve.wait_ge(src_sem, g + 1)
                for h in range(2):
                    last = dve.tensor_tensor(rt[:, h].rearrange("p (b t) -> p b t", b=GB),
                                      bank[bk][h * DR:(h + 1) * DR, :].rearrange("p (b t) -> p b t", b=GB),
                                      rope_sb[h * DR:(h + 1) * DR, :].unsqueeze(1).broadcast_to([DR, GB, T]), ALU.mult)
                link(last)
                link(dve.tensor_tensor(rt[:, 0], rt[:, 0], rt[:, 1], ALU.add))
                for r in ((0, 1), (0, 2))[side]:
                    last = dve.tensor_copy(rp[r * DR:(r + 1) * DR, side], rt[:, 0])
                link(last)
                r = (2, 1)[side]
                link(dve.tensor_tensor(rp[r * DR:(r + 1) * DR, side], rt[:, 0], rp[0:DR, side].bitcast(F32), ALU.subtract))
                dve.sem_inc(out_sem, 1)

            def lower(grp, side):
                dve.wait_ge((s_qh, s_kh)[side], grp.g + 1)
                dve.tensor_tensor(qkl[:, side], bank[2][:], qkh[:, side].bitcast(F32), ALU.subtract).then_inc((s_ql, s_kl)[side], 1)

            def rotate_q(grp):
                link = Chain(dve, c_N, grp.g, 8)
                if after(grp.g, 1):
                    for r in range(RD):
                        dve.wait_ge(s_fill[r], 96 * grp.g - 32)
                rotate(grp, 0, 3, s_qr, s_rq, link)
                link.end(4)

            def rotate_k(grp):
                link = Chain(dve, c_N, grp.g, 8, first=4)
                rotate(grp, 1, 3, s_kr, s_rk, link)
                link.end()

            def maxima(grp, i, h):
                u = grp.g * ND + i
                m = mx[:, i % 2]
                dve.wait_ge(s_max, u * 2 + h + 1)
                for c, lo, hi in ((0, P, 2 * P), (1, 2 * P, 4 * P)):
                    last = dve.tensor_reduce(m[:, h, :, c], pairbank[0][:].rearrange("p (b n) -> p b n", b=GB)[:, :, lo:hi], AX.X, ALU.max)
                last.then_inc(s_maxr, 1)
                if h == 1:
                    dve.wait_ge(s_maxr, u * 2 + 2)
                    mm = m.rearrange("p h b c -> p (h b c)")
                    dve.tensor_scalar(ms[:, i % 2, 0:8], mm, -1.0, None, ALU.mult).then_inc(s_ms, 1)
                    dve.wait_ge(s_ms, 2 * u + 1)
                    dve.scalar_tensor_tensor(ms[:, i % 2, 8:16], mm, -1.0, ms[:, i % 2, 0:8].bitcast(F32), ALU.mult, ALU.subtract).then_inc(s_ms, 1)

            def divide(grp, m):
                g = grp.g
                n = g * (ND // 2) + m
                dve.wait_ge(s_rawTp, n + 1)
                if m == 0 and after(g, 1):
                    dve.wait_ge(s_attTp, g)
                v5 = bank[7][:].rearrange("p (u c h b d) -> p u c h b d", u=2, c=2, h=2, b=2)
                dve.reciprocal(rec[:], bank[7][:].rearrange("p (u j d) -> p u j d", u=4, j=4)[:, :, :, HD]).then_inc(s_norm, 1)
                dve.wait_ge(s_norm, 2 * n + 1)
                r5 = rec[:].rearrange("p (u c) (h b) -> p u c h b", u=2, h=2)
                for c in range(2):
                    for b in range(2):
                        h0 = 4 * m * HD
                        last = dve.tensor_tensor(
                            att[:, 2 * b + c, h0:h0 + 4 * HD].rearrange("p (u h d) -> p u h d", u=2, h=2),
                            v5[:, :, c, :, b, 0:HD], r5[:, :, c, :, b].unsqueeze(3).broadcast_to([P, 2, 2, HD]), ALU.mult)
                last.then_inc(s_norm, 1)

            def output_stats(grp):
                g = grp.g
                link = Chain(dve, c_R, g, 3)
                dve.wait_ge(s_wo1, g + 1)
                xt = X[:, bass.ds(g * GT, GT), :]
                link(dve.tensor_tensor(xt, xt, bank[3][:].rearrange("p (t n) -> p t n", t=GT), ALU.add))
                dve.sem_inc(s_x3, 1)
                variance(4, link, xt)
                link.end()

            def output_norm(grp):
                g, p = grp.g, grp.par
                if after(g, 2):
                    dve.wait_ge(s_scat1[p], 16 * GT * K1 * grp.half)
                normalize(4, grp, X[:, bass.ds(g * GT, GT), :], xg[:, p]).then_inc(s_xg, 1)

            def choose1(grp):
                g, p = grp.g, grp.par
                link = Chain(dve, c_Q, g, 11)
                dve.wait_ge(s_lg1, g + 1)
                link(dve.tensor_copy(lg1[:], bank[3][:, 0:GT * E1].rearrange("p (t e) -> p t e", t=GT)))
                stands_alone(dve)
                for t in range(GT):
                    last = dve.max(best1[:, t, :], lg1[:, t, :])
                link(last)
                dve.tensor_copy(gt1[:, bass.ds(g * GT, GT), :], best1[:, :, 0:K1])
                for t in range(GT):
                    last = dve.max_index(ix1[:, t, :], best1[:, t, :], lg1[:, t, :])
                link(last)
                ixg, posg = ixa[:, bass.ds(g * GT, GT), :], posa[:, bass.ds(g * GT, GT), :]
                link(dve.tensor_copy(ixg, ix1[:, :, 0:K1]))
                for t in range(GT):
                    last = dve.tensor_tensor(oh1[:, t], iota_e[:, 0:E1].unsqueeze(1).broadcast_to([P, K1, E1]),
                                         ixa[:, bass.ds(g * GT + t, 1), :].rearrange("p o k -> p (o k)").unsqueeze(2).broadcast_to([P, K1, E1]), ALU.is_equal)
                link(last)
                dve.tensor_tensor(M1b[:], oh1[:, :, 0], oh1[:, :, 1], ALU.add).then_inc(s_M1, 1)
                link(dve.tensor_reduce(gcnt1[:], oh1[:].rearrange("p t k e -> p e (t k)"), AX.X, ALU.add))
                link.end(6)

            def place1(grp):
                g, p = grp.g, grp.par
                link = Chain(dve, c_Q, g, 11, first=6)
                ixg, posg = ixa[:, bass.ds(g * GT, GT), :], posa[:, bass.ds(g * GT, GT), :]
                dve.wait_ge(s_pos1, g + 1)
                for t in range(GT):
                    last = dve.tensor_tensor(ohp1[:, t], oh1[:, t], bank[3][:, 256 + t * E1:256 + (t + 1) * E1].unsqueeze(1).broadcast_to([P, K1, E1]), ALU.mult)
                link(last)
                link(dve.tensor_tensor(count1[:], count1[:], gcnt1[:], ALU.add))
                link(dve.tensor_copy(count1b[:], count1[:]))
                link(dve.tensor_reduce(posg, ohp1[:], AX.X, ALU.add))
                if after(g, 2):
                    dve.wait_ge(s_scat1[p], 16 * GT * K1 * grp.half)
                link(dve.scalar_tensor_tensor(srow1[:, p], ixg, float(REG), posg, ALU.mult, ALU.add))
                dve.sem_inc(s_row1, 1)
                link.end()

            def half(i, h):
                return lambda grp: maxima(grp, i, h)

            def division(m):
                return lambda grp: divide(grp, m)

            more = {1: [(output_stats, 3)], 2: [(lambda grp: lower(grp, 0), 1), (rotate_q, 1)],
                    3: [(lambda grp: lower(grp, 1), 1), (rotate_k, 1)], 4: [(output_norm, 3), (combine, 0)],
                    5: [(combined_stats, 0)], 6: [(choose1, 3), (combined_norm, 0)], 7: [(place1, 3)]}
            slots_of = []
            for i in range(ND):
                k, lag = next_duo(i, 2)
                slots_of.append((half(k, 0), lag))
                if i % 2 == 0:
                    slots_of.append((division((i // 2 - 1) % (ND // 2)), 2 if i else 3))
                slots_of.append((half(k, 1), lag))
                slots_of += more.get(i, [])
            steps(dve, slots_of)

            link = Chain(dve, c_T, 0, 33, base=8)
            link(dve.tensor_tensor(gw1[:], gt1[:], gt1[:, :, 0:1].broadcast_to([P, NT, K1]), ALU.subtract))
            dve.sem_inc(s_gsub, 1)
            dve.wait_ge(s_tot, 1)
            link(dve.tensor_copy(ntile[:], bank[0][:, 0:E1]))
            link(dve.tensor_tensor(cmp1[:], ntile[:].unsqueeze(2).broadcast_to([P, E1, NT]),
                                   iota128.unsqueeze(1).broadcast_to([P, E1, NT]), ALU.is_gt))
            link(dve.tensor_reduce(ntile[:], cmp1[:], AX.X, ALU.add))
            link(dve.tensor_tensor_scan(tend[:], ones8[:], ntile[:], 0.0, ALU.mult, ALU.add))
            link(dve.tensor_tensor(tbase[:], tend[:], ntile[:], ALU.subtract))
            link(dve.tensor_scalar(tbase[:], tbase[:], float(P), None, ALU.mult))
            link(dve.tensor_scalar(tw[:], ntile[:], -float(P), float(REG), ALU.mult, ALU.add))
            link(dve.tensor_tensor(cmp2[:], tend[:].unsqueeze(1).broadcast_to([P, ND1, E1]),
                                   iota_t.unsqueeze(2).broadcast_to([P, ND1, E1]), ALU.is_le))
            link(dve.tensor_tensor(cmp3[:], cmp2[:], tw[:].unsqueeze(1).broadcast_to([P, ND1, E1]), ALU.mult))
            dve.tensor_reduce(tl[:, 0], cmp2[:], AX.X, ALU.add)
            link(dve.tensor_reduce(tl[:, 1], cmp3[:], AX.X, ALU.add))
            link(dve.scalar_tensor_tensor(tl[:, 1], iota_t, float(P), tl[:, 1], ALU.mult, ALU.add))
            dve.tensor_scalar(tli[:, 0], tl[:, 0], float(E1 - 1), None, ALU.min)
            link(dve.tensor_scalar(tli[:, 1], tl[:, 1], float(E1 * REG - P), None, ALU.min))
            dve.sem_inc(s_tiles, 1)
            tmp = gw1
            dve.wait_ge(s_gexp, 2)
            for e in range(E1):
                link(dve.tensor_scalar(tmp[:], ixa[:], float(e), tbase[:, e:e + 1], ALU.is_equal, ALU.mult))
                link(dve.tensor_tensor(posa[:], posa[:], tmp[:], ALU.add))
            link(dve.tensor_copy(grow1[:], posa[:]))
            link(dve.tensor_tensor(gsum[:], gt1[:, :, 0], gt1[:, :, 1], ALU.add))
            link(dve.reciprocal(gsum[:], gsum[:]))
            link(dve.tensor_tensor(gw1[:], gt1[:], gsum[:].unsqueeze(2).broadcast_to([P, NT, K1]), ALU.mult))
            dve.sem_inc(s_tiles, 1)
            link.end()

            def d_act(t, p):
                dve.wait_ge(s_sg, t + 1)
                dve.tensor_tensor(ac[:, p], bank[2 + p][:, 0:F1], sg[:, p], ALU.mult).then_inc(s_ac, 1)

            def d_turn(t, p):
                dve.wait_ge(s_acTp, t + 1)
                dve.tensor_copy(acT[:, p], bank[4 + p][:, 0:F1]).then_inc(s_acT, 1)

            def lap_of(lap, left=ND1):
                for q in range(NQ1):
                    d_turn(lap * NQ1 + q, q % 2)
                    if q + AHEAD < left:
                        d_act(lap * NQ1 + q + AHEAD, q % 2)

            d_act(0, 0)
            d_act(1, 1)
            with dve.Fori(0, ND1 // NQ1 - 1) as lap:
                lap_of(lap)
            lap_of(ND1 // NQ1 - 1, left=NQ1)

            def final(g, p, half):
                dve.wait_ge(s_gat[p], 16 * GT * (K0 * (NG // 2) + K1 * (half + 1)))
                for k in range(K1):
                    for t in range(GT):
                        xt = X[:, bass.ds(g * GT + t, 1), :].rearrange("p o d -> p (o d)")
                        gate = gw1[:, bass.ds(g * GT + t, 1), k:k + 1].rearrange("p o k -> p (o k)")
                        last = dve.scalar_tensor_tensor(xt, R[:, p, t * K1 + k, :], gate, xt, ALU.mult, ALU.add)
                    if k < K1 - 1:
                        last.then_inc(s_fin1, 1)
                        dve.wait_ge(s_fin1, g + 1)
                last.then_inc(s_fin, 1)

            with dve.Fori(0, NG // 2) as j:
                for p in range(2):
                    final(2 * j + p, p, j)

        @block.tensor
        def _(pe):
            pe.wait_ge(s_const, 16 * NCONST)
            pe.wait_ge(s_tri, 1)



            def norm_in(grp):
                g, p = grp.g, grp.par
                pe.wait_ge(s_xn, g + 1)
                if after(g, 1):
                    pe.wait_ge(s_qe, g)
                for t in range(GT):
                    last = pe.transpose(bank[0][:, t * P:(t + 1) * P], xn[:, p, t, :], ident)
                last.then_inc(s_xnTp, 1)

            def queries_keys(grp):
                g = grp.g
                pe.wait_ge(s_xnT, g + 1)
                if after(g, 1):
                    pe.wait_ge(s_ge, g)
                pe.matmul(bank[1][:], wq_sb[:], xnT[:], start=True, stop=True).then_inc(s_q, 1)
                pe.matmul(bank[0][:], wk_sb[:], xnT[:], start=True, stop=True).then_inc(s_k, 1)

            def state_values(grp):
                if after(grp.g, 1):
                    pe.wait_ge(s_ve_, grp.g)
                for t in range(GT):
                    last = pe.matmul(bank[3][:, t * P:(t + 1) * P], xnT[:, t * P:(t + 1) * P], wv_sb[:], start=True, stop=True)
                last.then_inc(s_v, 1)

            def gate(grp):
                pe.wait_ge(s_qe, grp.g + 1)
                pe.matmul(bank[1][:], wg_sb[:], xnT[:], start=True, stop=True).then_inc(s_g, 1)

            def level(grp, lo, hi):
                g, p = grp.g, grp.par
                for lv in range(lo, hi):
                    if lv == 0:
                        pe.wait_ge(s_ge, g + 1)
                    else:
                        pe.wait_ge(s_upd, g * NLP + lv)
                    if lv >= 2:
                        pe.wait_ge(s_aev, g * NLP + lv - 1)
                    for t in range(GT):
                        last = pe.matmul(bank[2 if lv % 2 else 6][:, t * P:(t + 1) * P], K[:, p, t * P:(t + 1) * P],
                                         Q[:, p, t * P:(t + 1) * P], start=True, stop=True)
                    last.then_inc(s_lev, 1)

            def cross(grp):
                g, p = grp.g, grp.par
                pe.wait_ge(s_upd, (g + 1) * NLP)
                if after(g, 1):
                    pe.wait_ge(s_y, g)
                for b in range(GB):
                    last = pe.matmul(bank[4][:, b * P:(b + 1) * P], K[:, p, 2 * b * P:(2 * b + 1) * P],
                                     Q[:, p, (2 * b + 1) * P:(2 * b + 2) * P], start=True, stop=True)
                last.then_inc(s_cross, 1)

            def attended(grp):
                g, p = grp.g, grp.par
                pe.wait_ge(s_ve_, g + 1)
                pe.wait_ge(s_axt, g + 1)
                pe.wait_ge(s_aev, (g + 1) * NLP)
                for b in range(GB):
                    v0, v1 = V[:, p, 2 * b], V[:, p, 2 * b + 1]
                    o0, o1 = (bank[5][:, (2 * b + s) * P:(2 * b + s + 1) * P] for s in range(2))
                    pe.matmul(o0, v0, AD[:, 2 * b * P:(2 * b + 1) * P], start=True, stop=True)
                    pe.matmul(o1, v0, AXT[:, b], start=True, stop=False)
                    last = pe.matmul(o1, v1, AD[:, (2 * b + 1) * P:(2 * b + 2) * P], start=False, stop=True)
                last.then_inc(s_av, 1)

            def output(grp):
                pe.wait_ge(s_ot, grp.g + 1)
                for t in range(GT):
                    last = pe.matmul(bank[4][:, t * P:(t + 1) * P], OT[:, t * P:(t + 1) * P], wo_sb[:], start=True, stop=True)
                last.then_inc(s_wo, 1)

            def router_in0(grp):
                g, p = grp.g, grp.par
                pe.wait_ge(s_xf, g + 1)
                if after(g, 1):
                    pe.wait_ge(s_posr, g)
                for t in range(GT):
                    last = pe.transpose(bank[7][:, t * P:(t + 1) * P], xf[:, p, t, :], ident)
                last.then_inc(s_xfTp, 1)

            def logits0(grp):
                pe.wait_ge(s_xfT, grp.g + 1)
                for t in range(GT):
                    last = pe.matmul(bank[7][:, t * E0:(t + 1) * E0], xfT[:, t * P:(t + 1) * P], gw_sb[:], start=True, stop=True)
                last.then_inc(s_lg, 1)

            def earlier0(grp):
                g = grp.g
                pe.wait_ge(s_M, g + 1)
                if after(g, 1):
                    pe.wait_ge(s_slot, g)
                for t in range(GT):
                    dst = bank[7][:, 256 + t * E0:256 + (t + 1) * E0]
                    pe.matmul(dst, tri[:], Mb[:, t], start=True, stop=False)
                    for u in range(t):
                        pe.matmul(dst, ones[:], Mb[:, u], start=False, stop=False)
                    last = pe.matmul(dst, ones[:], countb[:, 0], start=False, stop=True)
                last.then_inc(s_pos, 1)

            def lev(lo, hi):
                return lambda grp: level(grp, lo, hi), 2

            steps(pe, [(router_in0, 4), (attended, 3), lev(0, 1), (logits0, 4), (norm_in, 1), (output, 3), lev(1, 2),
                       (queries_keys, 1), lev(2, 3), (earlier0, 4), lev(3, 4), (state_values, 1), lev(4, 5), (gate, 1),
                       lev(5, 8), (cross, 2)])

            def tokens_in(pair, i, lap):
                p, q = i % 2, i % NQ
                pe.wait_ge(s_xs[q], 16 * (lap * (PAIRS // NQ) + i // NQ + 1))
                pe.transpose(bank[7 * p][:, 0:P], xs[:, q, :], ident).then_inc(s_xsTp, 1)

            def hidden(pair, i, lap):
                p = i % 2
                pe.wait_ge(s_w[i], 32 * (lap + 1))
                pe.wait_ge(s_xsT, pair + 1)
                for h in range(2):
                    last = pe.matmul(bank[1 + p][h * CAP:(h + 1) * CAP, :], xsT[:, p, h * CAP:(h + 1) * CAP],
                                     w1r[:, 2 * i + h, :], start=True, stop=True)
                last.then_inc(s_h, 1)

            def turn(pair, i):
                p = i % 2
                pe.wait_ge(s_hs, pair + 1)
                for c in range(HC):
                    last = pe.transpose(bank[3 + p][:, c * P:(c + 1) * P], hs[:, p, c * P:(c + 1) * P], ident)
                last.then_inc(s_hTp, 1)

            def outputs(pair, i, first=False):
                p = i % 2
                pe.wait_ge(s_gT, pair + 1)
                if not first:
                    pe.wait_ge(s_ys, pair - 1)
                for h in range(2):
                    for c in range(HC):
                        last = pe.matmul(bank[5 + p][h * CAP:(h + 1) * CAP, 0:P], gT[:, p, c, h * CAP:(h + 1) * CAP],
                                         w2r[:, 2 * i + h, c, :], start=(c == 0), stop=(c == HC - 1))
                last.then_inc(s_yp, 1)

            def ahead(lap, i, n):
                return (i + n) % PAIRS, lap + (i + n) // PAIRS

            def pairs(lap, last_lap=False, first_lap=False):
                for i in range(PAIRS):
                    pair = lap * PAIRS + i
                    turn(pair, i)
                    if not (last_lap and i + AHEAD >= PAIRS):
                        hidden(pair + AHEAD, *ahead(lap, i, AHEAD))
                    if not (last_lap and i + AHEAD + 1 >= PAIRS):
                        tokens_in(pair + AHEAD + 1, *ahead(lap, i, AHEAD + 1))
                    outputs(pair, i, first_lap and i < 2)

            tokens_in(0, 0, 0)
            tokens_in(1, 1, 0)
            hidden(0, 0, 0)
            tokens_in(2, 2, 0)
            hidden(1, 1, 0)
            pairs(0, first_lap=True)
            with pe.Fori(1, NROUND - 1) as lap:
                pairs(lap)
            pairs(NROUND - 1, last_lap=True)

            pe.wait_ge(s_w2c, 16 * 15)
            pe.wait_ge(s_pre, 1)
            pe.wait_ge(s_ones1, 32)

            def norm1_in(grp):
                g = grp.g
                pe.wait_ge(s_xa, g + 1)
                if after(g, 1):
                    pe.wait_ge(s_v1, g)
                for t in range(GT):
                    last = pe.transpose(bank[2][:, t * P:(t + 1) * P], xa[:, t, :], ident)
                last.then_inc(s_xaTp, 1)

            def latent(grp):
                pe.wait_ge(s_xaT, grp.g + 1)
                pe.matmul(bank[2][:], wkvd_sb[:], xaT[:], start=True, stop=True).then_inc(s_ckvp, 1)

            def own_q(grp):
                g = grp.g
                pe.wait_ge(s_ckv, g + 1)
                pe.matmul(bank[2][:], wq1_sb[:], xaT[:], start=True, stop=True).then_inc(s_q1p, 1)
                if after(g, 2):
                    pe.wait_ge(s_x3, g - 1)
                pe.matmul(bank[3][0:2 * DR, :], wqr_sb[:], xaT[:], start=True, stop=True).then_inc(s_qr, 1)

            def own_k(grp):
                g = grp.g
                pe.wait_ge(s_ql, g + 1)
                pe.matmul(bank[2][:], wku_sb[:], ckvT[:], start=True, stop=True).then_inc(s_kp, 1)
                pe.wait_ge(s_rq, g + 1)
                pe.matmul(bank[3][0:2 * DR, :], wkr_sb[:], ckvT[:], start=True, stop=True).then_inc(s_kr, 1)

            def own_v(grp):
                pe.wait_ge(s_kl, grp.g + 1)
                for t in range(GT):
                    last = pe.matmul(bank[2][:, t * P:(t + 1) * P], ckvT[:, t * P:(t + 1) * P], wvu_sb[:], start=True, stop=True)
                last.then_inc(s_v1p, 1)

            def max_scores(grp, i, h):
                g, r = grp.g, i % RD
                u = g * ND + i
                if h == 0:
                    pe.wait_ge(s_fill[r], 96 * g + (64 if i < RD else 96))
                if h or i or after(g, 1):
                    pe.wait_ge(s_maxr, 2 * u + h)
                for b in range(GB):
                    bk = bank[b]
                    keys = SK[0:KM, 2 * r + h, :].rearrange("p (b c n) -> p b c n", b=GB, c=2)[:, b, ::-1, :]
                    for c in range(2):
                        n0 = (2 * b + c) * P
                        pe.matmul(bk[:, c * 2 * P:(c + 1) * 2 * P], SQ[0:KM, 2 * r + h, n0:n0 + P], keys,
                                  start=(c == 0), stop=False, skip_group_check=True)
                    last = pe.matmul(bk[:, P:3 * P], identb[:], maskq[:].rearrange("p a b -> p (a b)"), start=False, stop=True,
                                     skip_group_check=True)
                last.then_inc(s_max, 1)

            def turn_maxima(grp, i):
                g = grp.g
                u = g * ND + i
                pe.wait_ge(s_ms, 2 * u + 2)
                if i or after(g, 1):
                    pe.wait_ge(s_mT, u)
                if i >= 4 or after(g, 1):
                    pe.wait_ge(s_norm, 2 * turned_pairs(g, i))
                pe.transpose(bank[7][0:16, 0:P], ms[:, i % 2, :].bitcast(F32), ident).then_inc(s_mTp, 1)

            def scores(grp, i, n):
                g, r = grp.g, i % RD
                h, b = n // 2, n % 2
                k = (g * ND + i) * 4 + n
                if n >= 2 or i >= 1 or after(g, 1):
                    pe.wait_ge(s_exp, k - 1)
                if n == 0:
                    pe.wait_ge(s_shift[r], 64 * g + (32 if i < RD else 64))
                bk = bank[4 + n % 2]
                q = SQ[0:KS, 2 * r + h, b * T:(b + 1) * T]
                k1, k0 = (SK[0:KS, 2 * r + h, b * T + c * P:b * T + (c + 1) * P] for c in (1, 0))
                pe.matmul(bk[:, 0:2 * P], k1, q, start=True, stop=False, skip_group_check=True)
                pe.matmul(bk[:, 2 * P:4 * P], k0, q, start=False, stop=False, skip_group_check=True)
                last = pe.matmul(bk[:, P:3 * P], identb[:], maskk[:].rearrange("p a b -> p (a b)"), start=False, stop=True, skip_group_check=True)
                last.then_inc(s_st, 1)

            def values(grp, i):
                g, p = grp.g, grp.par
                pe.wait_ge(s_exp, (g * ND + i + 1) * 4)
                if i == 0:
                    pe.wait_ge(s_v1, g + 1)
                if i % 2 == 0 and (i or after(g, 1)):
                    pe.wait_ge(s_raw, g * (ND // 2) + i // 2)
                c0 = (i % 2) * T
                for n in range(4):
                    h, b = n // 2, n % 2
                    pe.matmul(bank[6][32 * n:32 * n + 32, c0:c0 + T], V1[:, p, 2 * b, 2 * i + h, :], PT[:, i % 2, n, P:3 * P],
                              start=True, stop=False, tile_position=(0, 32 * n), skip_group_check=True)
                for n in range(4):
                    h, b = n // 2, n % 2
                    last = pe.matmul(bank[6][32 * n:32 * n + 32, c0 + P:c0 + T], V1[:, p, 2 * b + 1, 2 * i + h, :], PT[:, i % 2, n, 0:P],
                              start=False, stop=True, tile_position=(0, 32 * n), skip_group_check=True)
                if i % 2:
                    last.then_inc(s_pv, 1)

            def turn_values(grp, m):
                g = grp.g
                n = g * (ND // 2) + m
                pe.wait_ge(s_raw, n + 1)
                pe.wait_ge(s_mT, g * ND + (2 * m + 4 if m < 3 or within(g, NG - 1) else ND))
                if m or after(g, 1):
                    pe.wait_ge(s_norm, 2 * n)
                for c in range(4):
                    last = pe.transpose(bank[7][:, c * P:(c + 1) * P], raw[:, c * P:(c + 1) * P], ident)
                last.then_inc(s_rawTp, 1)

            def attended_in(grp):
                g = grp.g
                pe.wait_ge(s_norm, 2 * (g + 1) * (ND // 2))
                if after(g, 1):
                    pe.wait_ge(s_row1, g)
                for t in range(GT):
                    last = pe.transpose(bank[3][:, t * P:(t + 1) * P], att[:, t, :], ident)
                last.then_inc(s_attTp, 1)

            def output1(grp):
                pe.wait_ge(s_attT, grp.g + 1)
                for t in range(GT):
                    last = pe.matmul(bank[3][:, t * P:(t + 1) * P], attT[:, t * P:(t + 1) * P], wo1_sb[:], start=True, stop=True)
                last.then_inc(s_wo1, 1)

            def router_in(grp):
                g, p = grp.g, grp.par
                pe.wait_ge(s_xg, g + 1)
                pe.wait_ge(s_rk, g + 3 if within(g, NG - 2) else NG)
                for t in range(GT):
                    last = pe.transpose(bank[3][:, t * P:(t + 1) * P], xg[:, p, t, :], ident)
                last.then_inc(s_xgTp, 1)

            def logits1(grp):
                pe.wait_ge(s_xgT, grp.g + 1)
                for t in range(GT):
                    last = pe.matmul(bank[3][:, t * E1:(t + 1) * E1], xgT[:, t * P:(t + 1) * P], wr_sb[:], start=True, stop=True)
                last.then_inc(s_lg1, 1)

            def earlier1(grp):
                g = grp.g
                pe.wait_ge(s_M1, g + 1)
                if after(g, 1):
                    pe.wait_ge(s_row1, g)
                for t in range(GT):
                    dst = bank[3][:, 256 + t * E1:256 + (t + 1) * E1]
                    pe.matmul(dst, tri[:], M1b[:, t], start=True, stop=False)
                    for u in range(t):
                        pe.matmul(dst, ones[:], M1b[:, u], start=False, stop=False)
                    last = pe.matmul(dst, ones[:], count1b[:], start=False, stop=True)
                last.then_inc(s_pos1, 1)

            def some_scores(i, lo, hi):
                def stage(grp):
                    for n in range(lo, hi):
                        scores(grp, i, n)
                return stage, 2

            def on(i, n, stage, *args):
                k, lag = next_duo(i, n)
                return lambda grp: stage(grp, k, *args), lag

            more = {0: [(norm1_in, 1), (attended_in, 3)], 1: [(latent, 1), (output1, 3)], 2: [(own_q, 1)], 3: [(own_k, 1)],
                    4: [(own_v, 1)], 5: [(router_in, 3)], 6: [(logits1, 3)], 7: [(earlier1, 3)]}
            slots_of = []
            for i in range(ND):
                slots_of += [some_scores(i, 0, 2), on(i, 1, turn_maxima), on(i, 2, max_scores, 0), some_scores(i, 2, 4),
                             on(i, 0, values)]
                if i % 2 == 0:
                    slots_of.append(((lambda m: lambda grp: turn_values(grp, m))((i // 2 - 1) % (ND // 2)), 2 if i else 3))
                slots_of += [on(i, 2, max_scores, 1)] + more[i]
            steps(pe, slots_of)

            pe.wait_ge(s_row1, NG)
            pe.matmul(bank[0][:, 0:E1], ones[:], count1b[:], start=True, stop=True).then_inc(s_tot, 1)

            pe.wait_ge(s_w2c, 16 * 15)
            pe.wait_ge(s_tiles, 1)

            def d_in(t, q, lap):
                p = q % 2
                pe.wait_ge(s_xs[q], 16 * (NPAIR // NQ + lap + 1))
                pe.transpose(bank[p][:, 0:P], xd[:, q, :], ident).then_inc(s_xsTp, 1)

            def d_hidden(t, p, e):
                pe.wait_ge(s_xsT, NPAIR + t + 1)
                pe.matmul(bank[2 + p][:], xdT[:, p], w1d[:, bass.ds(e, 1), :].rearrange("p o n -> p (o n)"), start=True, stop=True
                          ).then_inc(s_h, 1)

            def d_turn(t, p):
                pe.wait_ge(s_ac, t + 1)
                for c in range(2):
                    last = pe.transpose(bank[4 + p][:, c * P:(c + 1) * P], ac[:, p, c * P:(c + 1) * P], ident)
                last.then_inc(s_acTp, 1)

            def d_out(t, p, e, first):
                pe.wait_ge(s_acT, t + 1)
                if not first:
                    pe.wait_ge(s_yd, t - 1)
                for c in range(2):
                    last = pe.matmul(bank[6 + p][:, 0:P], acT[:, p, c * P:(c + 1) * P],
                                     w2d[:, bass.ds(e, 1), c, :].rearrange("p o n -> p (o n)"), start=(c == 0), stop=(c == 1))
                last.then_inc(s_ydp, 1)

            def expert(t):
                return pe.value_load(tli[0:1, 0, bass.ds(t, 1)], min_val=0, max_val=E1 - 1)

            def lap_of(lap, first=False, left=ND1):
                base = lap * LAP1
                experts = [expert(base + q) for q in range(AHEAD + 1)]
                for q in range(LAP1):
                    t, p = base + q, q % 2
                    d_turn(t, p)
                    if q + AHEAD < left:
                        d_hidden(t + AHEAD, p, experts[q + AHEAD])
                    if q + AHEAD + 1 < left:
                        d_in(t + AHEAD + 1, (q + AHEAD + 1) % NQ1, lap * (LAP1 // NQ1) + (q + AHEAD + 1) // NQ1)
                        if q + 1 < LAP1:
                            experts.append(expert(t + AHEAD + 1))
                    d_out(t, p, experts[q], first and q < 2)

            d_in(0, 0, 0)
            d_in(1, 1, 0)
            d_hidden(0, 0, expert(0))
            d_in(2, 2, 0)
            d_hidden(1, 1, expert(1))
            lap_of(0, first=True)
            with pe.Fori(1, ND1 // LAP1 - 1) as lap:
                lap_of(lap)
            lap_of(ND1 // LAP1 - 1, left=LAP1)


def constants():
    cst = np.zeros((P, 2 * P + E0 + ND1 + NT), np.float32)
    cst[:, 0:P] = np.eye(P)
    cst[:, P:2 * P] = np.triu(np.ones((P, P)), 1)
    cst[:, 2 * P:2 * P + E0] = np.arange(E0)
    cst[:, 2 * P + E0:2 * P + E0 + ND1] = np.arange(ND1)
    cst[:, 2 * P + E0 + ND1:] = np.arange(NT) * P
    masks = np.zeros((P, NL, P // 2), np.float32)
    for level, m in enumerate(LEVELS):
        j = np.arange(P)[:, None]
        i = np.array([i for i in range(P) if i // m % 2 == 1])[None]
        masks[:, level] = (j // m % 2 == 0) & (i // m == j // m + 1)
    inv = (1.0 / 10000.0 ** (np.arange(0, DR, 2, dtype=np.float32) / np.float32(DR))).astype(np.float32)
    angle = np.outer(np.arange(T, dtype=np.float32), inv).astype(np.float32)
    cos, sin = np.cos(angle).T, np.sin(angle).T
    rope = np.ascontiguousarray(np.concatenate([cos, cos, -sin, sin], 0).astype(np.float32))
    return {"const": cst, "masks": masks.reshape(P, -1), "rope": rope}


def layout(a):
    def by_dim(w):
        return w.reshape(P, NH, HD).transpose(0, 2, 1).reshape(P, NH * HD)

    out = {"x": a["L0_attn_x"].reshape(NTOK, P)}
    for n in ("Wq", "bq", "Wk", "bk", "Wv", "bv", "Wg", "bg", "Wo", "bo", "gamma", "beta"):
        out[n] = a["L0_attn_" + n]
    for n in ("gate_w", "gate_b", "w1", "w2", "b2"):
        out[n] = a["L0_ffn_" + n]
    out["b1t"] = a["L0_ffn_b1"].reshape(E0, HC, P).transpose(2, 0, 1).reshape(P, E0 * HC)
    out["Wkvd"] = a["L1_attn_W_kv_down"]
    out["Wku"] = by_dim(a["L1_attn_W_k_up"])
    out["Wvu"] = a["L1_attn_W_v_up"]
    out["Wq1"] = by_dim(a["L1_attn_W_q"])
    out["Wqr"] = a["L1_attn_W_q_rope"]
    out["Wkr"] = a["L1_attn_W_k_rope"]
    out["Wo1"] = a["L1_attn_W_o"]
    out["Wr"] = a["L1_ffn_Wr"].T
    out["W1t"] = a["L1_ffn_W1"].transpose(2, 0, 1).reshape(P, E1 * 2 * F1)
    out["W2t"] = a["L1_ffn_W2"].reshape(E1, P, 2, F1 // 2).transpose(3, 0, 2, 1).reshape(P, E1 * F1)
    return {n: np.ascontiguousarray(v) for n, v in out.items()}


def kernel(**inputs):
    import concourse.bacc as bacc
    from concourse.bass_utils import run_bass_kernel_spmd

    nc = bacc.Bacc("TRN2", target_bir_lowering=False, num_devices=1)
    arrays = {**layout({n: np.asarray(a) for n, a in inputs.items()}), **constants()}
    args = {n: nc.dram_tensor(n, a.shape, mybir.dt.from_np(a.dtype), kind="ExternalInput").ap() for n, a in arrays.items()}
    out = nc.dram_tensor("out", [NTOK, P], F32, kind="ExternalOutput").ap()
    build(nc, out=out, **args)
    r = run_bass_kernel_spmd(nc, [arrays], core_ids=[0])
    return r.results[0]["out"].reshape(B, T, P)
```

```python
from contextlib import ExitStack

import numpy as np

import concourse.bass as bass
from concourse import mybir

ALU = mybir.AluOpType
ACT = mybir.ActivationFunctionType
AX = mybir.AxisListType
F32 = mybir.dt.float32
BF16 = mybir.dt.bfloat16
U32 = mybir.dt.uint32
U8 = mybir.dt.uint8

P = 128
B, T = 16, 256
NTOK = B * T
NT = NTOK // P
GT = 4
GN = GT * P
NG = NT // GT
GB = GN // T
LEVELS = [1, 2, 4, 8, 16, 32, 64]
NL = len(LEVELS)
EPS = 1e-5
NLP = NL + 1
NCONST = 4

E0, K0, CAP, H0 = 64, 3, 64, 512
HC = H0 // P
NSLOT0 = E0 * CAP
RING = 16
NPAIR = E0 // 2
NH, HD, DR = 16, 8, 32
SCORE_SCALE = float(1.0 / np.sqrt(HD + DR))
ND = NH // 2
RD = 4
KR = 3 * DR
KN = 3 * HD
KM = KR + KN
KS = KM + 2
MASKED = -1e30
E1, K1, F1 = 8, 2, 256
REG = NTOK
ND1 = NTOK * K1 // P + E1
ND1 = (ND1 + 7) // 8 * 8
LAP1 = 8
NQ1 = 4
AHEAD = 2
F32R = mybir.dt.float32r
NROUND = E0 // RING
PX = P + 1
NPLACE = NTOK * K1
PAIRS = RING // 2
NQ = 4


class Chain:

    def __init__(self, eng, sem, group, n, base=0, first=0):
        self.eng, self.sem, self.base, self.n, self.k = eng, sem, group * n + base, n, first

    def __call__(self, ins):
        self.k += 1
        ins.then_inc(self.sem, 1)
        self.eng.wait_ge(self.sem, self.base + self.k)

    def end(self, last=None):
        last = self.n if last is None else last
        assert self.k == last, (self.k, last)


def after(g, n):
    return not isinstance(g, int) or g >= n


def within(g, n):
    return not isinstance(g, int) or g < n


class Group:

    def __init__(self, j, p, k):
        self.par, self.half = (p - k) % 2, j + (p - k) // 2
        self.g = self.half * 2 + self.par


def steps(eng, stages):
    lags = 1 + max(k for _, k in stages)

    def step(j, p, there):
        for stage, k in stages:
            if there(k):
                stage(Group(j, p, k))

    full = lags // 2
    for s in range(2 * full):
        step(s // 2, s % 2, lambda k: 0 <= s - k)
    with eng.Fori(full, NG // 2) as j:
        for p in range(2):
            step(j, p, lambda k: True)
    for s in range(NG, NG + lags - 1):
        step(s // 2, s % 2, lambda k: s - k < NG)


def next_duo(i, n):
    return ((i + n) % ND, 2 if i + n < ND else 1)


def turned_pairs(g, i):
    return g * (ND // 2) + i // 2 - 1


def build(nc, x, first_w, first_b, w1, b1t, w2, b2, second_w, W1t, W2t, out, const, masks, rope):
    with ExitStack() as ctx:
        def sb(name, shape, dt=F32):
            return ctx.enter_context(nc.sbuf_tensor("sb_" + name, shape, dt))

        def sem(name):
            return ctx.enter_context(nc.semaphore(name))

        slots_in = nc.dram_tensor("slots_in", [NSLOT0, P], F32).ap()
        slots_out = nc.dram_tensor("slots_out", [NSLOT0, P], F32).ap()
        parts = nc.dram_tensor("parts", [2, 2, KN, NH, GN], F32).ap()
        rows1_in = nc.dram_tensor("rows1_in", [E1 * REG, PX], F32).ap()
        rows1_out = nc.dram_tensor("rows1_out", [NPLACE, P], F32).ap()

        pairbank = [ctx.enter_context(nc.psum_tensor(f"banks{i}", [P, 1024], F32)) for i in range(2)]
        bank = [pairbank[i // 2][:, i % 2 * 512:(i % 2 + 1) * 512] for i in range(4)]
        bank += [ctx.enter_context(nc.psum_tensor(f"bank{i}", [P, 512], F32)) for i in range(4, 8)]

        X = sb("X", [P, NT, P])
        cst = sb("cst", [P, 2 * P + E0 + ND1 + (1 + K1) * NT])
        iota_t = cst[:, 2 * P + E0:2 * P + E0 + ND1]
        iota128 = cst[:, 2 * P + E0 + ND1:2 * P + E0 + ND1 + NT]
        places = cst[:, 2 * P + E0 + ND1 + NT:].rearrange("p (k t) -> p k t", k=K1)
        ident = cst[:, 0:128]
        iota_e = cst[:, 256:320]
        mask_sb = sb("mask_sb", [P, NL, GT, P // 2], U8)
        tri = sb("tri", [P, P], BF16)
        ones = sb("ones", [P, P], BF16)
        wa = sb("wa", [P, 5 * P + E0 + 3])
        wq_sb, wk_sb, wg_sb, wv_sb, wo_sb = (wa[:, i * P:(i + 1) * P] for i in range(5))
        gw_sb = wa[:, 5 * P:5 * P + E0]
        bq_c, bk_c, bg_c = (wa[:, 5 * P + E0 + i:5 * P + E0 + i + 1] for i in range(3))
        ba = sb("ba", [P, 4 * P + E0])
        bv_b, bo_b, gamma_b, beta_b = (ba[:, i * P:(i + 1) * P] for i in range(4))
        gb_b = ba[:, 4 * P:]
        mhalf = sb("mhalf", [P, GT])
        zrow = sb("zrow", [P, 8 * PX])
        top0 = sb("top0", [P, NT, K0])
        gslot = sb("gslot", [P, NT, K0], U32)
        valid = sb("valid", [P, NT, K0])
        count = sb("count", [P, E0])
        countb = sb("countb", [P, 2, E0], BF16)

        Y = sb("Y", [P, GT, P])
        st = sb("st", [P, 5, GT, 6])
        mv = sb("mv", [P, 5, GT, 2])
        ve = sb("ve", [P, 5, GT])
        rs = sb("rs", [P, 5, GT])

        early = ExitStack()

        def eb(name, shape, dt=F32):
            return early.enter_context(nc.sbuf_tensor("sb_" + name, shape, dt))

        xn = eb("xn", [P, 2, GT, P])
        xb = eb("xb", [P, 2, GT, P])
        xnT = eb("xnT", [P, GN])
        Q = eb("Q", [P, 2, GN])
        K = eb("K", [P, 2, GN])
        G = eb("G", [P, 2, GN])
        V = eb("V", [P, 2, GT, P])
        AD = eb("AD", [P, 2, GN])
        AXT = eb("AXT", [P, GB, P])
        OT = eb("OT", [P, GN])
        xf = eb("xf", [P, 2, GT, P])
        xfT = eb("xfT", [P, GN])
        Tm = [eb(f"T{m}", [P, GN // m]) for m in LEVELS[1:]]
        mask_in = eb("mask_in", [P, NL, P // 2])
        lg = eb("lg", [P, GT, E0])
        best = eb("best", [P, GT, 8])
        ix = eb("ix", [P, GT, 8], U32)
        ixf = eb("ixf", [P, GT, K0])
        oh = eb("oh", [P, GT, K0, E0])
        M = eb("M", [P, GT, E0])
        Mb = eb("Mb", [P, GT, E0], BF16)
        ohp = eb("ohp", [P, GT, K0, E0])
        pos = eb("pos", [P, GT, K0])
        r0 = eb("r0", [P, GT, K0])
        r1 = eb("r1", [P, GT, K0])
        r2 = eb("r2", [P, GT, K0])
        gcnt = eb("gcnt", [P, E0])
        sslot = eb("sslot", [P, 2, GT, K0], U32)

        w1r = eb("w1r", [P, RING, H0])
        w2r = eb("w2r", [P, RING, HC, P])
        xs = eb("xs", [P, NQ, P])
        xsT = eb("xsT", [P, 2, P])
        hs = eb("hs", [P, 2, H0])
        hT = eb("hT", [P, 2, HC, P])
        gT = eb("gT", [P, 2, HC, P])
        b1T = eb("b1T", [P, E0, HC])
        b2_b = eb("b2_b", [P, NPAIR, P])
        ys = eb("ys", [P, NQ, P])

        early.close()

        wc = sb("wc", [P, 5 * P + 4 * DR + E1])
        wkvd_sb, wku_sb, wvu_sb, wq1_sb, wo1_sb = (wc[:, i * P:(i + 1) * P] for i in range(5))
        wqr_sb, wkr_sb = (wc[:, 5 * P + 2 * DR * i:5 * P + 2 * DR * (i + 1)] for i in range(2))
        wr_sb = wc[:, 5 * P + 4 * DR:]
        rope_sb = sb("rope", [2 * DR, T])
        identb = sb("identb", [P, P], BF16)
        ones8 = sb("ones8", [P, E1])
        maskq = sb("maskq", [P, 2, P], BF16)
        maskk = sb("maskk", [P, 2, P], BF16)
        gates = sb("gates", [P, NT, K0])
        gsum = sb("gsum", [P, NT])
        gidx = sb("gidx", [P, 2, GT, K0], U32)
        R = sb("R", [P, 2, GT * K0, P])
        xa = sb("xa", [P, GT, P])
        xaT = sb("xaT", [P, GN])
        ckvT = sb("ckvT", [P, GN])
        qkh = sb("qkh", [P, 2, GN], F32R)
        qkl = sb("qkl", [P, 2, GN], F32R)
        rt = sb("rt", [DR, 2, GN])
        rp = sb("rp", [KR, 2, GN], F32R)
        SQ = sb("SQ", [P, 2 * RD, GN], F32R)
        SK = sb("SK", [P, 2 * RD, GN], F32R)
        V1 = sb("V1", [P, 2, GT, NH, 32])
        mx = sb("mx", [P, 2, 2, GB, 2])
        ms = sb("ms", [P, 2, 2 * 8], F32R)
        mT = sb("mT", [2 * 8, 2, P])
        onerow = sb("onerow", [2 * RD, GN])
        PT = sb("PT", [P, 2, 4, 384])
        raw = sb("raw", [P, GN])
        rec = sb("rec", [P, 4, 4])
        att = sb("att", [P, GT, P])
        attT = sb("attT", [P, GN])
        xg = sb("xg", [P, 2, GT, PX])
        xgT = sb("xgT", [P, GN])
        lg1 = sb("lg1", [P, GT, E1])
        best1 = sb("best1", [P, GT, 8])
        ix1 = sb("ix1", [P, GT, 8], U32)
        ixa = sb("ixa", [P, NT, K1])
        posa = sb("posa", [P, NT, K1])
        oh1 = sb("oh1", [P, GT, K1, E1])
        ohp1 = sb("ohp1", [P, GT, K1, E1])
        M1 = sb("M1", [P, GT, E1])
        M1b = sb("M1b", [P, GT, E1], BF16)
        gcnt1 = sb("gcnt1", [P, E1])
        count1 = sb("count1", [P, E1])
        count1b = sb("count1b", [P, E1], BF16)
        srow1 = sb("srow1", [P, 2, GT, K1], U32)
        w1d = sb("w1d", [P, E1, 2 * F1])
        w2d = sb("w2d", [P, E1, 2, P])
        ntile = sb("ntile", [P, E1])
        tend = sb("tend", [P, E1])
        tw = sb("tw", [P, E1])
        cmp1 = sb("cmp1", [P, E1, NT])
        cmp2 = sb("cmp2", [P, ND1, E1])
        cmp3 = sb("cmp3", [P, ND1, E1])
        tl = sb("tl", [P, 2, ND1])
        tli = sb("tli", [P, 2, ND1], mybir.dt.int32)
        gt1 = sb("gt1", [P, NT, K1])
        gw1 = sb("gw1", [P, NT, K1])
        xd = sb("xd", [P, NQ1, PX])
        dest = sb("dest", [P, LAP1], U32)
        xdT = sb("xdT", [P, 2, P])
        sg = sb("sg", [P, 2, F1])
        ac = sb("ac", [P, 2, F1])
        acT = sb("acT", [P, 2, F1])
        yd = sb("yd", [P, NQ1, P])

        s_const, s_x, s_zero = sem("s_const"), sem("s_x"), sem("s_zero")
        s_tri, s_step = sem("s_tri"), sem("s_step")
        s_ve = [sem(f"s_ve{i}") for i in range(3)]
        s_rs = [sem(f"s_rs{i}") for i in range(3)]
        s_xn = sem("s_xn")
        s_xnb = sem("s_xnb")
        s_xnTp, s_xnT = sem("s_xnTp"), sem("s_xnT")
        s_q, s_k, s_g, s_v = sem("s_q"), sem("s_k"), sem("s_g"), sem("s_v")
        s_qe, s_ge, s_ve_ = sem("s_qe"), sem("s_ge"), sem("s_vev")
        s_lev, s_upd, s_aev = sem("s_lev"), sem("s_upd"), sem("s_aev")
        s_cross, s_axt = sem("s_cross"), sem("s_axt")
        s_av, s_ot, s_wo, s_y = sem("s_av"), sem("s_ot"), sem("s_wo"), sem("s_y")
        s_xf, s_xfTp, s_xfT, s_lg = sem("s_xf"), sem("s_xfTp"), sem("s_xfT"), sem("s_lg")
        s_M, s_pos, s_posr, s_slot = sem("s_M"), sem("s_pos"), sem("s_posr"), sem("s_slot")
        s_scat = [sem("s_scat0"), sem("s_scat1")]
        c_F, c_G, c_H, c_W = sem("c_F"), sem("c_G"), sem("c_H"), sem("c_W")
        s_w = [sem(f"s_w{i}") for i in range(PAIRS)]
        s_b1 = sem("s_b1")
        s_xs = [sem(f"s_xs{i}") for i in range(NQ)]
        s_xsTp, s_xsT, s_h, s_hs, s_hTp, s_hT, s_gT, s_yp, s_ys = (
            sem(n) for n in ("s_xsTp", "s_xsT", "s_h", "s_hs", "s_hTp", "s_hT", "s_gT", "s_yp", "s_ys"))
        s_yo = [sem(f"s_yo{i}") for i in range(NQ)]
        s_out = sem("s_out")
        s_w2c, s_pre = sem("s_w2c"), sem("s_pre")
        s_gexp, s_gsub = sem("s_gexp"), sem("s_gsub")
        s_gat = [sem("s_gat0"), sem("s_gat1")]
        s_radd, s_gidx = sem("s_radd"), sem("s_gidx")
        s_ve += [sem("s_ve3"), sem("s_ve4")]
        s_rs += [sem("s_rs3"), sem("s_rs4")]
        (s_xa, s_xaTp, s_xaT, s_ckvp, s_ckv, s_q1p, s_qh, s_ql, s_qr, s_rq, s_kp, s_kh, s_kl, s_v1p, s_v1, s_kr, s_rk,
         s_parts, s_max, s_maxr, s_ms, s_mTp, s_mT, s_st, s_exp, s_pv, s_raw, s_rawTp, s_norm,
         s_attTp, s_attT, s_wo1, s_x3, s_xg, s_xgTp, s_xgT, s_lg1, s_M1, s_pos1, s_row1) = (
            sem(n) for n in ("s_xa s_xaTp s_xaT s_ckvp s_ckv s_q1p s_qh s_ql s_qr s_rq s_kp s_kh s_kl s_v1p s_v1 s_kr s_rk "
                             "s_parts s_max s_maxr s_ms s_mTp s_mT s_st s_exp s_pv s_raw s_rawTp s_norm "
                             "s_attTp s_attT s_wo1 s_x3 s_xg s_xgTp s_xgT s_lg1 s_M1 s_pos1 s_row1").split())
        s_fill = [sem(f"s_fill{i}") for i in range(RD)]
        s_shift = [sem(f"s_shift{i}") for i in range(RD)]
        s_scat1 = [sem("s_scat1_0"), sem("s_scat1_1")]
        s_put = s_scat + s_scat1
        put_from = [16 * GT * K0 * (NG // 2)] * 2 + [16 * GT * K1 * (NG // 2)] * 2
        c_C, c_N, c_R, c_T, c_Q = (sem(n) for n in ("c_C", "c_N", "c_R", "c_T", "c_Q"))
        s_fin1 = sem("s_fin1")
        s_tot, s_tiles = sem("s_tot"), sem("s_tiles")
        s_wd, s_xmore, s_place, s_dest = (sem(n) for n in ("s_wd", "s_xmore", "s_place", "s_dest"))
        s_sg, s_ac, s_acTp, s_acT, s_ydp, s_yd = (sem(n) for n in "s_sg s_ac s_acTp s_acT s_ydp s_yd".split())
        s_fin = sem("s_fin")
        s_ones1 = sem("s_ones1")
        s_zero1 = sem("s_zero1")
        s_vinit = sem("s_vinit")


        block = ctx.enter_context(nc.Block())

        def stands_alone(eng):
            eng.sem_inc(s_step, 1)

        def blocks(ap2, m):
            return ap2.rearrange("p (c two m) -> p c two m", two=2, m=m)

        @block.sync
        def _(sp):
            sp.dma_start(X[:, 0:GT, :], x[0:GN, :].rearrange("(t p) d -> p t d", p=P)).then_inc(s_x, 16)
            for dst, src in ((cst[:], const[:, :]), (wa[:], first_w[:, :]), (ba[:], first_b.partition_broadcast(P)),
                             (mask_in[:], masks.rearrange("p (l n) -> p l n", l=NL))):
                sp.dma_start(dst, src).then_inc(s_const, 16)
            sp.dma_start(X[:, GT:NT, :], x[GN:NTOK, :].rearrange("(t p) d -> p t d", p=P)).then_inc(s_xmore, 16)
            sp.wait_ge(s_vinit, 1)
            sp.dma_start(slots_in.rearrange("(p t) d -> p (t d)", p=P)[:, 0:1024], zrow[:, 0:1024]).then_inc(s_zero, 16)
            sp.dma_start(slots_in.rearrange("(p t) d -> p (t d)", p=P)[:, 1024:2048], zrow[:, 0:1024]).then_inc(s_zero, 16)
            sp.dma_start(slots_in.rearrange("(p t) d -> p (t d)", p=P)[:, 2048:3072], zrow[:, 0:1024]).then_inc(s_zero, 16)
            sp.dma_start(slots_in.rearrange("(p t) d -> p (t d)", p=P)[:, 3072:4096], zrow[:, 0:1024]).then_inc(s_zero, 16)
            z1 = rows1_in.rearrange("(a p t) d -> a p (t d)", p=P, t=8)
            for a in range(8):
                sp.dma_start(z1[4 * a:4 * a + 4].rearrange("a p n -> p a n"), zrow[:].unsqueeze(1).broadcast_to([P, 4, 8 * PX])).then_inc(s_zero1, 16)
            sp.dma_start(b1T[:], b1t.rearrange("p (e c) -> p e c", c=HC)).then_inc(s_b1, 16)
            for h in range(2):
                sp.dma_start(b2_b[h * CAP:(h + 1) * CAP], b2.rearrange("(a two) d -> two a d", two=2)[h].partition_broadcast(CAP)
                             ).then_inc(s_b1, 16)

            def weights(pair, i):
                e = pair * 2
                sp.dma_start(w1r[:, 2 * i:2 * i + 2, :], w1[bass.ds(e, 2)].rearrange("e d h -> d e h")).then_inc(s_w[i], 16)
                sp.dma_start(w2r[:, 2 * i:2 * i + 2].rearrange("p e c d -> p (e c) d"),
                             w2[bass.ds(e, 2)].rearrange("e (c p) d -> p (e c) d", p=P)).then_inc(s_w[i], 16)

            def slots(pair, q):
                sp.dma_start(xs[:, q, :], slots_in[bass.ds(pair * P, P), :]).then_inc(s_xs[q], 16)

            def store(pair, q):
                sp.wait_ge(s_ys, pair + 1)
                sp.dma_start(slots_out[bass.ds(pair * P, P), :], ys[:, q, :]).then_inc(s_yo[q], 16)

            for pair in range(PAIRS):
                weights(pair, pair)
            sp.wait_ge(s_zero, 16 * 4)
            for p in range(2):
                sp.wait_ge(s_scat[p], 16 * GT * K0 * (NG // 2))
            def slots_after(pair, q):
                sp.wait_ge(s_xsTp, pair - NQ + 1)
                slots(pair, q)

            for pair in range(NQ):
                slots(pair, pair)
            for pair in range(NQ, NQ + AHEAD):
                slots_after(pair, pair % NQ)
            with sp.Fori(0, NROUND - 1) as r:
                for i in range(PAIRS):
                    pair = r * PAIRS + i
                    slots_after(pair + NQ + AHEAD, (i + AHEAD) % NQ)
                    store(pair, i % NQ)
                    weights(pair + PAIRS, i)
            for pair in range(NPAIR - PAIRS, NPAIR):
                if pair + NQ + AHEAD < NPAIR:
                    slots_after(pair + NQ + AHEAD, (pair + AHEAD) % NQ)
                store(pair, pair % NQ)
            for q in range(NQ):
                sp.wait_ge(s_yo[q], 16 * (NPAIR // NQ))

            for dst, src in ((wc[:], second_w[:, :]), (rope_sb[:], rope[:, :])):
                sp.dma_start(dst, src).then_inc(s_w2c, 16)
            sp.wait_ge(s_pre, 1)
            for r in range(2):
                sp.dma_start(SK[KM + r:KM + r + 1].bitcast(F32), onerow[:]).then_inc(s_ones1, 16)
            sp.wait_ge(s_xa, 1)
            sp.dma_start(w1d[:], W1t.rearrange("p (e n) -> p e n", e=E1)).then_inc(s_wd, 16)
            sp.dma_start(w2d[:], W2t.rearrange("p (e c n) -> p e c n", e=E1, c=2)).then_inc(s_wd, 16)

            def write_parts(grp, side):
                g, p = grp.g, grp.par
                sp.wait_ge((s_ql, s_kl)[side], g + 1)
                for r, src in enumerate(((qkh, qkh, qkl), (qkh, qkl, qkh))[side]):
                    sp.dma_start(parts[p, side, r * HD:(r + 1) * HD].rearrange("d h n -> (d h) n"),
                                 src[:, side].bitcast(F32)).then_inc(s_parts, 16)

            def fill(grp, i):
                g, p, r = grp.g, grp.par, i % RD
                if i == 0:
                    sp.wait_ge(s_parts, 96 * (g + 1))
                    sp.wait_ge(s_rk, g + 1)
                if after(g, 1) or i >= RD:
                    sp.wait_ge(s_st, 4 * (g * ND + i - RD + 1))
                for side, S in ((0, SQ), (1, SK)):
                    if i < RD:
                        sp.dma_start(S[0:KR, 2 * r:2 * r + 2, :].bitcast(F32),
                                     rp[:, side].bitcast(F32).unsqueeze(1).broadcast_to([KR, 2, GN])).then_inc(s_fill[r], 16)
                    sp.dma_start(S[KR:KM, 2 * r:2 * r + 2, :].bitcast(F32), parts[p, side, :, 2 * i:2 * i + 2, :]).then_inc(s_fill[r], 16)

            def shift(grp, i):
                g, r = grp.g, i % RD
                sp.wait_ge(s_mT, g * ND + i + 1)
                for h in range(2):
                    sp.dma_start(SQ[KM + h:KM + h + 1, 2 * r:2 * r + 2, :].bitcast(F32), mT[8 * h:8 * h + 8, i % 2, :]
                                 ).then_inc(s_shift[r], 16)

            def on(i, n, stage):
                k, lag = next_duo(i, n)
                return lambda grp: stage(grp, k), lag

            slots_of = []
            for i in range(ND):
                slots_of += [on(i, 3, fill), on(i, 1, shift)]
                if i in (3, 4):
                    slots_of.append(((lambda side: lambda grp: write_parts(grp, side))(i - 3), 1))
            steps(sp, slots_of)

            for p in range(2):
                sp.wait_ge(s_scat1[p], 16 * GT * K1 * (NG // 2))
            sp.wait_ge(s_zero1, 16 * 8)
            sp.wait_ge(s_tiles, 1)

            def tile_in(t, q):
                row = sp.value_load(tli[0:1, 1, bass.ds(t, 1)], min_val=0, max_val=E1 * REG - P)
                sp.dma_start(xd[:, q, :], rows1_in[bass.ds(row, P), :]).then_inc(s_xs[q], 16)

            def tile_after(t, q):
                sp.wait_ge(s_xsTp, NPAIR + t - NQ1 + 1)
                stands_alone(sp)
                sp.wait_ge(s_dest, t - NQ1 + 1)
                stands_alone(sp)
                tile_in(t, q)

            for q in range(NQ1):
                tile_in(q, q)
            for t in range(NQ1, NQ1 + AHEAD):
                tile_after(t, t % NQ1)
            with sp.Fori(0, ND1 // NQ1 - 2) as lap:
                for q in range(NQ1):
                    tile_after(lap * NQ1 + q + NQ1 + AHEAD, (q + AHEAD) % NQ1)
            for t in range(ND1 - NQ1 + AHEAD, ND1):
                tile_after(t, t % NQ1)

            out_t = out.rearrange("(t p) d -> p t d", p=P)
            rows_t = rows1_out.rearrange("(t p k) d -> p t (k d)", p=P, k=K1)
            for q in range(NQ1):
                sp.wait_ge(s_put[q], put_from[q] + 16 * (ND1 // NQ1))

            def choices_in(g, p):
                sp.dma_start(R[:, p, 0:GT * K1, :].rearrange("p (t k) d -> p t (k d)", k=K1), rows_t[:, bass.ds(g * GT, GT), :]
                             ).then_inc(s_yo[p], 16)

            def result(g):
                sp.wait_ge(s_fin, g + 1)
                sp.dma_start(out_t[:, bass.ds(g * GT, GT), :], X[:, bass.ds(g * GT, GT), :]).then_inc(s_out, 16)

            choices_in(0, 0)
            choices_in(1, 1)
            with sp.Fori(0, NG // 2 - 1) as j:
                for p in range(2):
                    result(2 * j + p)
                    choices_in(2 * j + 2 + p, p)
            result(NG - 2)
            result(NG - 1)
            sp.wait_ge(s_out, 16 * NG)

        @block.gpsimd
        def _(pool):
            pool.wait_ge(s_const, 16 * NCONST)
            pool.wait_ge(s_x, 16)
            pool.wait_ge(s_vinit, 1)

            def power(i, grp):
                pool.wait_ge(s_ve[i], grp.g + 1)
                pool.tensor_tensor(rs[:, i, :], ve[:, i, :], mhalf[:], ALU.pow).then_inc(s_rs[i], 1)

            def residuals(grp):
                g = grp.g
                pool.wait_ge(s_xn, g + 1)
                if after(g, 2):
                    pool.wait_ge(s_y, g - 1)
                pool.tensor_tensor(xb[:, grp.par], xn[:, grp.par], bo_b.unsqueeze(1).broadcast_to([P, GT, P]),
                                   ALU.add).then_inc(s_xnb, 1)
                xt = X[:, bass.ds(g * GT, GT), :]
                pool.tensor_tensor(xt, xt, beta_b.unsqueeze(1).broadcast_to([P, GT, P]), ALU.add).then_inc(s_xnb, 1)

            def scatter0(grp):
                pool.wait_ge(s_slot, grp.g + 1)
                stands_alone(pool)
                for t in range(GT):
                    for k in range(K0):
                        pool.indirect_dma_start(
                            out=slots_in[:, :], out_offset=bass.IndirectOffsetOnAxis(ap=sslot[:, grp.par, t, k:k + 1], axis=0),
                            in_=xf[:, grp.par, t, :], in_offset=None, bounds_check=NSLOT0 - 1, oob_is_err=False,
                        ).then_inc(s_scat[grp.par], 16)

            pool.wait_ge(s_zero, 16 * 4)
            steps(pool, [(lambda grp: power(1, grp), 3), (lambda grp: power(2, grp), 3), (lambda grp: power(0, grp), 0),
                         (residuals, 1), (scatter0, 4)])

            for q in range(NQ):
                pool.wait_ge(s_yo[q], 16 * (NPAIR // NQ))

            def gather0(grp):
                if after(grp.g, 2):
                    pool.wait_ge(s_radd, grp.g - 1)
                pool.tensor_copy(gidx[:, grp.par, :, 0:K0], gslot[:, bass.ds(grp.g * GT, GT), :]).then_inc(s_gidx, 1)
                pool.wait_ge(s_gidx, grp.g + 1)
                stands_alone(pool)
                for t in range(GT):
                    for k in range(K0):
                        pool.indirect_dma_start(
                            out=R[:, grp.par, t * K0 + k, :], out_offset=None, in_=slots_out[:, :],
                            in_offset=bass.IndirectOffsetOnAxis(ap=gidx[:, grp.par, t, k:k + 1], axis=0),
                            bounds_check=NSLOT0 - 1, oob_is_err=False).then_inc(s_gat[grp.par], 16)

            def power3(grp):
                power(3, grp)

            def power4(grp):
                power(4, grp)

            def scatter1(grp):
                g, p = grp.g, grp.par
                pool.wait_ge(s_row1, g + 1)
                for k in range(K1):
                    if k:
                        pool.wait_ge(s_scat1[p], 16 * GT * (K1 * grp.half + k))
                    stands_alone(pool)
                    pool.tensor_copy(xg[:, p, :, P], places[:, k, bass.ds(g * GT, GT)]).then_inc(s_place, 1)
                    pool.wait_ge(s_place, K1 * g + k + 1)
                    stands_alone(pool)
                    for t in range(GT):
                        pool.indirect_dma_start(
                            out=rows1_in[:, :], out_offset=bass.IndirectOffsetOnAxis(ap=srow1[:, p, t, k:k + 1], axis=0),
                            in_=xg[:, p, t, :], in_offset=None, bounds_check=E1 * REG - 1, oob_is_err=False,
                        ).then_inc(s_scat1[p], 16)

            pool.wait_ge(s_zero1, 16 * 8)
            steps(pool, [(gather0, 0), (power4, 3), (power3, 0), (scatter1, 3)])

            with pool.Fori(0, ND1 // LAP1) as lap:
                for q in range(LAP1):
                    t = lap * LAP1 + q
                    pool.wait_ge(s_dest, t + 1)
                    pool.wait_ge(s_yd, t + 1)
                    stands_alone(pool)
                    pool.indirect_dma_start(
                        out=rows1_out[:, :], out_offset=bass.IndirectOffsetOnAxis(ap=dest[:, q:q + 1], axis=0),
                        in_=yd[:, q % NQ1, :], in_offset=None, bounds_check=NPLACE - 1, oob_is_err=False).then_inc(s_put[q % NQ1], 16)

        @block.scalar
        def _(act):
            act.wait_ge(s_const, 16 * NCONST)

            def norm_in(grp):
                act.wait_ge(s_xnTp, grp.g + 1)
                act.activation(xnT[:], bank[0][:], ACT.Copy).then_inc(s_xnT, 1)

            def queries_keys(grp):
                g, p = grp.g, grp.par
                act.wait_ge(s_q, g + 1)
                act.activation(Q[:, p], bank[1][:], ACT.Identity, bias=bq_c)
                act.wait_ge(s_k, g + 1)
                act.activation(K[:, p], bank[0][:], ACT.Identity, bias=bk_c).then_inc(s_qe, 1)

            def gate(grp):
                act.wait_ge(s_g, grp.g + 1)
                act.activation(G[:, grp.par], bank[1][:], ACT.Sigmoid, bias=bg_c).then_inc(s_ge, 1)

            def cross(grp):
                act.wait_ge(s_cross, grp.g + 1)
                act.activation(AXT[:], bank[4][:, 0:GB * P].rearrange("p (b n) -> p b n", b=GB), ACT.Copy).then_inc(s_axt, 1)

            def attended(grp):
                act.wait_ge(s_av, grp.g + 1)
                act.activation(OT[:], bank[5][:], ACT.Copy).then_inc(s_ot, 1)

            def router_in0(grp):
                act.wait_ge(s_xfTp, grp.g + 1)
                act.activation(xfT[:], bank[7][:], ACT.Copy).then_inc(s_xfT, 1)

            steps(act, [(router_in0, 4), (attended, 3), (norm_in, 1), (queries_keys, 1), (gate, 1), (cross, 2)])

            def gelus(pair, par):
                act.wait_ge(s_hT, pair + 1)
                act.activation(gT[:, par], hT[:, par], ACT.Gelu).then_inc(s_gT, 1)

            gelus(0, 0)
            gelus(1, 1)
            with act.Fori(1, NPAIR // 2) as j:
                for p in range(2):
                    gelus(2 * j + p, p)

            act.wait_ge(s_gsub, 1)
            act.activation(gates[:], gates[:], ACT.Exp).then_inc(s_gexp, 1)

            def norm1_in(grp):
                act.wait_ge(s_xaTp, grp.g + 1)
                act.activation(xaT[:], bank[2][:], ACT.Copy).then_inc(s_xaT, 1)

            def latent(grp):
                act.wait_ge(s_ckvp, grp.g + 1)
                act.activation(ckvT[:], bank[2][:], ACT.Copy).then_inc(s_ckv, 1)

            def upper(grp, side):
                if after(grp.g, 1):
                    act.wait_ge(s_parts, 96 * grp.g)
                act.wait_ge((s_q1p, s_kp)[side], grp.g + 1)
                act.activation(qkh[:, side], bank[2][:], ACT.Copy).then_inc((s_qh, s_kh)[side], 1)

            def values_in(grp):
                act.wait_ge(s_v1p, grp.g + 1)
                act.activation(V1[:, grp.par, :, :, 0:HD], bank[2][:].rearrange("p (t h d) -> p t h d", t=GT, h=NH), ACT.Copy).then_inc(s_v1, 1)

            def shift_rows(grp, i):
                act.wait_ge(s_mTp, grp.g * ND + i + 1)
                if after(grp.g, 1) or i >= 2:
                    r = (i - 2) % RD
                    act.wait_ge(s_shift[r], 64 * grp.g + (32 * (1 + (i - 2) // RD) if i >= 2 else 0))
                act.activation(mT[:, i % 2, :], bank[7][0:16, 0:P], ACT.Copy).then_inc(s_mT, 1)

            def exponentials(grp, i, n):
                act.wait_ge(s_st, (grp.g * ND + i) * 4 + n + 1)
                act.activation(PT[:, i % 2, n, :], bank[4 + n % 2][:, P:512], ACT.Exp, scale=SCORE_SCALE).then_inc(s_exp, 1)

            def raw_out(grp, i):
                act.wait_ge(s_pv, grp.g * (ND // 2) + i // 2 + 1)
                act.activation(raw[:], bank[6][:], ACT.Copy).then_inc(s_raw, 1)

            def attended_in(grp):
                act.wait_ge(s_attTp, grp.g + 1)
                act.activation(attT[:], bank[3][:], ACT.Copy).then_inc(s_attT, 1)

            def router_in(grp):
                act.wait_ge(s_xgTp, grp.g + 1)
                act.activation(xgT[:], bank[3][:], ACT.Copy).then_inc(s_xgT, 1)

            def some(i, lo, hi):
                def stage(grp):
                    for n in range(lo, hi):
                        exponentials(grp, i, n)
                return stage, 2

            def shifts(i):
                return lambda grp: shift_rows(grp, i)

            more = {0: [(norm1_in, 1), (attended_in, 3)], 1: [(latent, 1)], 2: [(lambda grp: upper(grp, 0), 1)],
                    3: [(lambda grp: upper(grp, 1), 1)], 4: [(values_in, 1)], 5: [(router_in, 3)]}
            slots_of = []
            for i in range(ND):
                k, lag = next_duo(i, 1)
                slots_of += [some(i, 0, 2)]
                if i % 2 == 0:
                    slots_of.append(((lambda k: lambda grp: raw_out(grp, k))((i - 1) % ND), 2 if i else 3))
                slots_of += [(shifts(k), lag), some(i, 2, 4)] + more.get(i, [])
            steps(act, slots_of)
            act.wait_ge(s_gsub, 2)
            act.activation(gt1[:], gw1[:], ACT.Exp).then_inc(s_gexp, 1)

            def d_in(t, p):
                act.wait_ge(s_xsTp, NPAIR + t + 1)
                act.activation(xdT[:, p], bank[p][:, 0:P], ACT.Copy).then_inc(s_xsT, 1)

            def d_silu(t, p):
                act.wait_ge(s_h, NPAIR + t + 1)
                act.activation(sg[:, p], bank[2 + p][:, F1:2 * F1], ACT.Silu).then_inc(s_sg, 1)

            def d_out(t, p, q, wait):
                act.wait_ge(s_ydp, t + 1)
                if wait is not None:
                    act.wait_ge(s_put[q], put_from[q] + 16 * wait)
                act.activation(yd[:, q], bank[6 + p][:, 0:P], ACT.Copy).then_inc(s_yd, 1)

            def lap_of(lap, wait, left=ND1):
                for q in range(NQ1):
                    t, p = lap * NQ1 + q, q % 2
                    if q + AHEAD < left:
                        d_silu(t + AHEAD, p)
                    if q + AHEAD + 1 < left:
                        d_in(t + AHEAD + 1, 1 - p)
                    d_out(t, p, q, wait)

            d_in(0, 0)
            d_in(1, 1)
            d_silu(0, 0)
            d_in(2, 0)
            d_silu(1, 1)
            lap_of(0, None)
            with act.Fori(1, ND1 // NQ1 - 1) as lap:
                lap_of(lap, lap)
            lap_of(ND1 // NQ1 - 1, ND1 // NQ1 - 1, left=NQ1)

        @block.vector
        def _(dve):
            dve.memset(mhalf[:], -0.5)
            dve.memset(zrow[:], 0.0).then_inc(s_vinit, 1)
            dve.memset(count[:], 0.0)
            dve.memset(countb[:], 0.0).then_inc(s_tri, 1)
            dve.wait_ge(s_tri, 1)
            dve.wait_ge(s_const, 16 * NCONST)
            dve.wait_ge(s_x, 16)
            dve.tensor_copy(tri[:], cst[:, 128:256])
            dve.tensor_copy(mask_sb[:], mask_in[:].unsqueeze(2).broadcast_to([P, NL, GT, P // 2]))
            dve.memset(ones[:], 1.0).then_inc(s_tri, 1)
            dve.wait_ge(s_tri, 2)

            def variance(i, link, src):
                stands_alone(dve)
                for t in range(GT):
                    last = dve.bn_stats(st[:, i, t, :], src[:, t, :])
                link(last)
                stands_alone(dve)
                for t in range(GT):
                    last = dve.bn_aggr(mv[:, i, t, :], st[:, i, t, :])
                link(last)
                dve.tensor_scalar(ve[:, i, :], mv[:, i, :, 1], EPS, None, ALU.add).then_inc(s_ve[i], 1)

            def normalize(i, grp, src, dst):
                dve.wait_ge(s_rs[i], grp.g + 1)
                for t in range(GT):
                    last = dve.tensor_scalar(dst[:, t, :], src[:, t, :], mv[:, i, t, 0:1], rs[:, i, t:t + 1],
                                             ALU.subtract, ALU.mult)
                return last

            def layernorm(i, grp, link, src, dst):
                variance(i, link, src)
                return normalize(i, grp, src, dst)

            def norm_stats(grp):
                if after(grp.g, 1):
                    dve.wait_ge(s_xmore, 16)
                link = Chain(dve, c_F, grp.g, 2)
                variance(0, link, X[:, bass.ds(grp.g * GT, GT), :])
                link.end()

            def norm(grp):
                g, p = grp.g, grp.par
                if after(g, 2):
                    dve.wait_ge(s_xnb, 2 * (g - 1))
                    dve.wait_ge(s_xnTp, g - 1)
                normalize(0, grp, X[:, bass.ds(g * GT, GT), :], xn[:, p]).then_inc(s_xn, 1)

            def values(grp):
                g, p = grp.g, grp.par
                dve.wait_ge(s_v, g + 1)
                if after(g, 2):
                    dve.wait_ge(s_av, g - 1)
                dve.tensor_tensor(V[:, p], bank[3][:].rearrange("p (t n) -> p t n", t=GT),
                                  bv_b.unsqueeze(1).broadcast_to([P, GT, P]), ALU.add).then_inc(s_ve_, 1)

            def diagonal(grp):
                g, p = grp.g, grp.par
                q, k, gg = Q[:, p], K[:, p], G[:, p]
                dve.wait_ge(s_ge, g + 1)
                dve.wait_ge(s_lev, g * NLP + 1)
                dve.tensor_tensor(q, q, gg, ALU.mult).then_inc(s_upd, 1)
                if after(g, 2):
                    dve.wait_ge(s_av, g - 1)
                dve.tensor_tensor(AD[:, p].rearrange("p (t n) -> p t n", t=GT), bank[6][:].rearrange("p (t n) -> p t n", t=GT),
                                  ident.unsqueeze(1).broadcast_to([P, GT, P]), ALU.mult).then_inc(s_aev, 1)
                dve.wait_ge(s_aev, g * NLP + 1)

            def level(grp, lo, hi):
                g, p = grp.g, grp.par
                link = Chain(dve, c_G, g, NL - 1, first=lo - 1)
                q, k = Q[:, p], K[:, p]
                for lv in range(lo, hi):
                    m = LEVELS[lv - 1]
                    tcur = Tm[lv - 2][:] if lv > 1 else G[:, p]
                    dve.wait_ge(s_lev, g * NLP + lv + 1)
                    if m < 64:
                        t3 = tcur.rearrange("p (c two) -> p c two", two=2)
                        dve.tensor_tensor(blocks(q, m)[:, :, 1], blocks(q, m)[:, :, 1],
                                          t3[:, :, 0:1].broadcast_to([P, GN // m // 2, m]), ALU.mult)
                        dve.tensor_tensor(blocks(k, m)[:, :, 0], blocks(k, m)[:, :, 0],
                                          t3[:, :, 1:2].broadcast_to([P, GN // m // 2, m]), ALU.mult).then_inc(s_upd, 1)
                    else:
                        q4 = q.rearrange("p (b s two m) -> p b s two m", b=GB, s=2, two=2)
                        k4 = k.rearrange("p (b s two m) -> p b s two m", b=GB, s=2, two=2)
                        t4 = tcur.rearrange("p (b s two) -> p b s two", b=GB, s=2)
                        dve.tensor_tensor(q4[:, :, 1, 1], q4[:, :, 1, 1], t4[:, :, 1, 0:1].broadcast_to([P, GB, m]), ALU.mult)
                        dve.tensor_tensor(k4[:, :, 0, 0], k4[:, :, 0, 0], t4[:, :, 0, 1:2].broadcast_to([P, GB, m]), ALU.mult
                                          ).then_inc(s_upd, 1)
                    dve.copy_predicated(blocks(AD[:, p], m)[:, :, 1], mask_sb[:, lv - 1].rearrange("p t n -> p (t n)").rearrange("p (c m) -> p c m", m=m),
                                        blocks(bank[2 if lv % 2 else 6][:], m)[:, :, 1]).then_inc(s_aev, 1)
                    if m < 64:
                        link(dve.tensor_tensor(Tm[lv - 1][:], t3[:, :, 0], t3[:, :, 1], ALU.mult))
                link.end(min(hi, NL) - 1)

            def post_a(grp):
                g, p = grp.g, grp.par
                link = Chain(dve, c_W, g, 7)
                dve.wait_ge(s_wo, g + 1)
                dve.wait_ge(s_xnb, 2 * (g + 1))
                dve.tensor_tensor(Y[:], bank[4][:].rearrange("p (t n) -> p t n", t=GT), xb[:, p], ALU.add).then_inc(s_y, 1)
                dve.wait_ge(s_y, g + 1)
                variance(1, link, Y[:])
                link.end(2)

            def post_b(grp):
                g, p = grp.g, grp.par
                link = Chain(dve, c_W, g, 7, first=2)
                link(normalize(1, grp, Y[:], Y[:]))
                link(dve.tensor_tensor(Y[:], Y[:], gamma_b.unsqueeze(1).broadcast_to([P, GT, P]), ALU.mult))
                xt = X[:, bass.ds(g * GT, GT), :]
                link(dve.tensor_tensor(xt, xt, Y[:], ALU.add))
                link.end(5)

            def post_stats(grp):
                link = Chain(dve, c_W, grp.g, 7, first=5)
                variance(2, link, X[:, bass.ds(grp.g * GT, GT), :])
                link.end(7)

            def post_c(grp):
                g, p = grp.g, grp.par
                if after(g, 2):
                    dve.wait_ge(s_scat[p], 16 * GT * K0 * grp.half)
                normalize(2, grp, X[:, bass.ds(g * GT, GT), :], xf[:, p]).then_inc(s_xf, 1)

            def choose(grp):
                g, p = grp.g, grp.par
                link = Chain(dve, c_H, g, 16)
                dve.wait_ge(s_lg, g + 1)
                link(dve.tensor_tensor(lg[:], bank[7][:, 0:GT * E0].rearrange("p (t e) -> p t e", t=GT),
                                       gb_b.unsqueeze(1).broadcast_to([P, GT, E0]), ALU.add))
                stands_alone(dve)
                for t in range(GT):
                    last = dve.max(best[:, t, :], lg[:, t, :])
                link(last)
                dve.tensor_copy(top0[:, bass.ds(g * GT, GT), :], best[:, :, 0:K0])
                for t in range(GT):
                    last = dve.max_index(ix[:, t, :], best[:, t, :], lg[:, t, :])
                link(last)
                link.end(3)

            def count_chosen(grp):
                link = Chain(dve, c_H, grp.g, 16, first=3)
                link(dve.tensor_copy(ixf[:], ix[:, :, 0:K0]))
                for t in range(GT):
                    last = dve.tensor_tensor(oh[:, t], iota_e.unsqueeze(1).broadcast_to([P, K0, E0]),
                                         ixf[:, t, :].unsqueeze(2).broadcast_to([P, K0, E0]), ALU.is_equal)
                link(last)
                link(dve.tensor_reduce(M[:], oh[:].rearrange("p t k e -> p t e k"), AX.X, ALU.add))
                dve.tensor_copy(Mb[:], M[:]).then_inc(s_M, 1)
                link(dve.tensor_reduce(gcnt[:], M[:].rearrange("p t e -> p e t"), AX.X, ALU.add))
                link.end(7)

            def place(grp):
                g, p = grp.g, grp.par
                link = Chain(dve, c_H, g, 16, first=7)
                dve.wait_ge(s_pos, g + 1)
                for t in range(GT):
                    last = dve.tensor_tensor(ohp[:, t], oh[:, t],
                                     bank[7][:, 256 + t * E0:256 + (t + 1) * E0].unsqueeze(1).broadcast_to([P, K0, E0]), ALU.mult)
                link(last)
                dve.sem_inc(s_posr, 1)
                link(dve.tensor_tensor(count[:], count[:], gcnt[:], ALU.add))
                link(dve.tensor_copy(countb[:, 0, :], count[:]))
                link(dve.tensor_reduce(pos[:], ohp[:], AX.X, ALU.add))
                vg = valid[:, bass.ds(g * GT, GT), :]
                link(dve.tensor_scalar(vg, pos[:], float(CAP), None, ALU.is_lt))
                link(dve.tensor_scalar(r0[:], ixf[:], float(CAP), None, ALU.mult))
                link(dve.scalar_tensor_tensor(r1[:], vg, -float(NSLOT0), r0[:], ALU.mult, ALU.add))
                link(dve.scalar_tensor_tensor(sslot[:, p], pos[:], float(NSLOT0), r1[:], ALU.add, ALU.add))
                link(dve.scalar_tensor_tensor(gslot[:, bass.ds(g * GT, GT), :], pos[:], float(CAP - 1), r0[:], ALU.min, ALU.add))
                dve.sem_inc(s_slot, 1)
                link.end()

            def lev(n):
                return lambda grp: level(grp, n, n + 1), 2

            steps(dve, [(diagonal, 2), (values, 2), lev(1), (choose, 4), lev(2), (count_chosen, 4), lev(3), (post_a, 3), lev(4),
                        (place, 4), lev(5), (post_b, 3), lev(6), (post_stats, 3), (norm_stats, 0), lev(7), (post_c, 3), (norm, 0)])

            def tokens_in(pair, i):
                dve.wait_ge(s_xsTp, pair + 1)
                dve.tensor_copy(xsT[:, i % 2], bank[7 * (i % 2)][:, 0:P]).then_inc(s_xsT, 1)

            def hidden(pair, i):
                dve.wait_ge(s_h, pair + 1)
                dve.tensor_copy(hs[:, i % 2], bank[1 + i % 2][:]).then_inc(s_hs, 1)

            def turn(pair, i):
                p = i % 2
                dve.wait_ge(s_hTp, pair + 1)
                dve.tensor_tensor(hT[:, p].rearrange("p c (e s) -> p c e s", e=2),
                                  bank[3 + p][:].rearrange("p (c e s) -> p c e s", c=HC, e=2),
                                  b1T[:, bass.ds(2 * pair, 2), :].rearrange("p e c -> p c e").unsqueeze(3).broadcast_to([P, HC, 2, CAP]),
                                  ALU.add).then_inc(s_hT, 1)

            def outputs(pair, i, lap):
                q = i % NQ
                dve.wait_ge(s_yp, pair + 1)
                if not (isinstance(lap, int) and lap == 0):
                    dve.wait_ge(s_yo[q], 16 * lap)
                dve.tensor_tensor(ys[:, q], bank[5 + i % 2][:, 0:P],
                                  b2_b[:, bass.ds(pair, 1)].rearrange("p o d -> p (o d)"), ALU.add).then_inc(s_ys, 1)

            def pairs(lap, left=NPAIR):
                for i in range(NQ):
                    pair = lap * NQ + i
                    turn(pair, i)
                    if i + AHEAD < left:
                        hidden(pair + AHEAD, i + AHEAD)
                    if i + AHEAD + 1 < left:
                        tokens_in(pair + AHEAD + 1, i + AHEAD + 1)
                    outputs(pair, i, lap)

            dve.wait_ge(s_b1, 48)
            tokens_in(0, 0)
            tokens_in(1, 1)
            hidden(0, 0)
            tokens_in(2, 2)
            hidden(1, 1)
            pairs(0)
            with dve.Fori(1, NPAIR // NQ - 1) as lap:
                pairs(lap)
            pairs(NPAIR // NQ - 1, left=NQ)

            link = Chain(dve, c_T, 0, 8)
            for q in range(NQ):
                dve.wait_ge(s_yo[q], 16 * (NPAIR // NQ))
            dve.memset(onerow[:], 1.0)
            dve.memset(ones8[:], 1.0)
            dve.tensor_copy(identb[:], ident)
            for h in range(2):
                dve.tensor_scalar(maskq[:, h], cst[:, 128:256], MASKED, None, ALU.mult)
            dve.memset(count1[:], 0.0)
            dve.memset(count1b[:], 0.0)
            dve.memset(V1[:], 0.0)
            link(dve.tensor_tensor(Y[:, 0], cst[:, 128:256], ident, ALU.add))
            for h in range(2):
                last = dve.tensor_scalar(maskk[:, h], Y[:, 0], -MASKED, MASKED, ALU.mult, ALU.add)
            link(last)
            link(dve.memset(V1[:, :, :, :, HD:HD + 1], 1.0))
            dve.sem_inc(s_pre, 1)
            link(dve.tensor_tensor(gates[:], top0[:], top0[:, :, 0:1].broadcast_to([P, NT, K0]), ALU.subtract))
            dve.sem_inc(s_gsub, 1)
            dve.wait_ge(s_gexp, 1)
            link(dve.tensor_reduce(gsum[:], gates[:], AX.X, ALU.add))
            link(dve.reciprocal(gsum[:], gsum[:]))
            link(dve.tensor_tensor(gates[:], gates[:], gsum[:].unsqueeze(2).broadcast_to([P, NT, K0]), ALU.mult))
            link(dve.tensor_tensor(gates[:], gates[:], valid[:], ALU.mult))
            link.end()
            dve.wait_ge(s_w2c, 32)

            def combine(grp, lo, hi):
                g, p = grp.g, grp.par
                link = Chain(dve, c_C, g, 5, first=lo)
                dve.wait_ge(s_gat[p], 16 * GT * K0 * (grp.half + 1))
                for k in range(lo, hi):
                    for t in range(GT):
                        xt = X[:, bass.ds(g * GT + t, 1), :].rearrange("p o d -> p (o d)")
                        gate = gates[:, bass.ds(g * GT + t, 1), k:k + 1].rearrange("p o k -> p (o k)")
                        last = dve.scalar_tensor_tensor(xt, R[:, p, t * K0 + k, :], gate, xt, ALU.mult, ALU.add)
                    link(last)
                if hi == K0:
                    dve.sem_inc(s_radd, 1)
                link.end(hi)

            def combined_stats(grp):
                link = Chain(dve, c_C, grp.g, 5, first=3)
                variance(3, link, X[:, bass.ds(grp.g * GT, GT), :])
                link.end()

            def combined_norm(grp):
                if after(grp.g, 1):
                    dve.wait_ge(s_xaTp, grp.g)
                normalize(3, grp, X[:, bass.ds(grp.g * GT, GT), :], xa[:]).then_inc(s_xa, 1)

            def rotate(grp, side):
                g = grp.g
                link = Chain(dve, c_N, g, 8, first=4 * side)
                dve.wait_ge((s_qr, s_kr)[side], g + 1)
                for h in range(2):
                    last = dve.tensor_tensor(rt[:, h].rearrange("p (b t) -> p b t", b=GB),
                                      bank[3][h * DR:(h + 1) * DR, :].rearrange("p (b t) -> p b t", b=GB),
                                      rope_sb[h * DR:(h + 1) * DR, :].unsqueeze(1).broadcast_to([DR, GB, T]), ALU.mult)
                link(last)

            def rotated(grp, side):
                g = grp.g
                link = Chain(dve, c_N, g, 8, first=4 * side + 1)
                if side == 0 and after(g, 1):
                    for r in range(RD):
                        dve.wait_ge(s_fill[r], 96 * g - 32)
                link(dve.tensor_tensor(rt[:, 0], rt[:, 0], rt[:, 1], ALU.add))
                for r in ((0, 1), (0, 2))[side]:
                    last = dve.tensor_copy(rp[r * DR:(r + 1) * DR, side], rt[:, 0])
                link(last)
                r = (2, 1)[side]
                link(dve.tensor_tensor(rp[r * DR:(r + 1) * DR, side], rt[:, 0], rp[0:DR, side].bitcast(F32), ALU.subtract))
                dve.sem_inc((s_rq, s_rk)[side], 1)
                link.end(4 * side + 4)

            def lower(grp, side):
                dve.wait_ge((s_qh, s_kh)[side], grp.g + 1)
                dve.tensor_tensor(qkl[:, side], bank[2][:], qkh[:, side].bitcast(F32), ALU.subtract).then_inc((s_ql, s_kl)[side], 1)

            def maxima(grp, i, h):
                u = grp.g * ND + i
                m = mx[:, i % 2]
                dve.wait_ge(s_max, u * 2 + h + 1)
                for c, lo, hi in ((0, P, 2 * P), (1, 2 * P, 4 * P)):
                    last = dve.tensor_reduce(m[:, h, :, c], pairbank[0][:].rearrange("p (b n) -> p b n", b=GB)[:, :, lo:hi], AX.X, ALU.max)
                last.then_inc(s_maxr, 1)
                if h == 1:
                    dve.wait_ge(s_maxr, u * 2 + 2)
                    mm = m.rearrange("p h b c -> p (h b c)")
                    dve.tensor_scalar(ms[:, i % 2, 0:8], mm, -1.0, None, ALU.mult).then_inc(s_ms, 1)
                    dve.wait_ge(s_ms, 2 * u + 1)
                    dve.scalar_tensor_tensor(ms[:, i % 2, 8:16], mm, -1.0, ms[:, i % 2, 0:8].bitcast(F32), ALU.mult, ALU.subtract).then_inc(s_ms, 1)

            def divide(grp, m):
                g = grp.g
                n = g * (ND // 2) + m
                dve.wait_ge(s_rawTp, n + 1)
                if m == 0 and after(g, 1):
                    dve.wait_ge(s_attTp, g)
                v5 = bank[7][:].rearrange("p (u c h b d) -> p u c h b d", u=2, c=2, h=2, b=2)
                dve.reciprocal(rec[:], bank[7][:].rearrange("p (u j d) -> p u j d", u=4, j=4)[:, :, :, HD]).then_inc(s_norm, 1)
                dve.wait_ge(s_norm, 2 * n + 1)
                r5 = rec[:].rearrange("p (u c) (h b) -> p u c h b", u=2, h=2)
                for c in range(2):
                    for b in range(2):
                        h0 = 4 * m * HD
                        last = dve.tensor_tensor(
                            att[:, 2 * b + c, h0:h0 + 4 * HD].rearrange("p (u h d) -> p u h d", u=2, h=2),
                            v5[:, :, c, :, b, 0:HD], r5[:, :, c, :, b].unsqueeze(3).broadcast_to([P, 2, 2, HD]), ALU.mult)
                last.then_inc(s_norm, 1)

            def output_stats(grp):
                g = grp.g
                link = Chain(dve, c_R, g, 3)
                dve.wait_ge(s_wo1, g + 1)
                xt = X[:, bass.ds(g * GT, GT), :]
                link(dve.tensor_tensor(xt, xt, bank[3][:].rearrange("p (t n) -> p t n", t=GT), ALU.add))
                dve.sem_inc(s_x3, 1)
                variance(4, link, xt)
                link.end()

            def output_norm(grp):
                g, p = grp.g, grp.par
                if after(g, 2):
                    dve.wait_ge(s_scat1[p], 16 * GT * K1 * grp.half)
                normalize(4, grp, X[:, bass.ds(g * GT, GT), :], xg[:, p, :, 0:P]).then_inc(s_xg, 1)

            def choose1(grp):
                g, p = grp.g, grp.par
                link = Chain(dve, c_Q, g, 11)
                dve.wait_ge(s_lg1, g + 1)
                link(dve.tensor_copy(lg1[:], bank[3][:, 0:GT * E1].rearrange("p (t e) -> p t e", t=GT)))
                stands_alone(dve)
                for t in range(GT):
                    last = dve.max(best1[:, t, :], lg1[:, t, :])
                link(last)
                dve.tensor_copy(gt1[:, bass.ds(g * GT, GT), :], best1[:, :, 0:K1])
                for t in range(GT):
                    last = dve.max_index(ix1[:, t, :], best1[:, t, :], lg1[:, t, :])
                link(last)
                ixg, posg = ixa[:, bass.ds(g * GT, GT), :], posa[:, bass.ds(g * GT, GT), :]
                link(dve.tensor_copy(ixg, ix1[:, :, 0:K1]))
                for t in range(GT):
                    last = dve.tensor_tensor(oh1[:, t], iota_e[:, 0:E1].unsqueeze(1).broadcast_to([P, K1, E1]),
                                         ixa[:, bass.ds(g * GT + t, 1), :].rearrange("p o k -> p (o k)").unsqueeze(2).broadcast_to([P, K1, E1]), ALU.is_equal)
                link(last)
                dve.tensor_tensor(M1b[:], oh1[:, :, 0], oh1[:, :, 1], ALU.add).then_inc(s_M1, 1)
                link(dve.tensor_reduce(gcnt1[:], oh1[:].rearrange("p t k e -> p e (t k)"), AX.X, ALU.add))
                link.end(6)

            def place1(grp):
                g, p = grp.g, grp.par
                link = Chain(dve, c_Q, g, 11, first=6)
                ixg, posg = ixa[:, bass.ds(g * GT, GT), :], posa[:, bass.ds(g * GT, GT), :]
                dve.wait_ge(s_pos1, g + 1)
                for t in range(GT):
                    last = dve.tensor_tensor(ohp1[:, t], oh1[:, t], bank[3][:, 256 + t * E1:256 + (t + 1) * E1].unsqueeze(1).broadcast_to([P, K1, E1]), ALU.mult)
                link(last)
                link(dve.tensor_tensor(count1[:], count1[:], gcnt1[:], ALU.add))
                link(dve.tensor_copy(count1b[:], count1[:]))
                link(dve.tensor_reduce(posg, ohp1[:], AX.X, ALU.add))
                if after(g, 2):
                    dve.wait_ge(s_scat1[p], 16 * GT * K1 * grp.half)
                link(dve.scalar_tensor_tensor(srow1[:, p], ixg, float(REG), posg, ALU.mult, ALU.add))
                dve.sem_inc(s_row1, 1)
                link.end()

            def half(i, h):
                return lambda grp: maxima(grp, i, h)

            def division(m):
                return lambda grp: divide(grp, m)

            def side(stage, which):
                return lambda grp: stage(grp, which), 1

            def choices(lo, hi):
                return lambda grp: combine(grp, lo, hi), 0

            before = {3: [side(rotated, 0)], 4: [side(rotated, 1)], 5: [choices(0, 1)], 6: [choices(2, 3)],
                      7: [(combined_stats, 0)]}
            behind = {1: [(output_stats, 3)], 2: [side(lower, 0), side(rotate, 0)], 3: [side(lower, 1), side(rotate, 1)],
                      4: [(output_norm, 3)], 5: [choices(1, 2)], 6: [(choose1, 3)], 7: [(place1, 3), (combined_norm, 0)]}
            slots_of = []
            for i in range(ND):
                k, lag = next_duo(i, 2)
                slots_of.append((half(k, 0), lag))
                if i % 2 == 0:
                    slots_of.append((division((i // 2 - 1) % (ND // 2)), 2 if i else 3))
                slots_of += before.get(i, []) + [(half(k, 1), lag)] + behind.get(i, [])
            steps(dve, slots_of)

            link = Chain(dve, c_T, 0, 14, base=8)
            link(dve.tensor_tensor(gw1[:], gt1[:], gt1[:, :, 0:1].broadcast_to([P, NT, K1]), ALU.subtract))
            dve.sem_inc(s_gsub, 1)
            dve.wait_ge(s_tot, 1)
            link(dve.tensor_copy(ntile[:], bank[0][:, 0:E1]))
            link(dve.tensor_tensor(cmp1[:], ntile[:].unsqueeze(2).broadcast_to([P, E1, NT]),
                                   iota128.unsqueeze(1).broadcast_to([P, E1, NT]), ALU.is_gt))
            link(dve.tensor_reduce(ntile[:], cmp1[:], AX.X, ALU.add))
            link(dve.tensor_tensor_scan(tend[:], ones8[:], ntile[:], 0.0, ALU.mult, ALU.add))
            link(dve.tensor_scalar(tw[:], ntile[:], -float(P), float(REG), ALU.mult, ALU.add))
            link(dve.tensor_tensor(cmp2[:], tend[:].unsqueeze(1).broadcast_to([P, ND1, E1]),
                                   iota_t.unsqueeze(2).broadcast_to([P, ND1, E1]), ALU.is_le))
            link(dve.tensor_tensor(cmp3[:], cmp2[:], tw[:].unsqueeze(1).broadcast_to([P, ND1, E1]), ALU.mult))
            dve.tensor_reduce(tl[:, 0], cmp2[:], AX.X, ALU.add)
            link(dve.tensor_reduce(tl[:, 1], cmp3[:], AX.X, ALU.add))
            link(dve.scalar_tensor_tensor(tl[:, 1], iota_t, float(P), tl[:, 1], ALU.mult, ALU.add))
            dve.tensor_scalar(tli[:, 0], tl[:, 0], float(E1 - 1), None, ALU.min)
            link(dve.tensor_scalar(tli[:, 1], tl[:, 1], float(E1 * REG - P), None, ALU.min))
            dve.sem_inc(s_tiles, 1)
            dve.wait_ge(s_gexp, 2)
            link(dve.tensor_tensor(gsum[:], gt1[:, :, 0], gt1[:, :, 1], ALU.add))
            link(dve.reciprocal(gsum[:], gsum[:]))
            link(dve.tensor_tensor(gw1[:], gt1[:], gsum[:].unsqueeze(2).broadcast_to([P, NT, K1]), ALU.mult))
            dve.sem_inc(s_tiles, 1)
            link.end()

            def d_act(t, p):
                dve.wait_ge(s_sg, t + 1)
                dve.tensor_tensor(ac[:, p], bank[2 + p][:, 0:F1], sg[:, p], ALU.mult).then_inc(s_ac, 1)

            def d_turn(t, p):
                dve.wait_ge(s_acTp, t + 1)
                dve.tensor_copy(acT[:, p], bank[4 + p][:, 0:F1]).then_inc(s_acT, 1)

            def d_dest(t, q, lap):
                dve.wait_ge(s_xs[q % NQ1], 16 * (NPAIR // NQ + lap * (LAP1 // NQ1) + q // NQ1 + 1))
                if q >= LAP1 or not isinstance(lap, int) or lap:
                    dve.wait_ge(s_yd, t - LAP1 + NQ1 + 1)
                dve.tensor_scalar(dest[:, q % LAP1:q % LAP1 + 1], xd[:, q % NQ1, P:PX], -1.0, float(NPLACE), ALU.mult, ALU.add
                                  ).then_inc(s_dest, 1)

            def lap_of(lap, left=ND1):
                for q in range(LAP1):
                    t = lap * LAP1 + q
                    d_turn(t, q % 2)
                    if q + AHEAD < left:
                        d_act(t + AHEAD, q % 2)
                    if q + AHEAD + 1 < left:
                        d_dest(t + AHEAD + 1, q + AHEAD + 1, lap)

            for t in range(AHEAD + 1):
                d_dest(t, t, 0)
            d_act(0, 0)
            d_act(1, 1)
            lap_of(0)
            with dve.Fori(1, ND1 // LAP1 - 1) as lap:
                lap_of(lap)
            lap_of(ND1 // LAP1 - 1, left=LAP1)

            def final(g, p, half):
                dve.wait_ge(s_yo[p], 16 * (NPAIR // NQ + half + 1))
                for k in range(K1):
                    for t in range(GT):
                        xt = X[:, bass.ds(g * GT + t, 1), :].rearrange("p o d -> p (o d)")
                        gate = gw1[:, bass.ds(g * GT + t, 1), k:k + 1].rearrange("p o k -> p (o k)")
                        last = dve.scalar_tensor_tensor(xt, R[:, p, t * K1 + k, :], gate, xt, ALU.mult, ALU.add)
                    if k < K1 - 1:
                        last.then_inc(s_fin1, 1)
                        dve.wait_ge(s_fin1, g + 1)
                last.then_inc(s_fin, 1)

            with dve.Fori(0, NG // 2) as j:
                for p in range(2):
                    final(2 * j + p, p, j)

        @block.tensor
        def _(pe):
            pe.wait_ge(s_const, 16 * NCONST)
            pe.wait_ge(s_tri, 2)



            def norm_in(grp):
                g, p = grp.g, grp.par
                pe.wait_ge(s_xn, g + 1)
                if after(g, 1):
                    pe.wait_ge(s_qe, g)
                for t in range(GT):
                    last = pe.transpose(bank[0][:, t * P:(t + 1) * P], xn[:, p, t, :], ident)
                last.then_inc(s_xnTp, 1)

            def queries_keys(grp):
                g = grp.g
                pe.wait_ge(s_xnT, g + 1)
                if after(g, 1):
                    pe.wait_ge(s_ge, g)
                pe.matmul(bank[1][:], wq_sb[:], xnT[:], start=True, stop=True).then_inc(s_q, 1)
                pe.matmul(bank[0][:], wk_sb[:], xnT[:], start=True, stop=True).then_inc(s_k, 1)

            def state_values(grp):
                if after(grp.g, 1):
                    pe.wait_ge(s_ve_, grp.g)
                for t in range(GT):
                    last = pe.matmul(bank[3][:, t * P:(t + 1) * P], xnT[:, t * P:(t + 1) * P], wv_sb[:], start=True, stop=True)
                last.then_inc(s_v, 1)

            def gate(grp):
                pe.wait_ge(s_qe, grp.g + 1)
                pe.matmul(bank[1][:], wg_sb[:], xnT[:], start=True, stop=True).then_inc(s_g, 1)

            def level(grp, lo, hi):
                g, p = grp.g, grp.par
                for lv in range(lo, hi):
                    if lv == 0:
                        pe.wait_ge(s_ge, g + 1)
                        if after(g, 1):
                            pe.wait_ge(s_aev, g * NLP - 1)
                    else:
                        pe.wait_ge(s_upd, g * NLP + lv)
                    if lv >= 2:
                        pe.wait_ge(s_aev, g * NLP + lv - 1)
                    for t in range(GT):
                        last = pe.matmul(bank[2 if lv % 2 else 6][:, t * P:(t + 1) * P], K[:, p, t * P:(t + 1) * P],
                                         Q[:, p, t * P:(t + 1) * P], start=True, stop=True)
                    last.then_inc(s_lev, 1)

            def cross(grp):
                g, p = grp.g, grp.par
                pe.wait_ge(s_upd, (g + 1) * NLP)
                if after(g, 1):
                    pe.wait_ge(s_y, g)
                for b in range(GB):
                    last = pe.matmul(bank[4][:, b * P:(b + 1) * P], K[:, p, 2 * b * P:(2 * b + 1) * P],
                                     Q[:, p, (2 * b + 1) * P:(2 * b + 2) * P], start=True, stop=True)
                last.then_inc(s_cross, 1)

            def attended(grp):
                g, p = grp.g, grp.par
                pe.wait_ge(s_ve_, g + 1)
                pe.wait_ge(s_axt, g + 1)
                pe.wait_ge(s_aev, (g + 1) * NLP)
                for b in range(GB):
                    v0, v1 = V[:, p, 2 * b], V[:, p, 2 * b + 1]
                    o0, o1 = (bank[5][:, (2 * b + s) * P:(2 * b + s + 1) * P] for s in range(2))
                    pe.matmul(o0, v0, AD[:, p, 2 * b * P:(2 * b + 1) * P], start=True, stop=True)
                    pe.matmul(o1, v0, AXT[:, b], start=True, stop=False)
                    last = pe.matmul(o1, v1, AD[:, p, (2 * b + 1) * P:(2 * b + 2) * P], start=False, stop=True)
                last.then_inc(s_av, 1)

            def output(grp):
                pe.wait_ge(s_ot, grp.g + 1)
                for t in range(GT):
                    last = pe.matmul(bank[4][:, t * P:(t + 1) * P], OT[:, t * P:(t + 1) * P], wo_sb[:], start=True, stop=True)
                last.then_inc(s_wo, 1)

            def router_in0(grp):
                g, p = grp.g, grp.par
                pe.wait_ge(s_xf, g + 1)
                if after(g, 1):
                    pe.wait_ge(s_posr, g)
                for t in range(GT):
                    last = pe.transpose(bank[7][:, t * P:(t + 1) * P], xf[:, p, t, :], ident)
                last.then_inc(s_xfTp, 1)

            def logits0(grp):
                pe.wait_ge(s_xfT, grp.g + 1)
                for t in range(GT):
                    last = pe.matmul(bank[7][:, t * E0:(t + 1) * E0], xfT[:, t * P:(t + 1) * P], gw_sb[:], start=True, stop=True)
                last.then_inc(s_lg, 1)

            def earlier0(grp):
                g = grp.g
                pe.wait_ge(s_M, g + 1)
                if after(g, 1):
                    pe.wait_ge(s_slot, g)
                for t in range(GT):
                    dst = bank[7][:, 256 + t * E0:256 + (t + 1) * E0]
                    pe.matmul(dst, tri[:], Mb[:, t], start=True, stop=False)
                    for u in range(t):
                        pe.matmul(dst, ones[:], Mb[:, u], start=False, stop=False)
                    last = pe.matmul(dst, ones[:], countb[:, 0], start=False, stop=True)
                last.then_inc(s_pos, 1)

            def lev(lo, hi):
                return lambda grp: level(grp, lo, hi), 2

            steps(pe, [(router_in0, 4), (attended, 3), lev(1, 2), (logits0, 4), (output, 3), (norm_in, 1), lev(2, 3),
                       (queries_keys, 1), lev(3, 4), (earlier0, 4), lev(4, 5), (state_values, 1), lev(5, 6), (gate, 1),
                       lev(6, 8), (lambda grp: level(grp, 0, 1), 1), (cross, 2)])

            def tokens_in(pair, i, lap):
                p, q = i % 2, i % NQ
                pe.wait_ge(s_xs[q], 16 * (lap * (PAIRS // NQ) + i // NQ + 1))
                pe.transpose(bank[7 * p][:, 0:P], xs[:, q, :], ident).then_inc(s_xsTp, 1)

            def hidden(pair, i, lap):
                p = i % 2
                pe.wait_ge(s_w[i], 32 * (lap + 1))
                pe.wait_ge(s_xsT, pair + 1)
                for h in range(2):
                    last = pe.matmul(bank[1 + p][h * CAP:(h + 1) * CAP, :], xsT[:, p, h * CAP:(h + 1) * CAP],
                                     w1r[:, 2 * i + h, :], start=True, stop=True)
                last.then_inc(s_h, 1)

            def turn(pair, i):
                p = i % 2
                pe.wait_ge(s_hs, pair + 1)
                for c in range(HC):
                    last = pe.transpose(bank[3 + p][:, c * P:(c + 1) * P], hs[:, p, c * P:(c + 1) * P], ident)
                last.then_inc(s_hTp, 1)

            def outputs(pair, i, first=False):
                p = i % 2
                pe.wait_ge(s_gT, pair + 1)
                if not first:
                    pe.wait_ge(s_ys, pair - 1)
                for c in range(HC):
                    for h in range(2):
                        last = pe.matmul(bank[5 + p][h * CAP:(h + 1) * CAP, 0:P], gT[:, p, c, h * CAP:(h + 1) * CAP],
                                         w2r[:, 2 * i + h, c, :], start=(c == 0), stop=(c == HC - 1), skip_group_check=True)
                last.then_inc(s_yp, 1)

            def ahead(lap, i, n):
                return (i + n) % PAIRS, lap + (i + n) // PAIRS

            def pairs(lap, last_lap=False, first_lap=False):
                for i in range(PAIRS):
                    pair = lap * PAIRS + i
                    turn(pair, i)
                    if not (last_lap and i + AHEAD >= PAIRS):
                        hidden(pair + AHEAD, *ahead(lap, i, AHEAD))
                    if not (last_lap and i + AHEAD + 1 >= PAIRS):
                        tokens_in(pair + AHEAD + 1, *ahead(lap, i, AHEAD + 1))
                    outputs(pair, i, first_lap and i < 2)

            tokens_in(0, 0, 0)
            tokens_in(1, 1, 0)
            hidden(0, 0, 0)
            tokens_in(2, 2, 0)
            hidden(1, 1, 0)
            pairs(0, first_lap=True)
            with pe.Fori(1, NROUND - 1) as lap:
                pairs(lap)
            pairs(NROUND - 1, last_lap=True)

            pe.wait_ge(s_w2c, 32)
            pe.wait_ge(s_pre, 1)
            pe.wait_ge(s_ones1, 32)

            def norm1_in(grp):
                g = grp.g
                pe.wait_ge(s_xa, g + 1)
                if after(g, 1):
                    pe.wait_ge(s_v1, g)
                for t in range(GT):
                    last = pe.transpose(bank[2][:, t * P:(t + 1) * P], xa[:, t, :], ident)
                last.then_inc(s_xaTp, 1)

            def latent(grp):
                pe.wait_ge(s_xaT, grp.g + 1)
                pe.matmul(bank[2][:], wkvd_sb[:], xaT[:], start=True, stop=True).then_inc(s_ckvp, 1)

            def own_q(grp):
                g = grp.g
                pe.wait_ge(s_ckv, g + 1)
                pe.matmul(bank[2][:], wq1_sb[:], xaT[:], start=True, stop=True).then_inc(s_q1p, 1)
                if after(g, 2):
                    pe.wait_ge(s_x3, g - 1)
                pe.matmul(bank[3][0:2 * DR, :], wqr_sb[:], xaT[:], start=True, stop=True).then_inc(s_qr, 1)

            def own_k(grp):
                g = grp.g
                pe.wait_ge(s_ql, g + 1)
                pe.matmul(bank[2][:], wku_sb[:], ckvT[:], start=True, stop=True).then_inc(s_kp, 1)
                pe.wait_ge(c_N, 8 * g + 1)
                pe.matmul(bank[3][0:2 * DR, :], wkr_sb[:], ckvT[:], start=True, stop=True).then_inc(s_kr, 1)

            def own_v(grp):
                pe.wait_ge(s_kl, grp.g + 1)
                for t in range(GT):
                    last = pe.matmul(bank[2][:, t * P:(t + 1) * P], ckvT[:, t * P:(t + 1) * P], wvu_sb[:], start=True, stop=True)
                last.then_inc(s_v1p, 1)

            def max_scores(grp, i, h):
                g, r = grp.g, i % RD
                u = g * ND + i
                if h == 0:
                    pe.wait_ge(s_fill[r], 96 * g + (64 if i < RD else 96))
                if h or i or after(g, 1):
                    pe.wait_ge(s_maxr, 2 * u + h)
                for b in range(GB):
                    bk = bank[b]
                    keys = SK[0:KM, 2 * r + h, :].rearrange("p (b c n) -> p b c n", b=GB, c=2)[:, b, ::-1, :]
                    for c in range(2):
                        n0 = (2 * b + c) * P
                        pe.matmul(bk[:, c * 2 * P:(c + 1) * 2 * P], SQ[0:KM, 2 * r + h, n0:n0 + P], keys,
                                  start=(c == 0), stop=False, skip_group_check=True)
                    last = pe.matmul(bk[:, P:3 * P], identb[:], maskq[:].rearrange("p a b -> p (a b)"), start=False, stop=True,
                                     skip_group_check=True)
                last.then_inc(s_max, 1)

            def turn_maxima(grp, i):
                g = grp.g
                u = g * ND + i
                pe.wait_ge(s_ms, 2 * u + 2)
                if i or after(g, 1):
                    pe.wait_ge(s_mT, u)
                if i >= 4 or after(g, 1):
                    pe.wait_ge(s_norm, 2 * turned_pairs(g, i))
                pe.transpose(bank[7][0:16, 0:P], ms[:, i % 2, :].bitcast(F32), ident).then_inc(s_mTp, 1)

            def scores(grp, i, n):
                g, r = grp.g, i % RD
                h, b = n // 2, n % 2
                k = (g * ND + i) * 4 + n
                if n >= 2 or i >= 1 or after(g, 1):
                    pe.wait_ge(s_exp, k - 1)
                if n == 0:
                    pe.wait_ge(s_shift[r], 64 * g + (32 if i < RD else 64))
                bk = bank[4 + n % 2]
                q = SQ[0:KS, 2 * r + h, b * T:(b + 1) * T]
                k1, k0 = (SK[0:KS, 2 * r + h, b * T + c * P:b * T + (c + 1) * P] for c in (1, 0))
                pe.matmul(bk[:, 0:2 * P], k1, q, start=True, stop=False, skip_group_check=True)
                pe.matmul(bk[:, 2 * P:4 * P], k0, q, start=False, stop=False, skip_group_check=True)
                last = pe.matmul(bk[:, P:3 * P], identb[:], maskk[:].rearrange("p a b -> p (a b)"), start=False, stop=True, skip_group_check=True)
                last.then_inc(s_st, 1)

            def values(grp, i):
                g, p = grp.g, grp.par
                pe.wait_ge(s_exp, (g * ND + i + 1) * 4)
                if i == 0:
                    pe.wait_ge(s_v1, g + 1)
                if i % 2 == 0 and (i or after(g, 1)):
                    pe.wait_ge(s_raw, g * (ND // 2) + i // 2)
                c0 = (i % 2) * T
                for n in range(4):
                    h, b = n // 2, n % 2
                    pe.matmul(bank[6][32 * n:32 * n + 32, c0:c0 + T], V1[:, p, 2 * b, 2 * i + h, :], PT[:, i % 2, n, P:3 * P],
                              start=True, stop=False, tile_position=(0, 32 * n), skip_group_check=True)
                for n in range(4):
                    h, b = n // 2, n % 2
                    last = pe.matmul(bank[6][32 * n:32 * n + 32, c0 + P:c0 + T], V1[:, p, 2 * b + 1, 2 * i + h, :], PT[:, i % 2, n, 0:P],
                              start=False, stop=True, tile_position=(0, 32 * n), skip_group_check=True)
                if i % 2:
                    last.then_inc(s_pv, 1)

            def turn_values(grp, m):
                g = grp.g
                n = g * (ND // 2) + m
                pe.wait_ge(s_raw, n + 1)
                pe.wait_ge(s_mT, g * ND + (2 * m + 4 if m < 3 or within(g, NG - 1) else ND))
                if m or after(g, 1):
                    pe.wait_ge(s_norm, 2 * n)
                for c in range(4):
                    last = pe.transpose(bank[7][:, c * P:(c + 1) * P], raw[:, c * P:(c + 1) * P], ident)
                last.then_inc(s_rawTp, 1)

            def attended_in(grp):
                g = grp.g
                pe.wait_ge(s_norm, 2 * (g + 1) * (ND // 2))
                if after(g, 1):
                    pe.wait_ge(s_row1, g)
                for t in range(GT):
                    last = pe.transpose(bank[3][:, t * P:(t + 1) * P], att[:, t, :], ident)
                last.then_inc(s_attTp, 1)

            def output1(grp):
                pe.wait_ge(s_attT, grp.g + 1)
                for t in range(GT):
                    last = pe.matmul(bank[3][:, t * P:(t + 1) * P], attT[:, t * P:(t + 1) * P], wo1_sb[:], start=True, stop=True)
                last.then_inc(s_wo1, 1)

            def router_in(grp):
                g, p = grp.g, grp.par
                pe.wait_ge(s_xg, g + 1)
                pe.wait_ge(s_rk, g + 3 if within(g, NG - 2) else NG)
                for t in range(GT):
                    last = pe.transpose(bank[3][:, t * P:(t + 1) * P], xg[:, p, t, 0:P], ident)
                last.then_inc(s_xgTp, 1)

            def logits1(grp):
                pe.wait_ge(s_xgT, grp.g + 1)
                for t in range(GT):
                    last = pe.matmul(bank[3][:, t * E1:(t + 1) * E1], xgT[:, t * P:(t + 1) * P], wr_sb[:], start=True, stop=True)
                last.then_inc(s_lg1, 1)

            def earlier1(grp):
                g = grp.g
                pe.wait_ge(s_M1, g + 1)
                if after(g, 1):
                    pe.wait_ge(s_row1, g)
                for t in range(GT):
                    dst = bank[3][:, 256 + t * E1:256 + (t + 1) * E1]
                    pe.matmul(dst, tri[:], M1b[:, t], start=True, stop=False)
                    for u in range(t):
                        pe.matmul(dst, ones[:], M1b[:, u], start=False, stop=False)
                    last = pe.matmul(dst, ones[:], count1b[:], start=False, stop=True)
                last.then_inc(s_pos1, 1)

            def some_scores(i, lo, hi):
                def stage(grp):
                    for n in range(lo, hi):
                        scores(grp, i, n)
                return stage, 2

            def on(i, n, stage, *args):
                k, lag = next_duo(i, n)
                return lambda grp: stage(grp, k, *args), lag

            more = {0: [(norm1_in, 1), (attended_in, 3)], 1: [(latent, 1), (output1, 3)], 2: [(own_q, 1)], 3: [(own_k, 1)],
                    4: [(own_v, 1)], 5: [(router_in, 3)], 6: [(logits1, 3)], 7: [(earlier1, 3)]}
            slots_of = []
            for i in range(ND):
                slots_of += [some_scores(i, 0, 2), ((lambda k: lambda grp: values(grp, k))((i - 1) % ND), 2 if i else 3),
                             on(i, 1, turn_maxima), on(i, 2, max_scores, 0), some_scores(i, 2, 4)]
                if i % 2 == 0:
                    slots_of.append(((lambda m: lambda grp: turn_values(grp, m))((i // 2 - 1) % (ND // 2)), 2 if i else 3))
                slots_of += more[i] + [on(i, 2, max_scores, 1)]
            steps(pe, slots_of)

            pe.wait_ge(s_row1, NG)
            pe.matmul(bank[0][:, 0:E1], ones[:], count1b[:], start=True, stop=True).then_inc(s_tot, 1)

            pe.wait_ge(s_wd, 32)
            pe.wait_ge(s_tiles, 1)

            def d_in(t, q, lap):
                p = q % 2
                pe.wait_ge(s_xs[q], 16 * (NPAIR // NQ + lap + 1))
                pe.transpose(bank[p][:, 0:P], xd[:, q, 0:P], ident).then_inc(s_xsTp, 1)

            def d_hidden(t, p, e):
                pe.wait_ge(s_xsT, NPAIR + t + 1)
                pe.matmul(bank[2 + p][:], xdT[:, p], w1d[:, bass.ds(e, 1), :].rearrange("p o n -> p (o n)"), start=True, stop=True
                          ).then_inc(s_h, 1)

            def d_turn(t, p):
                pe.wait_ge(s_ac, t + 1)
                for c in range(2):
                    last = pe.transpose(bank[4 + p][:, c * P:(c + 1) * P], ac[:, p, c * P:(c + 1) * P], ident)
                last.then_inc(s_acTp, 1)

            def d_out(t, p, e, first):
                pe.wait_ge(s_acT, t + 1)
                if not first:
                    pe.wait_ge(s_yd, t - 1)
                for c in range(2):
                    last = pe.matmul(bank[6 + p][:, 0:P], acT[:, p, c * P:(c + 1) * P],
                                     w2d[:, bass.ds(e, 1), c, :].rearrange("p o n -> p (o n)"), start=(c == 0), stop=(c == 1))
                last.then_inc(s_ydp, 1)

            def expert(t):
                return pe.value_load(tli[0:1, 0, bass.ds(t, 1)], min_val=0, max_val=E1 - 1)

            def lap_of(lap, first=False, left=ND1):
                base = lap * LAP1
                experts = [expert(base + q) for q in range(AHEAD + 1)]
                for q in range(LAP1):
                    t, p = base + q, q % 2
                    d_turn(t, p)
                    if q + AHEAD < left:
                        d_hidden(t + AHEAD, p, experts[q + AHEAD])
                    if q + AHEAD + 1 < left:
                        d_in(t + AHEAD + 1, (q + AHEAD + 1) % NQ1, lap * (LAP1 // NQ1) + (q + AHEAD + 1) // NQ1)
                        if q + 1 < LAP1:
                            experts.append(expert(t + AHEAD + 1))
                    d_out(t, p, experts[q], first and q < 2)

            d_in(0, 0, 0)
            d_in(1, 1, 0)
            d_hidden(0, 0, expert(0))
            d_in(2, 2, 0)
            d_hidden(1, 1, expert(1))
            lap_of(0, first=True)
            with pe.Fori(1, ND1 // LAP1 - 1) as lap:
                lap_of(lap)
            lap_of(ND1 // LAP1 - 1, left=LAP1)


def constants():
    cst = np.zeros((P, 2 * P + E0 + ND1 + (1 + K1) * NT), np.float32)
    cst[:, 0:P] = np.eye(P)
    cst[:, P:2 * P] = np.triu(np.ones((P, P)), 1)
    cst[:, 2 * P:2 * P + E0] = np.arange(E0)
    cst[:, 2 * P + E0:2 * P + E0 + ND1] = np.arange(ND1)
    cst[:, 2 * P + E0 + ND1:2 * P + E0 + ND1 + NT] = np.arange(NT) * P
    token = np.arange(NT)[None] * P + np.arange(P)[:, None]
    cst[:, 2 * P + E0 + ND1 + NT:] = np.concatenate([NPLACE - K1 * token - k for k in range(K1)], 1)
    masks = np.zeros((P, NL, P // 2), np.float32)
    for level, m in enumerate(LEVELS):
        j = np.arange(P)[:, None]
        i = np.array([i for i in range(P) if i // m % 2 == 1])[None]
        masks[:, level] = (j // m % 2 == 0) & (i // m == j // m + 1)
    inv = (1.0 / 10000.0 ** (np.arange(0, DR, 2, dtype=np.float32) / np.float32(DR))).astype(np.float32)
    angle = np.outer(np.arange(T, dtype=np.float32), inv).astype(np.float32)
    cos, sin = np.cos(angle).T, np.sin(angle).T
    rope = np.ascontiguousarray(np.concatenate([cos, cos, -sin, sin], 0).astype(np.float32))
    return {"const": cst, "masks": masks.reshape(P, -1), "rope": rope}


def layout(a):
    def by_dim(w):
        return w.reshape(P, NH, HD).transpose(0, 2, 1).reshape(P, NH * HD)

    def swapped(w):
        return np.concatenate([w[:, DR // 2:], w[:, :DR // 2]], 1)

    out = {"x": a["L0_attn_x"].reshape(NTOK, P)}
    out["first_w"] = np.concatenate([a["L0_attn_" + n] for n in ("Wq", "Wk", "Wg", "Wv", "Wo")] + [a["L0_ffn_gate_w"]]
                                    + [a["L0_attn_" + n][:, None] for n in ("bq", "bk", "bg")], 1)
    out["first_b"] = np.concatenate([a["L0_attn_" + n] for n in ("bv", "bo", "gamma", "beta")] + [a["L0_ffn_gate_b"]])
    for n in ("w1", "w2", "b2"):
        out[n] = a["L0_ffn_" + n]
    out["b1t"] = a["L0_ffn_b1"].reshape(E0, HC, P).transpose(2, 0, 1).reshape(P, E0 * HC)
    qr, kr = a["L1_attn_W_q_rope"], a["L1_attn_W_k_rope"]
    out["second_w"] = np.concatenate([a["L1_attn_W_kv_down"], by_dim(a["L1_attn_W_k_up"]), a["L1_attn_W_v_up"],
                                      by_dim(a["L1_attn_W_q"]), a["L1_attn_W_o"], qr, swapped(qr), kr, swapped(kr),
                                      a["L1_ffn_Wr"].T], 1)
    out["W1t"] = a["L1_ffn_W1"].transpose(2, 0, 1).reshape(P, E1 * 2 * F1)
    out["W2t"] = a["L1_ffn_W2"].reshape(E1, P, 2, F1 // 2).transpose(3, 0, 2, 1).reshape(P, E1 * F1)
    return {n: np.ascontiguousarray(v) for n, v in out.items()}


def kernel(**inputs):
    import concourse.bacc as bacc
    from concourse.bass_utils import run_bass_kernel_spmd

    nc = bacc.Bacc("TRN2", target_bir_lowering=False, num_devices=1)
    arrays = {**layout({n: np.asarray(a) for n, a in inputs.items()}), **constants()}
    args = {n: nc.dram_tensor(n, a.shape, mybir.dt.from_np(a.dtype), kind="ExternalInput").ap() for n, a in arrays.items()}
    out = nc.dram_tensor("out", [NTOK, P], F32, kind="ExternalOutput").ap()
    build(nc, out=out, **args)
    r = run_bass_kernel_spmd(nc, [arrays], core_ids=[0])
    return r.results[0]["out"].reshape(B, T, P)
```
